# Optimizing a Trainium2 kernel written in Bass

```python
import numpy as np
import jax
import jax.numpy as jnp

def _softmax(x, axis=-1):
    return jax.nn.softmax(x, axis=axis)

def _gelu(x):
    return jax.nn.gelu(x, approximate=True)

def _silu(x):
    return jax.nn.silu(x)

def _sigmoid(x):
    return jax.nn.sigmoid(x)

def _layernorm(x, axis=-1, eps=1e-05):
    m = jnp.mean(x, axis=axis, keepdims=True)
    v = jnp.var(x, axis=axis, keepdims=True)
    return (x - m) / jnp.sqrt(v + eps)

def _scatter_add(tgt, idx, src, axis=0):
    return tgt.at[idx].add(src)

def _segment_sum(src, seg, n):
    return jax.ops.segment_sum(src, seg, n)
kernel_name = 'mk_perceiver_d2_seqx_r2_bd2e25'

def setup_inputs(seed: int=0):
    np.random.seed(seed)
    _w = jnp.asarray

    def _rec_inputs():
        import jax
        import jax.numpy as jnp
        _rk = jax.random.key(seed)
        x = 7.22e-05 + 1 * jax.random.normal(jax.random.fold_in(_rk, 1), (8, 64, 512), jnp.float32)
        _lenS = 64 - jax.random.randint(jax.random.fold_in(_rk, 7), (8,), 0, max(1, 64 // 4) + 1, jnp.int32)
        _lenS2 = 1601 - jax.random.randint(jax.random.fold_in(_rk, 8), (8,), 0, max(1, 1601 // 4) + 1, jnp.int32)
        _ctx_768P = jax.random.normal(jax.random.fold_in(_rk, 11), (8, 16, 384), jnp.float32)
        _ctx_768c = jax.random.dirichlet(jax.random.fold_in(_rk, 511), 0.3 * jnp.ones((16,), jnp.float32), (8, 1601))
        _ctx_768t = jnp.einsum('bsk,bkd->bsd', _ctx_768c, _ctx_768P)
        _ctx_768t = _ctx_768t * jax.lax.rsqrt(jnp.mean(jnp.square(_ctx_768t)) + 1e-12) * 0.953939
        ctx_768 = 2.09791e-05 + 1.00001 * (_ctx_768t + 0.3 * jax.random.normal(jax.random.fold_in(_rk, 611), (8, 1601, 384), jnp.float32))
        _validS = jnp.arange(64)[None, :] < _lenS[:, None]
        _validS2 = jnp.arange(1601)[None, :] < _lenS2[:, None]
        _causal = jnp.tril(jnp.ones((64, 64), dtype=bool))
        mask_BxS_bf1 = jnp.ones((8, 64), dtype=bool)
        mask_BxS2_bf1 = jnp.ones((8, 1601), dtype=bool)
        return (x, ctx_768, mask_BxS_bf1, mask_BxS2_bf1)
    x, ctx_768, mask_BxS_bf1, mask_BxS2_bf1 = _rec_inputs()

    def _L0_xattn_setup():
        import jax, jax.numpy as jnp
        import numpy as np
        HEADS = 8
        DIM_HEAD = 64
        SCALE = DIM_HEAD ** (-0.5)
        key = jax.random.key(seed)
        ks = jax.random.split(key, 7)
        b, n, m = (4, 1024, 512)
        qd, cd, inner = (512, 384, HEADS * DIM_HEAD)
        s = lambda fan_in: 1.0 / np.sqrt(fan_in)
        return {'x': jax.random.normal(ks[0], (b, n, qd), jnp.float32), 'context': jax.random.normal(ks[1], (b, m, cd), jnp.float32), 'Wq': jax.random.normal(ks[2], (qd, inner), jnp.float32) * s(qd), 'Wk': jax.random.normal(ks[3], (cd, inner), jnp.float32) * s(cd), 'Wv': jax.random.normal(ks[4], (cd, inner), jnp.float32) * s(cd), 'Wout': jax.random.normal(ks[5], (inner, qd), jnp.float32) * s(inner), 'bout': jax.random.normal(ks[6], (qd,), jnp.float32) * 0.01}
    _L0_xattn_all = _L0_xattn_setup()
    _L0_xattn_in = {k: v for k, v in _L0_xattn_all.items() if k in ('Wq', 'Wk', 'Wv', 'Wout', 'bout')}
    del _L0_xattn_all

    def _L0_attn_setup():
        import jax, jax.numpy as jnp
        import numpy as np

        def _rope_tables(T, d):
            half = d // 2
            i = jnp.arange(half, dtype=jnp.float32)
            theta = 10000.0 ** (-2.0 * i / d)
            m = jnp.arange(T, dtype=jnp.float32)[:, None]
            ang = m * theta[None, :]
            return (jnp.cos(ang), jnp.sin(ang))

        def _rotate(v, cos, sin):
            B, T, d = v.shape
            half = d // 2
            v2 = v.reshape(B, T, half, 2)
            even, odd = (v2[..., 0], v2[..., 1])
            c = cos[None, :, :]
            s = sin[None, :, :]
            new_even = even * c - odd * s
            new_odd = even * s + odd * c
            return jnp.stack([new_even, new_odd], axis=-1).reshape(B, T, d)
        key = jax.random.key(seed)
        k1, k2, k3, k4 = jax.random.split(key, 4)
        B, T, d = (4, 1024, 512)
        x = jax.random.normal(k1, (B, T, d), dtype=jnp.float32)
        scale = 0.02
        Wq = jax.random.normal(k2, (d, d), dtype=jnp.float32) * scale
        Wk = jax.random.normal(k3, (d, d), dtype=jnp.float32) * scale
        Wv = jax.random.normal(k4, (d, d), dtype=jnp.float32) * scale
        return {'x': x, 'Wq': Wq, 'Wk': Wk, 'Wv': Wv}
    _L0_attn_all = _L0_attn_setup()
    _L0_attn_in = {k: v for k, v in _L0_attn_all.items() if k in ('Wq', 'Wk', 'Wv')}
    del _L0_attn_all

    def _L0_ffn_setup():
        import jax, jax.numpy as jnp
        import numpy as np
        ALPHA = 1.702
        LIMIT = 7.0
        K = 2
        key = jax.random.key(seed)
        ks = jax.random.split(key, 4)
        B, S, H, E, I = (1, 512, 512, 8, 512)
        return {'hidden_states': jax.random.normal(ks[0], (B, S, H), jnp.float32), 'router_weight': jax.random.normal(ks[1], (E, H), jnp.float32), 'router_bias': jnp.zeros((E,), jnp.float32), 'gate_up_proj': jax.random.normal(ks[2], (E, H, 2 * I), jnp.float32) * 0.02, 'gate_up_bias': jnp.zeros((E, 2 * I), jnp.float32), 'down_proj': jax.random.normal(ks[3], (E, I, H), jnp.float32) * 0.02, 'down_bias': jnp.zeros((E, H), jnp.float32)}
    _L0_ffn_all = _L0_ffn_setup()
    _L0_ffn_in = {k: v for k, v in _L0_ffn_all.items() if k in ('router_weight', 'router_bias', 'gate_up_proj', 'gate_up_bias', 'down_proj', 'down_bias')}
    del _L0_ffn_all

    def _L1_xattn_setup():
        import jax, jax.numpy as jnp
        import numpy as np
        B, T, DT, G, DV = (16, 256, 512, 288, 384)
        H, DH = (4, 32)
        INNER = H * DH
        HID = 4 * DT
        N_STATE = 64
        K_TOP = 32

        def layernorm(x, g, b, eps=1e-05):
            m = x.mean(-1, keepdims=True)
            v = x.var(-1, keepdims=True)
            return (x - m) * jax.lax.rsqrt(v + eps) * g + b

        def s4d(x, log_dt, A_re, A_im, C_re, C_im, D_skip):
            Bb, L, D = x.shape
            dt = jnp.exp(log_dt)
            A = A_re + 1j * A_im
            C = C_re + 1j * C_im
            dtA = dt[:, None] * A
            dC = C * (jnp.exp(dtA) - 1.0) / A
            powers = jnp.exp(dtA[:, :, None] * jnp.arange(L))
            K = 2.0 * jnp.einsum('dn,dnl->dl', dC, powers).real
            n = 2 * L
            Kf = jnp.fft.rfft(K, n=n, axis=-1)
            xf = jnp.fft.rfft(x, n=n, axis=1)
            y = jnp.fft.irfft(xf * Kf.T[None], n=n, axis=1)[:, :L]
            return y + x * D_skip
        key = jax.random.key(seed)
        ks = jax.random.split(key, 16)
        s = 0.02
        inp = {'x_text': jax.random.normal(ks[0], (B, T, DT), jnp.float32), 'x_vision': jax.random.normal(ks[1], (B, G, DV), jnp.float32), 'text_mask': jnp.ones((B, T), bool), 'vision_mask': jnp.ones((B, G), bool), 'Wq': jax.random.normal(ks[2], (DT, INNER), jnp.float32) * s, 'Wk': jax.random.normal(ks[3], (DV, INNER), jnp.float32) * s, 'Wv': jax.random.normal(ks[4], (DV, DT), jnp.float32) * s, 'W_film_in': jax.random.normal(ks[5], (DT, 2 * DT), jnp.float32) * s, 'b_film_in': jnp.zeros((2 * DT,), jnp.float32), 'W_film_out': jax.random.normal(ks[6], (DT, 2 * DT), jnp.float32) * s, 'b_film_out': jnp.zeros((2 * DT,), jnp.float32), 'g_norm_in': jnp.ones((DT,), jnp.float32), 'b_norm_in': jnp.zeros((DT,), jnp.float32), 'g_norm_out': jnp.ones((DT,), jnp.float32), 'b_norm_out': jnp.zeros((DT,), jnp.float32), 'g_ffn': jnp.ones((DT,), jnp.float32), 'b_ffn': jnp.zeros((DT,), jnp.float32), 'W1': jax.random.normal(ks[7], (DT, HID), jnp.float32) * s, 'b1': jnp.zeros((HID,), jnp.float32), 'W2': jax.random.normal(ks[8], (HID, DT), jnp.float32) * s, 'b2': jnp.zeros((DT,), jnp.float32), 'log_dt': jnp.log(0.001) + jax.random.uniform(ks[9], (DT,), jnp.float32) * (jnp.log(0.1) - jnp.log(0.001)), 'A_re': -0.5 * jnp.ones((DT, N_STATE), jnp.float32), 'A_im': jnp.tile(jnp.pi * jnp.arange(N_STATE, dtype=jnp.float32), (DT, 1)), 'C_re': jax.random.normal(ks[10], (DT, N_STATE), jnp.float32) * 0.5 ** 0.5, 'C_im': jax.random.normal(ks[11], (DT, N_STATE), jnp.float32) * 0.5 ** 0.5, 'D_skip': jax.random.normal(ks[12], (DT,), jnp.float32), 'mod_gate': jnp.array(0.5, jnp.float32)}
        return inp
    _L1_xattn_all = _L1_xattn_setup()
    _L1_xattn_in = {k: v for k, v in _L1_xattn_all.items() if k in ('Wq', 'Wk', 'Wv', 'W_film_in', 'b_film_in', 'W_film_out', 'b_film_out', 'g_norm_in', 'b_norm_in', 'g_norm_out', 'b_norm_out', 'g_ffn', 'b_ffn', 'W1', 'b1', 'W2', 'b2', 'log_dt', 'A_re', 'A_im', 'C_re', 'C_im', 'D_skip', 'mod_gate')}
    del _L1_xattn_all

    def _L1_attn_setup():
        import math
        import jax, jax.numpy as jnp
        import numpy as np
        B, C, D = (4, 1024, 512)
        DQ = DV = 64
        H = 16
        key = jax.random.key(seed)
        kx, kq, kk, kv, kw = jax.random.split(key, 5)
        x = jax.random.normal(kx, (B, C, D), dtype=jnp.float32)
        Q = jax.random.normal(kq, (DQ, D, H), dtype=jnp.float32) / math.sqrt(D)
        K = jax.random.normal(kk, (DQ, D, H), dtype=jnp.float32) / math.sqrt(D)
        V = jax.random.normal(kv, (DV, D, H), dtype=jnp.float32) / math.sqrt(D)
        W = jax.random.normal(kw, (D, DV, H), dtype=jnp.float32) / math.sqrt(DV)
        return {'x': x, 'Q': Q, 'K': K, 'V': V, 'W': W}
    _L1_attn_all = _L1_attn_setup()
    _L1_attn_in = {k: v for k, v in _L1_attn_all.items() if k in ('Q', 'K', 'V', 'W')}
    del _L1_attn_all

    def _L1_ffn_setup():
        import jax, jax.numpy as jnp
        import numpy as np
        B, S, D, E, H, DO = (4, 1024, 512, 8, 2048, 512)
        TOP_K = 2
        LN_EPS = 1e-05
        key = jax.random.key(seed)
        ks = jax.random.split(key, 9)
        s = 0.02
        return {'x': jax.random.normal(ks[0], (B, S, D), dtype=jnp.float32), 'W1': jax.random.normal(ks[1], (E, D, H), dtype=jnp.float32) * s, 'b1': jnp.zeros((E, H), dtype=jnp.float32), 'W2': jax.random.normal(ks[2], (E, H, DO), dtype=jnp.float32) * s, 'b2': jnp.zeros((E, DO), dtype=jnp.float32), 'gate_W': jax.random.normal(ks[3], (D, E), dtype=jnp.float32) * s, 'shared_W': jax.random.normal(ks[4], (D, DO), dtype=jnp.float32) * s, 'shared_b': jnp.zeros((DO,), dtype=jnp.float32), 'gamma': jnp.ones((DO,), dtype=jnp.float32), 'beta': jnp.zeros((DO,), dtype=jnp.float32)}
    _L1_ffn_all = _L1_ffn_setup()
    _L1_ffn_in = {k: v for k, v in _L1_ffn_all.items() if k in ('W1', 'b1', 'W2', 'b2', 'gate_W', 'shared_W', 'shared_b', 'gamma', 'beta')}
    del _L1_ffn_all
    return {'x': x, 'ctx_768': ctx_768, 'mask_BxS_bf1': mask_BxS_bf1, 'mask_BxS2_bf1': mask_BxS2_bf1, 'L0_xattn_Wq': _L0_xattn_in['Wq'], 'L0_xattn_Wk': _L0_xattn_in['Wk'], 'L0_xattn_Wv': _L0_xattn_in['Wv'], 'L0_xattn_Wout': _L0_xattn_in['Wout'], 'L0_xattn_bout': _L0_xattn_in['bout'], 'L0_attn_Wq': _L0_attn_in['Wq'], 'L0_attn_Wk': _L0_attn_in['Wk'], 'L0_attn_Wv': _L0_attn_in['Wv'], 'L0_ffn_router_weight': _L0_ffn_in['router_weight'], 'L0_ffn_router_bias': _L0_ffn_in['router_bias'], 'L0_ffn_gate_up_proj': _L0_ffn_in['gate_up_proj'], 'L0_ffn_gate_up_bias': _L0_ffn_in['gate_up_bias'], 'L0_ffn_down_proj': _L0_ffn_in['down_proj'], 'L0_ffn_down_bias': _L0_ffn_in['down_bias'], 'L1_xattn_Wq': _L1_xattn_in['Wq'], 'L1_xattn_Wk': _L1_xattn_in['Wk'], 'L1_xattn_Wv': _L1_xattn_in['Wv'], 'L1_xattn_W_film_in': _L1_xattn_in['W_film_in'], 'L1_xattn_b_film_in': _L1_xattn_in['b_film_in'], 'L1_xattn_W_film_out': _L1_xattn_in['W_film_out'], 'L1_xattn_b_film_out': _L1_xattn_in['b_film_out'], 'L1_xattn_g_norm_in': _L1_xattn_in['g_norm_in'], 'L1_xattn_b_norm_in': _L1_xattn_in['b_norm_in'], 'L1_xattn_g_norm_out': _L1_xattn_in['g_norm_out'], 'L1_xattn_b_norm_out': _L1_xattn_in['b_norm_out'], 'L1_xattn_g_ffn': _L1_xattn_in['g_ffn'], 'L1_xattn_b_ffn': _L1_xattn_in['b_ffn'], 'L1_xattn_W1': _L1_xattn_in['W1'], 'L1_xattn_b1': _L1_xattn_in['b1'], 'L1_xattn_W2': _L1_xattn_in['W2'], 'L1_xattn_b2': _L1_xattn_in['b2'], 'L1_xattn_log_dt': _L1_xattn_in['log_dt'], 'L1_xattn_A_re': _L1_xattn_in['A_re'], 'L1_xattn_A_im': _L1_xattn_in['A_im'], 'L1_xattn_C_re': _L1_xattn_in['C_re'], 'L1_xattn_C_im': _L1_xattn_in['C_im'], 'L1_xattn_D_skip': _L1_xattn_in['D_skip'], 'L1_xattn_mod_gate': _L1_xattn_in['mod_gate'], 'L1_attn_Q': _L1_attn_in['Q'], 'L1_attn_K': _L1_attn_in['K'], 'L1_attn_V': _L1_attn_in['V'], 'L1_attn_W': _L1_attn_in['W'], 'L1_ffn_W1': _L1_ffn_in['W1'], 'L1_ffn_b1': _L1_ffn_in['b1'], 'L1_ffn_W2': _L1_ffn_in['W2'], 'L1_ffn_b2': _L1_ffn_in['b2'], 'L1_ffn_gate_W': _L1_ffn_in['gate_W'], 'L1_ffn_shared_W': _L1_ffn_in['shared_W'], 'L1_ffn_shared_b': _L1_ffn_in['shared_b'], 'L1_ffn_gamma': _L1_ffn_in['gamma'], 'L1_ffn_beta': _L1_ffn_in['beta']}

def reference(x, ctx_768, mask_BxS_bf1, mask_BxS2_bf1, L0_xattn_Wq, L0_xattn_Wk, L0_xattn_Wv, L0_xattn_Wout, L0_xattn_bout, L0_attn_Wq, L0_attn_Wk, L0_attn_Wv, L0_ffn_router_weight, L0_ffn_router_bias, L0_ffn_gate_up_proj, L0_ffn_gate_up_bias, L0_ffn_down_proj, L0_ffn_down_bias, L1_xattn_Wq, L1_xattn_Wk, L1_xattn_Wv, L1_xattn_W_film_in, L1_xattn_b_film_in, L1_xattn_W_film_out, L1_xattn_b_film_out, L1_xattn_g_norm_in, L1_xattn_b_norm_in, L1_xattn_g_norm_out, L1_xattn_b_norm_out, L1_xattn_g_ffn, L1_xattn_b_ffn, L1_xattn_W1, L1_xattn_b1, L1_xattn_W2, L1_xattn_b2, L1_xattn_log_dt, L1_xattn_A_re, L1_xattn_A_im, L1_xattn_C_re, L1_xattn_C_im, L1_xattn_D_skip, L1_xattn_mod_gate, L1_attn_Q, L1_attn_K, L1_attn_V, L1_attn_W, L1_ffn_W1, L1_ffn_b1, L1_ffn_W2, L1_ffn_b2, L1_ffn_gate_W, L1_ffn_shared_W, L1_ffn_shared_b, L1_ffn_gamma, L1_ffn_beta):
    import jax
    import jax.numpy as jnp

    def _L0_xattn_ref(x, context, Wq, Wk, Wv, Wout, bout):
        import jax, jax.numpy as jnp
        import numpy as np
        HEADS = 8
        DIM_HEAD = 64
        SCALE = DIM_HEAD ** (-0.5)
        b, n, _ = x.shape
        m = context.shape[1]
        q = (x @ Wq).reshape(b, n, HEADS, DIM_HEAD)
        k = (context @ Wk).reshape(b, m, HEADS, DIM_HEAD)
        v = (context @ Wv).reshape(b, m, HEADS, DIM_HEAD)
        sim = jnp.einsum('bihd,bjhd->bhij', q, k) * SCALE
        attn = jax.nn.softmax(sim, axis=-1)
        out = jnp.einsum('bhij,bjhd->bihd', attn, v).reshape(b, n, HEADS * DIM_HEAD)
        return out @ Wout + bout

    def _L0_attn_ref(x, Wq, Wk, Wv):
        import jax, jax.numpy as jnp
        import numpy as np

        def _rope_tables(T, d):
            half = d // 2
            i = jnp.arange(half, dtype=jnp.float32)
            theta = 10000.0 ** (-2.0 * i / d)
            m = jnp.arange(T, dtype=jnp.float32)[:, None]
            ang = m * theta[None, :]
            return (jnp.cos(ang), jnp.sin(ang))

        def _rotate(v, cos, sin):
            B, T, d = v.shape
            half = d // 2
            v2 = v.reshape(B, T, half, 2)
            even, odd = (v2[..., 0], v2[..., 1])
            c = cos[None, :, :]
            s = sin[None, :, :]
            new_even = even * c - odd * s
            new_odd = even * s + odd * c
            return jnp.stack([new_even, new_odd], axis=-1).reshape(B, T, d)
        B, T, d = x.shape
        cos, sin = _rope_tables(T, d)
        Q = jnp.einsum('btd,ed->bte', x, Wq)
        K = jnp.einsum('btd,ed->bte', x, Wk)
        V = jnp.einsum('btd,ed->bte', x, Wv)
        Qr = _rotate(Q, cos, sin)
        Kr = _rotate(K, cos, sin)
        scores = jnp.einsum('bqd,bkd->bqk', Qr, Kr) / jnp.sqrt(jnp.float32(d))
        mask = jnp.tril(jnp.ones((T, T), dtype=bool), k=1)
        scores = jnp.where(mask[None, :, :], scores, -jnp.inf)
        attn = jax.nn.softmax(scores, axis=-1)
        out = jnp.einsum('bqk,bkd->bqd', attn, V)
        return out

    def _L0_ffn_ref(hidden_states, router_weight, router_bias, gate_up_proj, gate_up_bias, down_proj, down_bias):
        import jax, jax.numpy as jnp
        import numpy as np
        ALPHA = 1.702
        LIMIT = 7.0
        K = 2
        B, S, H = hidden_states.shape
        E = router_weight.shape[0]
        I = down_proj.shape[1]
        T = B * S
        flat = hidden_states.reshape(T, H)
        logits = flat @ router_weight.T + router_bias
        scores = jax.nn.softmax(logits, axis=-1)
        topk_vals, topk_idx = jax.lax.top_k(scores, K)
        w = jnp.zeros((T, E), scores.dtype).at[jnp.arange(T)[:, None], topk_idx].set(topk_vals)
        gu = jnp.einsum('th,ehf->tef', flat, gate_up_proj) + gate_up_bias
        gate = jnp.minimum(gu[..., :I], LIMIT)
        up = jnp.clip(gu[..., I:], -LIMIT, LIMIT)
        glu = gate * jax.nn.sigmoid(gate * ALPHA)
        act = (up + 1.0) * glu
        down = jnp.einsum('tei,eih->teh', act, down_proj) + down_bias
        out = jnp.einsum('teh,te->th', down, w)
        return out.reshape(B, S, H)

    def _L1_xattn_ref(x_text, x_vision, text_mask, vision_mask, Wq, Wk, Wv, W_film_in, b_film_in, W_film_out, b_film_out, g_norm_in, b_norm_in, g_norm_out, b_norm_out, g_ffn, b_ffn, W1, b1, W2, b2, log_dt, A_re, A_im, C_re, C_im, D_skip, mod_gate):
        import jax, jax.numpy as jnp
        import numpy as np
        B, T, DT, G, DV = (16, 256, 512, 288, 384)
        H, DH = (4, 32)
        INNER = H * DH
        HID = 4 * DT
        N_STATE = 64
        K_TOP = 32

        def layernorm(x, g, b, eps=1e-05):
            m = x.mean(-1, keepdims=True)
            v = x.var(-1, keepdims=True)
            return (x - m) * jax.lax.rsqrt(v + eps) * g + b

        def s4d(x, log_dt, A_re, A_im, C_re, C_im, D_skip):
            Bb, L, D = x.shape
            dt = jnp.exp(log_dt)
            A = A_re + 1j * A_im
            C = C_re + 1j * C_im
            dtA = dt[:, None] * A
            dC = C * (jnp.exp(dtA) - 1.0) / A
            powers = jnp.exp(dtA[:, :, None] * jnp.arange(L))
            K = 2.0 * jnp.einsum('dn,dnl->dl', dC, powers).real
            n = 2 * L
            Kf = jnp.fft.rfft(K, n=n, axis=-1)
            xf = jnp.fft.rfft(x, n=n, axis=1)
            y = jnp.fft.irfft(xf * Kf.T[None], n=n, axis=1)[:, :L]
            return y + x * D_skip
        Bb, Tt, D = x_text.shape
        Gg = x_vision.shape[1]
        Q = (x_text @ Wq).reshape(Bb, Tt, H, DH)
        K = (x_vision @ Wk).reshape(Bb, Gg, H, DH)
        scores = jnp.einsum('bthd,bghd->bhtg', Q, K) / np.sqrt(DH).astype(np.float32)
        scores = jnp.where(vision_mask[:, None, None, :], scores, -jnp.inf)
        topv, topi = jax.lax.top_k(scores, K_TOP)
        probs = jax.nn.softmax(topv, axis=-1)
        bi = jnp.arange(Bb)[:, None, None, None]
        hi = jnp.arange(H)[None, :, None, None]
        ti = jnp.arange(Tt)[None, None, :, None]
        attn = jnp.zeros_like(scores).at[bi, hi, ti, topi].set(probs)
        attn_mean = attn.mean(axis=1)
        V = x_vision @ Wv
        c_t = jnp.einsum('btg,bgd->btd', attn_mean, V)
        c_t = c_t * text_mask[..., None]
        x = layernorm(x_text, g_norm_in, b_norm_in)
        scale_in, shift_in = jnp.split(c_t @ W_film_in + b_film_in, 2, axis=-1)
        x = x * (1.0 + mod_gate * scale_in) + mod_gate * shift_in
        y = s4d(x, log_dt, A_re, A_im, C_re, C_im, D_skip)
        scale_out, shift_out = jnp.split(c_t @ W_film_out + b_film_out, 2, axis=-1)
        y = y * (1.0 + mod_gate * scale_out) + mod_gate * shift_out
        xt = x_text + y
        h = layernorm(xt, g_ffn, b_ffn)
        h = jax.nn.gelu(h @ W1 + b1, approximate=False) @ W2 + b2
        xt = xt + h
        return layernorm(xt, g_norm_out, b_norm_out)

    def _L1_attn_ref(x, Q, K, V, W):
        import math
        import jax, jax.numpy as jnp
        import numpy as np
        B, C, D = (4, 1024, 512)
        DQ = DV = 64
        H = 16
        d_query, d_embed, num_heads = Q.shape
        d_value = V.shape[0]
        sq = math.sqrt(d_query / d_embed)
        sv = math.sqrt(d_value / d_embed)
        q = jnp.einsum('qdh,bcd->bhcq', Q, x) * sq
        k = jnp.einsum('qdh,bcd->bhcq', K, x) * sq
        v = jnp.einsum('vdh,bcd->bhcv', V, x) * sv
        att = jnp.einsum('bhcq,bhCq->bhcC', q, k) / d_query
        T = x.shape[1]
        causal = jnp.arange(T)[:, None] >= jnp.arange(T)[None, :]
        att = jnp.where(causal, att, -jnp.inf)
        p = jax.nn.softmax(att, axis=-1)
        y = jnp.einsum('bhcC,bhCv->bhcv', p, v)
        z = jnp.einsum('dvh,bhcv->bcd', W, y) * (math.sqrt(d_embed / d_value) / num_heads)
        return z

    def _L1_ffn_ref(x, W1, b1, W2, b2, gate_W, shared_W, shared_b, gamma, beta):
        import jax, jax.numpy as jnp
        import numpy as np
        B, S, D, E, H, DO = (4, 1024, 512, 8, 2048, 512)
        TOP_K = 2
        LN_EPS = 1e-05
        d = x.shape[-1]
        flat = x.reshape(-1, d)
        n_exp = gate_W.shape[-1]
        probs = jax.nn.softmax(flat @ gate_W, axis=-1)
        topk_w, topk_idx = jax.lax.top_k(probs, TOP_K)
        topk_w = topk_w / topk_w.sum(axis=-1, keepdims=True)
        combine = (jax.nn.one_hot(topk_idx, n_exp, dtype=flat.dtype) * topk_w[..., None]).sum(axis=1)
        out = 0.5 * jax.nn.gelu(flat @ shared_W + shared_b, approximate=False)
        for e in range(n_exp):
            h = jax.nn.gelu(flat @ W1[e] + b1[e], approximate=False)
            out = out + combine[:, e:e + 1] * (h @ W2[e] + b2[e])
        mean = out.mean(axis=-1, keepdims=True)
        var = ((out - mean) ** 2).mean(axis=-1, keepdims=True)
        out = (out - mean) * jax.lax.rsqrt(var + LN_EPS) * gamma + beta
        return out.reshape(*x.shape[:-1], out.shape[-1])
    x = x + _L0_xattn_ref(_layernorm(x, axis=-1), ctx_768, L0_xattn_Wq, L0_xattn_Wk, L0_xattn_Wv, L0_xattn_Wout, L0_xattn_bout)
    x = x + _L0_attn_ref(_layernorm(x, axis=-1), L0_attn_Wq, L0_attn_Wk, L0_attn_Wv)
    x = x + _L0_ffn_ref(_layernorm(x, axis=-1), L0_ffn_router_weight, L0_ffn_router_bias, L0_ffn_gate_up_proj, L0_ffn_gate_up_bias, L0_ffn_down_proj, L0_ffn_down_bias)
    x = x + _L1_xattn_ref(_layernorm(x, axis=-1), ctx_768, mask_BxS_bf1, mask_BxS2_bf1, L1_xattn_Wq, L1_xattn_Wk, L1_xattn_Wv, L1_xattn_W_film_in, L1_xattn_b_film_in, L1_xattn_W_film_out, L1_xattn_b_film_out, L1_xattn_g_norm_in, L1_xattn_b_norm_in, L1_xattn_g_norm_out, L1_xattn_b_norm_out, L1_xattn_g_ffn, L1_xattn_b_ffn, L1_xattn_W1, L1_xattn_b1, L1_xattn_W2, L1_xattn_b2, L1_xattn_log_dt, L1_xattn_A_re, L1_xattn_A_im, L1_xattn_C_re, L1_xattn_C_im, L1_xattn_D_skip, L1_xattn_mod_gate)
    x = x + _L1_attn_ref(_layernorm(x, axis=-1), L1_attn_Q, L1_attn_K, L1_attn_V, L1_attn_W)
    x = x + _L1_ffn_ref(_layernorm(x, axis=-1), L1_ffn_W1, L1_ffn_b1, L1_ffn_W2, L1_ffn_b2, L1_ffn_gate_W, L1_ffn_shared_W, L1_ffn_shared_b, L1_ffn_gamma, L1_ffn_beta)
    return x

_drawn_inputs = setup_inputs


def setup_inputs(seed=0):
    import zlib

    import numpy as np

    out = dict(_drawn_inputs(seed))
    spreads = {'L0_ffn_router_bias': (0.0, 0.8),
     'L0_ffn_gate_up_bias': (0.0, 0.1),
     'L0_ffn_down_bias': (0.0, 0.1),
     'L1_xattn_b_film_in': (0.0, 0.1),
     'L1_xattn_b_film_out': (0.0, 0.1),
     'L1_xattn_g_norm_in': (1.0, 0.2),
     'L1_xattn_b_norm_in': (0.0, 0.1),
     'L1_xattn_g_norm_out': (1.0, 0.2),
     'L1_xattn_b_norm_out': (0.0, 0.1),
     'L1_xattn_g_ffn': (1.0, 0.2),
     'L1_xattn_b_ffn': (0.0, 0.311),
     'L1_xattn_b1': (0.0, 0.272),
     'L1_xattn_b2': (0.0, 0.1),
     'L1_xattn_A_re': (-0.5, 0.2),
     'L1_ffn_b1': (0.0, 0.1),
     'L1_ffn_b2': (0.0, 0.1),
     'L1_ffn_shared_b': (0.0, 0.1),
     'L1_ffn_gamma': (1.0, 0.2),
     'L1_ffn_beta': (0.0, 0.1)}
    factors = {'L1_attn_Q': 8.0, 'L1_attn_K': 8.0}
    for name, (base, spread) in spreads.items():
        noise = np.random.default_rng([zlib.crc32(name.encode()), seed]).standard_normal(out[name].shape)
        drawn = base * np.exp(spread * noise) if base else spread * noise
        out[name] = jnp.asarray(drawn.astype(out[name].dtype))
    for name, factor in factors.items():
        out[name] = (out[name] * factor).astype(out[name].dtype)
    return out
```

```python
import math
from contextlib import ExitStack

import numpy as np
import concourse.bass as bass
from concourse import mybir

F32 = mybir.dt.float32
U8 = mybir.dt.uint8
ALU = mybir.AluOpType
ACT = mybir.ActivationFunctionType
AXIS = mybir.AxisListType

P = 128
B, S, D = 8, 64, 512
TOK = B * S
TT = TOK // P
KC = D // P
CTX, CD = 1601, 384
CC = CD // P
KT = -(-CTX // P)
LAST = CTX - (KT - 1) * P
EPS = 1e-5
PRIMED = 1
NEG = -1e30
EXPERTS = 8
PI = math.pi


class Core:

    def __init__(self, nc, ctx):
        self.nc, self.ctx = nc, ctx

    def sb(self, ctx, name, shape, dt=F32):
        return ctx.enter_context(self.nc.sbuf_tensor(name, list(shape), dt))

    def pb(self, ctx, name, shape, dt=F32):
        return ctx.enter_context(self.nc.psum_tensor(name, list(shape), dt))

    def sems(self, ctx, stage, names):
        made = [self.nc.alloc_semaphore(name=f"{stage}_{n}") for n in names.split()]

        def release():
            self.nc.clear_and_free_semaphores(made)
            self.nc.all_engine_barrier()

        ctx.callback(release)
        return made

    @staticmethod
    def prime(engine, *semaphores):
        for semaphore in semaphores:
            engine.sem_inc(semaphore, PRIMED)


def bcast(v, parts=P):
    return v.partition_broadcast(parts)


def norm_stage(core, name, src, normed, normed_t, ident, gamma=None, beta=None, out=None):
    nc = core.nc
    with ExitStack() as ctx:
        stats = core.sb(ctx, f"{name}_stats", [P, TT, 6])
        mv = core.sb(ctx, f"{name}_mv", [P, TT, 2])
        var = core.sb(ctx, f"{name}_var", [P, TT])
        half = core.sb(ctx, f"{name}_half", [P, TT])
        rstd = core.sb(ctx, f"{name}_rstd", [P, TT])
        tps = core.pb(ctx, f"{name}_tps", [P, TT, KC, P]) if normed_t is not None else None
        stats_ready, mv_ready, rstd_ready, normed_ready, t_ready, t_used = core.sems(
            ctx, name, "stats_ready mv_ready rstd_ready normed_ready t_ready t_used")
        steps = 1 + (gamma is not None) + (beta is not None)
        with nc.Block() as block:
            @block.vector
            def _(dve):
                for t in range(TT):
                    nc.vector.bn_stats(stats[:, t, :], src[:, t, :]).then_inc(stats_ready, 1)
                for t in range(TT):
                    dve.wait_ge(stats_ready, t + 1)
                    nc.vector.bn_aggr(mv[:, t, :], stats[:, t, :]).then_inc(mv_ready, 1)
                dve.wait_ge(rstd_ready, 3)
                for t in range(TT):
                    nc.vector.tensor_scalar(normed[:, t, :], src[:, t, :], mv[:, t, 0:1], rstd[:, t:t + 1],
                                            ALU.subtract, ALU.mult).then_inc(normed_ready, 1)
                if gamma is not None:
                    for t in range(TT):
                        dve.wait_ge(normed_ready, t + 1)
                        nc.vector.tensor_tensor(normed[:, t, :], normed[:, t, :], gamma[:, :], ALU.mult).then_inc(normed_ready, 1)
                if beta is not None:
                    for t in range(TT):
                        dve.wait_ge(normed_ready, TT + t + 1)
                        nc.vector.tensor_tensor(normed[:, t, :], normed[:, t, :], beta[:, :], ALU.add).then_inc(normed_ready, 1)
                if out is not None:
                    for t in range(TT):
                        dve.wait_ge(normed_ready, (steps - 1) * TT + t + 1)
                        nc.vector.tensor_tensor(out[:, t, :], out[:, t, :], normed[:, t, :], ALU.add)

            @block.gpsimd
            def _(pool):
                nc.gpsimd.memset(half[:, :], -0.5).then_inc(rstd_ready, 1)
                pool.wait_ge(mv_ready, TT)
                nc.gpsimd.tensor_scalar_add(var[:, :], mv[:, :, 1], EPS).then_inc(rstd_ready, 1)
                pool.wait_ge(rstd_ready, 2)
                nc.gpsimd.tensor_tensor(rstd[:, :], var[:, :], half[:, :], ALU.pow).then_inc(rstd_ready, 1)

            if normed_t is not None:
                @block.tensor
                def _(pe):
                    for t in range(TT):
                        pe.wait_ge(normed_ready, (steps - 1) * TT + t + 1)
                        for c in range(KC):
                            last = nc.tensor.transpose(tps[:, t, c, :], normed[:, t, c * P:(c + 1) * P], ident[:, :])
                        last.then_inc(t_ready, 1)

                @block.scalar
                def _(act):
                    for t in range(TT):
                        act.wait_ge(t_ready, t + 1)
                        nc.scalar.copy(normed_t[:, :, t * P:(t + 1) * P], tps[:, t, :, :])


def cross_attention_L0(core, x, xt, ident, w):
    nc = core.nc
    H, DH = 8, 64
    PAIR = 2
    UNITS = PAIR * H // 2
    with ExitStack() as ctx:
        qp = core.sb(ctx, "x0_qp", [P, CC, H, TOK])
        wv = core.sb(ctx, "x0_wv", [P, CC, D])
        wout = core.sb(ctx, "x0_wout", [P, KC, D])
        bout = core.sb(ctx, "x0_bout", [P, D])
        (w_in,) = core.sems(ctx, "x0", "w_in")
        with ExitStack() as c2:
            wq = core.sb(c2, "x0_wq", [P, KC, D])
            wkt = core.sb(c2, "x0_wkt", [P, KC, CD])
            qt = core.sb(c2, "x0_qt", [P, KC, TOK])
            ps = core.pb(c2, "x0_ps", [P, 8, 512])
            wq_in, q_ready, qt_ready, qp_ready, qp_used = core.sems(c2, "x0", "wq_in q_ready qt_ready qp_ready qp_used")
            with nc.Block() as block:
                @block.sync
                def _(sp):
                    sp.dma_start(wq[:, :, :], w["L0_xattn_Wq"].rearrange("(c p) n -> p c n", p=P)).then_inc(wq_in, 16)
                    sp.dma_start(wkt[:, :, :], w["L0_xattn_WkT"].rearrange("(c p) n -> p c n", p=P)).then_inc(wq_in, 16)
                    sp.dma_start(wv[:, :, :], w["L0_xattn_Wv"].rearrange("(c p) n -> p c n", p=P)).then_inc(w_in, 16)
                    sp.dma_start(wout[:, :, :], w["L0_xattn_Wout"].rearrange("(c p) n -> p c n", p=P)).then_inc(w_in, 16)
                    sp.dma_start(bout[:, :], bcast(w["L0_xattn_bout"])).then_inc(w_in, 16)

                @block.tensor
                def _(pe):
                    pe.wait_ge(wq_in, 32)
                    for m in range(KC):
                        for c in range(KC):
                            last = nc.tensor.matmul(ps[:, m, :], wq[:, c, m * P:(m + 1) * P], xt[:, c, :],
                                                    start=(c == 0), stop=(c == KC - 1))
                        last.then_inc(q_ready, 1)
                    for n in range(H * CC):
                        h, c = n // CC, n % CC
                        lo = (h % 2) * DH
                        pe.wait_ge(qt_ready, h // 2 + 1)
                        if n >= 4:
                            pe.wait_ge(qp_used, n - 3)
                        nc.tensor.matmul(ps[:, 4 + n % 4, :], wkt[lo:lo + DH, h // 2, c * P:(c + 1) * P],
                                         qt[lo:lo + DH, h // 2, :], start=True, stop=True).then_inc(qp_ready, 1)

                @block.scalar
                def _(act):
                    for m in range(KC):
                        act.wait_ge(q_ready, m + 1)
                        nc.scalar.mul(qt[:, m, :], ps[:, m, :], DH ** -0.5).then_inc(qt_ready, 1)
                    for n in range(H * CC):
                        act.wait_ge(qp_ready, n + 1)
                        nc.scalar.copy(qp[:, n % CC, n // CC, :], ps[:, 4 + n % 4, :]).then_inc(qp_used, 1)

        with ExitStack() as c2:
            cx = core.sb(c2, "x0_cx", [P, PAIR, KT, CD])
            cxt = core.sb(c2, "x0_cxt", [P, PAIR, CC, CTX])
            qs = core.sb(c2, "x0_qs", [P, 2, CC, P])
            pr = core.sb(c2, "x0_pr", [P, 2, CTX])
            pt = core.sb(c2, "x0_pt", [P, 2, KT, P])
            o = core.sb(c2, "x0_o", [P, 2, CD])
            nmax = core.sb(c2, "x0_nmax", [P, 2])
            total = core.sb(c2, "x0_total", [P, 2])
            inv = core.sb(c2, "x0_inv", [P, 2])
            s_ps = core.pb(c2, "x0_s_ps", [P, 4 * 512])
            t_ps = core.pb(c2, "x0_t_ps", [P, 2, 512])
            o_ps = core.pb(c2, "x0_o_ps", [P, 512])
            ot_ps = core.pb(c2, "x0_ot_ps", [P, 512])
            cx_in0, cx_in1, cxt_in0, cxt_in1, qs_ready, s_ready, max_ready, exp_ready, inv_ready, t_ready, pt_ready, \
                o_ready, o_scaled, ot_ready, ot_stored = core.sems(
                    c2, "x0", "cx_in0 cx_in1 cxt_in0 cxt_in1 qs_ready s_ready max_ready exp_ready inv_ready t_ready pt_ready "
                    "o_ready o_scaled ot_ready ot_stored")
            cx_in, cxt_in = (cx_in0, cx_in1), (cxt_in0, cxt_in1)
            GR = -(-KT // 4)
            groups = [(4 * g, min(KT, 4 * g + 4)) for g in range(GR)]
            ROUNDS = B // PAIR
            with nc.Block() as block:
                @block.sync
                def _(sp):
                    def load(b, j, i):
                        if i is not None:
                            sp.wait_ge(s_ready, i * UNITS + 4 * (j + 1) + PRIMED)
                        sp.dma_start(cxt[:, j, :, :],
                                     w["ctxT"][bass.ds(b, 1), :, :].rearrange("b (c p) n -> p (b c) n", p=P)).then_inc(cxt_in[j], 16)
                        if i is not None:
                            sp.wait_ge(o_ready, i * UNITS + 4 * (j + 1))
                        sp.dma_start(cx[:, j, 0:KT - 1, :],
                                     w["ctx"][bass.ds(b, 1), 0:(KT - 1) * P, :].rearrange("b (t p) n -> p (b t) n", p=P)
                                     ).then_inc(cx_in[j], 16)
                        sp.dma_start(cx[0:LAST, j, KT - 1, :],
                                     w["ctx"][bass.ds(b, 1), (KT - 1) * P:CTX, :].rearrange("b p n -> (b p) n")
                                     ).then_inc(cx_in[j], 16)

                    for j in range(PAIR):
                        load(j, j, None)
                    with sp.Fori(0, ROUNDS - 1) as i:
                        for j in range(PAIR):
                            load((i + 1) * PAIR + j, j, i)

                @block.gpsimd
                def _(pool):
                    with pool.Fori(0, ROUNDS) as i:
                        for u in range(UNITS):
                            j, r = u // 4, u % 4
                            if u >= 2:
                                pool.wait_ge(s_ready, i * UNITS + u - 1 + PRIMED)
                            else:
                                pool.wait_ge(s_ready, i * UNITS + PRIMED)
                            nc.gpsimd.tensor_copy(
                                qs[:, u % 2, :, :].rearrange("p c (h s) -> p c h s", h=2),
                                qp[:, :, 2 * r:2 * r + 2, bass.ds((i * PAIR + j) * S, S)]).then_inc(qs_ready, 1)

                @block.tensor
                def _(pe):
                    core.prime(pe, s_ready, t_ready)
                    with pe.Fori(0, ROUNDS) as i:
                        def scores_and_turn(u):
                            if u == UNITS:
                                for g in range(GR):
                                    turn(u - 1, g)
                                return
                            j = u // 4
                            pe.wait_ge(qs_ready, i * UNITS + u + 1)
                            if u % 4 == 0:
                                pe.wait_ge(cxt_in[j], i * 16 + 16)
                            pe.wait_ge(exp_ready, i * UNITS + u + PRIMED)
                            for n in range(4):
                                a, b = 512 * n, min(512 * n + 512, CTX)
                                for c in range(CC):
                                    last = nc.tensor.matmul(s_ps[:, a:b], qs[:, u % 2, c, :], cxt[:, j, c, a:b],
                                                            start=(c == 0), stop=(c == CC - 1))
                                if n == 3:
                                    last.then_inc(s_ready, 1)
                                if u >= 1:
                                    turn(u - 1, n)

                        def turn(u, g):
                            a, b = groups[g]
                            if g == 0:
                                pe.wait_ge(exp_ready, i * UNITS + u + 1 + PRIMED)
                            pe.wait_ge(pt_ready, i * (UNITS * GR) + max(u * GR + g - 1, 0) + PRIMED)
                            for t in range(a, b):
                                rows = P if t < KT - 1 else LAST
                                last = nc.tensor.transpose(t_ps[0:rows, g % 2, (t - a) * P:(t - a + 1) * P],
                                                           pr[:, u % 2, t * P:t * P + rows], ident[:, :])
                            last.then_inc(t_ready, 1)

                        def weigh(u):
                            j = u // 4
                            if u % 4 == 0:
                                pe.wait_ge(cx_in[j], i * 32 + 32)
                            pe.wait_ge(o_scaled, i * UNITS + u + PRIMED)
                            for t in range(KT):
                                if t % 4 == 0:
                                    pe.wait_ge(pt_ready, i * (UNITS * GR) + u * GR + t // 4 + 1 + PRIMED)
                                rows = P if t < KT - 1 else LAST
                                last = nc.tensor.matmul(o_ps[:, 0:CD], pt[0:rows, u % 2, t, :], cx[0:rows, j, t, :],
                                                        start=(t == 0), stop=(t == KT - 1))
                            last.then_inc(o_ready, 1)

                        def turn_out(u):
                            pe.wait_ge(o_scaled, i * UNITS + u + 1 + PRIMED)
                            pe.wait_ge(ot_stored, i * UNITS + u + PRIMED)
                            for c in range(CC):
                                last = nc.tensor.transpose(ot_ps[:, c * P:(c + 1) * P], o[:, u % 2, c * P:(c + 1) * P],
                                                           ident[:, :])
                            last.then_inc(ot_ready, 1)

                        scores_and_turn(0)
                        for u in range(UNITS):
                            scores_and_turn(u + 1)
                            weigh(u)
                            if u >= 1:
                                turn_out(u - 1)
                        turn_out(UNITS - 1)

                @block.vector
                def _(dve):
                    core.prime(dve, pt_ready, o_scaled, inv_ready)
                    with dve.Fori(0, ROUNDS) as i:
                        def row_max(u):
                            dve.wait_ge(s_ready, i * UNITS + u + 1 + PRIMED)
                            dve.wait_ge(exp_ready, i * UNITS + max(u - 1, 0) + PRIMED)
                            nc.vector.reduce_max(nmax[:, u % 2:u % 2 + 1], s_ps[:, 0:CTX], AXIS.X, negate=True).then_inc(max_ready, 1)

                        row_max(0)
                        for u in range(UNITS):
                            dve.wait_ge(exp_ready, i * UNITS + u + 1 + PRIMED)
                            nc.vector.reciprocal(inv[:, u % 2:u % 2 + 1], total[:, u % 2:u % 2 + 1]).then_inc(inv_ready, 1)
                            for g in (0, 2):
                                a, b = groups[g]
                                dve.wait_ge(t_ready, i * (UNITS * GR) + u * GR + g + 1 + PRIMED)
                                dve.wait_ge(pt_ready, i * (UNITS * GR) + u * GR + g + PRIMED)
                                if u >= 2:
                                    dve.wait_ge(o_ready, i * UNITS + u - 1)
                                nc.vector.tensor_copy(pt[:, u % 2, a:b, :],
                                                      t_ps[:, g % 2, 0:(b - a) * P].rearrange("p (t n) -> p t n", n=P)
                                                      ).then_inc(pt_ready, 1)
                            if u + 1 < UNITS:
                                row_max(u + 1)
                            dve.wait_ge(o_ready, i * UNITS + u + 1)
                            dve.wait_ge(inv_ready, i * UNITS + u + 1 + PRIMED)
                            if u >= 2:
                                dve.wait_ge(ot_ready, i * UNITS + u - 1)
                            nc.vector.tensor_scalar(o[:, u % 2, :], o_ps[:, 0:CD], inv[:, u % 2:u % 2 + 1], None,
                                                    ALU.mult).then_inc(o_scaled, 1)

                @block.scalar
                def _(act):
                    core.prime(act, exp_ready, ot_stored)
                    def store_out(act, i, u):
                        j, r = u // 4, u % 4
                        act.wait_ge(ot_ready, i * UNITS + u + 1)
                        nc.scalar.copy(qp[:, :, 2 * r:2 * r + 2, bass.ds((i * PAIR + j) * S, S)],
                                       ot_ps[:, 0:CC * P].rearrange("p (c h s) -> p c h s", c=CC, h=2)).then_inc(ot_stored, 1)

                    with act.Fori(0, ROUNDS) as i:
                        def exponent(u):
                            act.wait_ge(max_ready, i * UNITS + u + 1)
                            act.wait_ge(inv_ready, i * UNITS + max(u - 1, 0) + PRIMED)
                            act.wait_ge(t_ready, (i * UNITS + max(u - 1, 0)) * GR + PRIMED)
                            nc.scalar.activation(pr[:, u % 2, :], s_ps[:, 0:CTX], ACT.Exp, bias=nmax[:, u % 2:u % 2 + 1],
                                                 accum_out=total[:, u % 2:u % 2 + 1]).then_inc(exp_ready, 1)

                        exponent(0)
                        for u in range(UNITS):
                            for g in (1, 3):
                                a, b = groups[g]
                                rows = P if b < KT else LAST
                                act.wait_ge(t_ready, i * (UNITS * GR) + u * GR + g + 1 + PRIMED)
                                act.wait_ge(pt_ready, i * (UNITS * GR) + u * GR + g + PRIMED)
                                nc.scalar.copy(pt[0:rows, u % 2, a:b, :],
                                               t_ps[0:rows, g % 2, 0:(b - a) * P].rearrange("p (t n) -> p t n", n=P)
                                               ).then_inc(pt_ready, 1)
                            if u + 1 < UNITS:
                                exponent(u + 1)
                            if u >= 1:
                                store_out(act, i, u - 1)
                        store_out(act, i, UNITS - 1)

        with ExitStack() as c2:
            at = core.sb(c2, "x0_at", [P, KC, TOK])
            a_ps = core.pb(c2, "x0_a_ps", [P, KC, 512])
            y_ps = core.pb(c2, "x0_y_ps", [P, TT, 512])
            a_ready, at_ready, y_ready, xb_ready = core.sems(c2, "x0", "a_ready at_ready y_ready xb_ready")
            with nc.Block() as block:
                @block.tensor
                def _(pe):
                    pe.wait_ge(w_in, 48)
                    for m in range(KC):
                        for h in (2 * m, 2 * m + 1):
                            lo = (h % 2) * DH
                            for c in range(CC):
                                last = nc.tensor.matmul(a_ps[lo:lo + DH, m, :], wv[:, c, h * DH:(h + 1) * DH], qp[:, c, h, :],
                                                        start=(c == 0), stop=(c == CC - 1))
                        last.then_inc(a_ready, 1)
                    for m in range(KC):
                        pe.wait_ge(at_ready, m + 1)
                    for t in range(TT):
                        for c in range(KC):
                            last = nc.tensor.matmul(y_ps[:, t, :], at[:, c, t * P:(t + 1) * P], wout[:, c, :],
                                                    start=(c == 0), stop=(c == KC - 1))
                        last.then_inc(y_ready, 1)

                @block.scalar
                def _(act):
                    for m in range(KC):
                        act.wait_ge(a_ready, m + 1)
                        nc.scalar.copy(at[:, m, :], a_ps[:, m, :]).then_inc(at_ready, 1)

                @block.vector
                def _(dve):
                    dve.wait_ge(w_in, 48)
                    for t in range(TT):
                        nc.vector.tensor_tensor(x[:, t, :], x[:, t, :], bout[:, :], ALU.add).then_inc(xb_ready, 1)
                    for t in range(TT):
                        dve.wait_ge(y_ready, t + 1)
                        dve.wait_ge(xb_ready, t + 1)
                        nc.vector.tensor_tensor(x[:, t, :], x[:, t, :], y_ps[:, t, :], ALU.add)


def self_attention_L0(core, x, xt, ident, w):
    nc = core.nc
    HALF = KC // 2
    with ExitStack() as ctx:
        wq = core.sb(ctx, "s0_wq", [P, KC, D])
        wk = core.sb(ctx, "s0_wk", [P, KC, D])
        wv = core.sb(ctx, "s0_wv", [P, KC, D])
        cos = core.sb(ctx, "s0_cos", [P, HALF, TOK])
        sin = core.sb(ctx, "s0_sin", [P, HALF, TOK])
        mask = core.sb(ctx, "s0_mask", [P, P])
        rot = core.sb(ctx, "s0_rot", [P, 2, KC, TOK])
        tmp = core.sb(ctx, "s0_tmp", [P, 4, HALF, TOK])
        v = core.sb(ctx, "s0_v", [P, TT, D])
        pr = core.sb(ctx, "s0_pr", [P, TT, P])
        pt = core.sb(ctx, "s0_pt", [P, TT, P])
        red = core.sb(ctx, "s0_red", [P, 3, TT])
        in_q, in_k, in_v, in_tab, qk_ready, prod_ready, rot_ready, v_ready, vs_ready, s_ready, sm_ready, max_ready, \
            exp_ready, inv_ready, norm_ready, t_ready, pt_ready, y_ready = core.sems(
                ctx, "s0", "in_q in_k in_v in_tab qk_ready prod_ready rot_ready v_ready vs_ready s_ready sm_ready "
                "max_ready exp_ready inv_ready norm_ready t_ready pt_ready y_ready")
        qk_ps = core.pb(ctx, "s0_qk_ps", [P, KC, 512])
        r_ps = core.pb(ctx, "s0_r_ps", [P, 4, 512])
        with nc.Block() as block:
            @block.sync
            def _(sp):
                for dst, name, s in ((wq, "L0_attn_Wq", in_q), (wk, "L0_attn_Wk", in_k), (wv, "L0_attn_Wv", in_v)):
                    sp.dma_start(dst[:, :, :], w[name].rearrange("(c p) n -> p c n", p=P)).then_inc(s, 16)
                sp.dma_start(cos[:, :, :], w["rope_cos"].rearrange("(c p) n -> p c n", p=P)).then_inc(in_tab, 16)
                sp.dma_start(sin[:, :, :], w["rope_sin"].rearrange("(c p) n -> p c n", p=P)).then_inc(in_tab, 16)
                sp.dma_start(mask[:, :], w["mask_L0"]).then_inc(in_tab, 16)

            @block.tensor
            def _(pe):
                for a, (wt, s) in enumerate(((wq, in_q), (wk, in_k))):
                    pe.wait_ge(s, 16)
                    if a == 1:
                        pe.wait_ge(prod_ready, 4)
                    for m in range(KC):
                        for c in range(KC):
                            last = nc.tensor.matmul(qk_ps[:, m, :], wt[:, c, m * P:(m + 1) * P], xt[:, c, :],
                                                    start=(c == 0), stop=(c == KC - 1))
                    last.then_inc(qk_ready, 1)
                pe.wait_ge(in_v, 16)
                for t in range(TT):
                    for c in range(KC):
                        last = nc.tensor.matmul(r_ps[:, t, :], xt[:, c, t * P:(t + 1) * P], wv[:, c, :],
                                                start=(c == 0), stop=(c == KC - 1))
                    last.then_inc(v_ready, 1)
                pe.wait_ge(rot_ready, 4)
                for t in range(TT):
                    pe.wait_ge(vs_ready, t + 1)
                    for c in range(KC):
                        last = nc.tensor.matmul(r_ps[:, t, 0:P], rot[:, 0, c, t * P:(t + 1) * P], rot[:, 1, c, t * P:(t + 1) * P],
                                                start=(c == 0), stop=(c == KC - 1))
                    last.then_inc(s_ready, 1)
                for t in range(TT):
                    pe.wait_ge(norm_ready, t + 1)
                    nc.tensor.transpose(qk_ps[:, t, 0:P], pr[:, t, :], ident[:, :]).then_inc(t_ready, 1)
                for t in range(TT):
                    pe.wait_ge(pt_ready, t + 1)
                    nc.tensor.matmul(r_ps[:, t, :], pt[:, t, :], v[:, t, :], start=True, stop=True).then_inc(y_ready, 1)

            @block.vector
            def _(dve):
                dve.wait_ge(in_tab, 48)
                for a in range(2):
                    even, odd = qk_ps[:, 0:HALF, :], qk_ps[:, HALF:KC, :]
                    dve.wait_ge(qk_ready, a + 1)
                    dve.wait_ge(rot_ready, 2 * a)
                    for n, (part, table) in enumerate(((even, cos), (odd, sin), (even, sin), (odd, cos))):
                        nc.vector.tensor_tensor(tmp[:, n, :, :], part, table[:, :, :], ALU.mult).then_inc(prod_ready, 1)
                    dve.wait_ge(prod_ready, 4 * a + 4)
                    nc.vector.tensor_tensor(rot[:, a, 0:HALF, :], tmp[:, 0, :, :], tmp[:, 1, :, :], ALU.subtract).then_inc(rot_ready, 1)
                    nc.vector.tensor_tensor(rot[:, a, HALF:KC, :], tmp[:, 2, :, :], tmp[:, 3, :, :], ALU.add).then_inc(rot_ready, 1)
                for t in range(TT):
                    dve.wait_ge(s_ready, t + 1)
                    nc.vector.scalar_tensor_tensor(pr[:, t, :], r_ps[:, t, 0:P], D ** -0.5, mask[:, :],
                                                   ALU.mult, ALU.add).then_inc(sm_ready, 1)
                for t in range(TT):
                    dve.wait_ge(sm_ready, t + 1)
                    nc.vector.reduce_max(red[:, 0, t:t + 1], pr[:, t, :], AXIS.X, negate=True).then_inc(max_ready, 1)
                for t in range(TT):
                    dve.wait_ge(exp_ready, t + 1)
                    nc.vector.reciprocal(red[:, 2, t:t + 1], red[:, 1, t:t + 1]).then_inc(inv_ready, 1)
                for t in range(TT):
                    dve.wait_ge(inv_ready, t + 1)
                    nc.vector.tensor_scalar(pr[:, t, :], pr[:, t, :], red[:, 2, t:t + 1], None, ALU.mult).then_inc(norm_ready, 1)
                for t in range(TT):
                    dve.wait_ge(y_ready, t + 1)
                    nc.vector.tensor_tensor(x[:, t, :], x[:, t, :], r_ps[:, t, :], ALU.add)

            @block.scalar
            def _(act):
                for t in range(TT):
                    act.wait_ge(v_ready, t + 1)
                    nc.scalar.copy(v[:, t, :], r_ps[:, t, :]).then_inc(vs_ready, 1)
                for t in range(TT):
                    act.wait_ge(max_ready, t + 1)
                    nc.scalar.activation(pr[:, t, :], pr[:, t, :], ACT.Exp, bias=red[:, 0, t:t + 1],
                                         accum_out=red[:, 1, t:t + 1]).then_inc(exp_ready, 1)
                for t in range(TT):
                    act.wait_ge(t_ready, t + 1)
                    nc.scalar.copy(pt[:, t, :], qk_ps[:, t, 0:P]).then_inc(pt_ready, 1)


def route(core, name, normed_t, weight, bias, normalise, gate, gate_t, ident):
    nc = core.nc
    E = EXPERTS
    KEPT, FILL, TAKEN = 2, -1.0, -2.0
    with ExitStack() as ctx:
        wr = core.sb(ctx, f"{name}_wr", [P, KC, E])
        br = core.sb(ctx, f"{name}_br", [P, E])
        sc = core.sb(ctx, f"{name}_sc", [P, TT, 2 * E])
        rep = core.sb(ctx, f"{name}_rep", [P, TT, 2 * E])
        top = core.sb(ctx, f"{name}_top", [P, TT, E])
        red = core.sb(ctx, f"{name}_red", [P, 5, TT])
        l_ps = core.pb(ctx, f"{name}_l_ps", [P, 512])
        g_ps = core.pb(ctx, f"{name}_g_ps", [P, 512])
        w_in, l_ready, steps, exp_ready, gate_ready, gt_ready = core.sems(
            ctx, name, "w_in l_ready steps exp_ready gate_ready gt_ready")
        with nc.Block() as block:
            @block.sync
            def _(sp):
                sp.dma_start(wr[:, :, :], weight.rearrange("(c p) n -> p c n", p=P)).then_inc(w_in, 16)
                if bias is not None:
                    sp.dma_start(br[:, :], bcast(bias)).then_inc(w_in, 16)

            @block.tensor
            def _(pe):
                pe.wait_ge(w_in, 32 if bias is not None else 16)
                for t in range(TT):
                    for c in range(KC):
                        last = nc.tensor.matmul(l_ps[:, t * E:(t + 1) * E], normed_t[:, c, t * P:(t + 1) * P], wr[:, c, :],
                                                start=(c == 0), stop=(c == KC - 1))
                last.then_inc(l_ready, 1)
                pe.wait_ge(gate_ready, TT)
                for t in range(TT):
                    last = nc.tensor.transpose(g_ps[0:E, t * P:(t + 1) * P], gate[:, t, :], ident[:, :])
                last.then_inc(gt_ready, 1)

            @block.scalar
            def _(act):
                for t in range(TT):
                    act.wait_ge(steps, 3 + t + 1)
                    nc.scalar.activation(sc[:, t, 0:E], sc[:, t, 0:E], ACT.Exp, bias=red[:, 0, t:t + 1],
                                         accum_out=red[:, 1, t:t + 1]).then_inc(exp_ready, 1)
                act.wait_ge(gt_ready, 1)
                nc.scalar.copy(gate_t[:, :], g_ps[0:E, :])

            @block.vector
            def _(dve):
                done = [0]

                def step(instruction):
                    done[0] += 1
                    instruction.then_inc(steps, 1)

                def sync():
                    dve.wait_ge(steps, done[0])

                step(nc.vector.memset(sc[:, :, E:2 * E], FILL))
                step(nc.vector.memset(top[:, :, :], FILL))
                dve.wait_ge(l_ready, 1)
                logits = l_ps[:, 0:TT * E].rearrange("p (t e) -> p t e", e=E)
                if bias is not None:
                    step(nc.vector.tensor_tensor(sc[:, :, 0:E], logits, br[:, :].unsqueeze(1).broadcast_to([P, TT, E]), ALU.add))
                else:
                    step(nc.vector.tensor_copy(sc[:, :, 0:E], logits))
                sync()
                for t in range(TT):
                    step(nc.vector.reduce_max(red[:, 0, t:t + 1], sc[:, t, 0:E], AXIS.X, negate=True))
                dve.wait_ge(exp_ready, TT)
                step(nc.vector.reciprocal(red[:, 2, :], red[:, 1, :]))
                sync()
                for t in range(TT):
                    step(nc.vector.tensor_scalar(sc[:, t, 0:E], sc[:, t, 0:E], red[:, 2, t:t + 1], None, ALU.mult))
                sync()
                for t in range(TT):
                    step(nc.vector.max(rep[:, t, 0:E], sc[:, t, 0:E]))
                sync()
                step(nc.vector.tensor_copy(top[:, :, 0:KEPT], rep[:, :, 0:KEPT]))
                step(nc.vector.tensor_tensor(red[:, 3, :], rep[:, :, 0], rep[:, :, 1], ALU.add))
                sync()
                step(nc.vector.reciprocal(red[:, 4, :], red[:, 3, :]))
                for t in range(TT):
                    step(nc.vector.match_replace(rep[:, t, :], top[:, t, :], sc[:, t, :], TAKEN))
                sync()
                for t in range(TT):
                    ins = nc.vector.scalar_tensor_tensor(gate[:, t, :], rep[:, t, 0:E], TAKEN, sc[:, t, 0:E],
                                                         ALU.is_equal, ALU.mult)
                    if normalise:
                        step(ins)
                    else:
                        ins.then_inc(gate_ready, 1)
                if normalise:
                    sync()
                    for t in range(TT):
                        nc.vector.tensor_scalar(gate[:, t, :], gate[:, t, :], red[:, 4, t:t + 1], None,
                                                ALU.mult).then_inc(gate_ready, 1)


def experts(core, name, normed_t, acc, gate, gate_t, up_w, up_b, down_w, down_b, hidden, gated):
    nc = core.nc
    E = EXPERTS
    ALPHA, LIMIT = 1.702, 7.0
    WIDE = up_w.shape[2]
    HC = hidden // P
    UPS = WIDE // hidden
    PAIR = 2
    N = PAIR * HC
    ROUNDS = E // PAIR
    with ExitStack() as ctx:
        w1 = core.sb(ctx, f"{name}_w1", [P, PAIR, KC, WIDE])
        w2 = core.sb(ctx, f"{name}_w2", [P, PAIR, HC, D])
        b1 = core.sb(ctx, f"{name}_b1", [P, PAIR, UPS * HC])
        b2 = core.sb(ctx, f"{name}_b2", [E, D])
        g2 = core.sb(ctx, f"{name}_g2", [P, PAIR, TT])
        h = core.sb(ctx, f"{name}_h", [P, 2, TOK])
        tmp = core.sb(ctx, f"{name}_tmp", [P, 4, TOK]) if gated else None
        u_ps = core.pb(ctx, f"{name}_u_ps", [P, 2, 2, 512]) if gated else core.pb(ctx, f"{name}_u_ps", [P, 2, 1, 512])
        a_ps = core.pb(ctx, f"{name}_a_ps", [P, TT, 512])
        b2_in, w1_in0, w1_in1, w2_in0, w2_in1, up_ready, h_ready, down_ready, e_ready, acc_ready, g2_ready, parts, sig_ready = \
            core.sems(ctx, name, "b2_in w1_in0 w1_in1 w2_in0 w2_in1 up_ready h_ready down_ready e_ready acc_ready g2_ready "
                      "parts sig_ready")
        w1_in, w2_in = (w1_in0, w1_in1), (w2_in0, w2_in1)
        with nc.Block() as block:
            @block.sync
            def _(sp):
                def load(e, j, i):
                    if i is not None:
                        sp.wait_ge(down_ready, i * N + (j + 1) * HC)
                    sp.dma_start(w1[:, j, :, :], up_w[bass.ds(e, 1), :, :].rearrange("e (c p) n -> p (e c) n", p=P)).then_inc(w1_in[j], 16)
                    sp.dma_start(b1[:, j, :], up_b[bass.ds(e, 1), :, :].rearrange("e p n -> (e p) n")).then_inc(w1_in[j], 16)
                    sp.dma_start(w2[:, j, :, :], down_w[bass.ds(e, 1), :, :].rearrange("e (c p) n -> p (e c) n", p=P)).then_inc(w2_in[j], 16)

                load(0, 0, None)
                sp.dma_start(b2[:, :], down_b).then_inc(b2_in, 16)
                load(1, 1, None)
                with sp.Fori(0, ROUNDS - 1) as i:
                    for j in range(PAIR):
                        load((i + 1) * PAIR + j, j, i)

            @block.tensor
            def _(pe):
                pe.wait_ge(b2_in, 16)
                for t in range(TT):
                    last = nc.tensor.matmul(a_ps[:, t, :], gate_t[:, t * P:(t + 1) * P], b2[:, :], start=True, stop=True)
                last.then_inc(e_ready, 1)
                with pe.Fori(0, ROUNDS) as i:
                    def up(n):
                        j, c = n // HC, n % HC
                        if c == 0:
                            pe.wait_ge(w1_in[j], i * 32 + 32)
                        pe.wait_ge(h_ready, i * N + max(n - 1, 0) + PRIMED)
                        for a in range(UPS):
                            for k in range(KC):
                                last = nc.tensor.matmul(u_ps[:, n % 2, a, :], w1[:, j, k, a * hidden + c * P:a * hidden + (c + 1) * P],
                                                        normed_t[:, k, :], start=(k == 0), stop=(k == KC - 1))
                        last.then_inc(up_ready, 1)

                    def down(n):
                        j, c = n // HC, n % HC
                        if c == 0:
                            pe.wait_ge(w2_in[j], i * 16 + 16)
                            pe.wait_ge(acc_ready, (i * PAIR + j + 1) * TT)
                        pe.wait_ge(h_ready, i * N + n + 1 + PRIMED)
                        for t in range(TT):
                            last = nc.tensor.matmul(a_ps[:, t, :], h[:, n % 2, t * P:(t + 1) * P], w2[:, j, c, :],
                                                    start=(c == 0), stop=(c == HC - 1))
                        last.then_inc(down_ready, 1)

                    up(0)
                    for n in range(N):
                        if n + 1 < N:
                            up(n + 1)
                        down(n)

            @block.vector
            def _(dve):
                dve.wait_ge(e_ready, 1)
                for t in range(TT):
                    nc.vector.tensor_tensor(acc[:, t, :], acc[:, t, :], a_ps[:, t, :], ALU.add).then_inc(acc_ready, 1)
                with dve.Fori(0, ROUNDS) as i:
                    dve.wait_ge(acc_ready, (i * PAIR + 1) * TT)
                    nc.vector.tensor_copy(g2[:, :, :], gate[:, :, bass.ds(i * PAIR, PAIR)].rearrange("p t e -> p e t")).then_inc(g2_ready, 1)
                    for j in range(PAIR):
                        if gated:
                            for c in range(HC):
                                n = j * HC + c
                                dve.wait_ge(up_ready, i * N + n + 1)
                                dve.wait_ge(h_ready, i * N + n + PRIMED)
                                nc.vector.tensor_scalar(tmp[:, 0, :], u_ps[:, n % 2, 0, :], b1[:, j, c:c + 1], LIMIT,
                                                        ALU.add, ALU.min).then_inc(parts, 1)
                                nc.vector.tensor_scalar(tmp[:, 1, :], u_ps[:, n % 2, 1, :], b1[:, j, HC + c:HC + c + 1], LIMIT,
                                                        ALU.add, ALU.min).then_inc(parts, 1)
                                dve.wait_ge(parts, (i * N + n) * 4 + 2)
                                nc.vector.tensor_scalar(tmp[:, 2, :], tmp[:, 1, :], -LIMIT, 1.0, ALU.max, ALU.add).then_inc(parts, 1)
                                dve.wait_ge(sig_ready, i * N + n + 1)
                                nc.vector.tensor_tensor(tmp[:, 3, :], tmp[:, 0, :], tmp[:, 3, :], ALU.mult).then_inc(parts, 1)
                                dve.wait_ge(parts, (i * N + n) * 4 + 4)
                                if n >= 2:
                                    dve.wait_ge(down_ready, i * N + n - 1)
                                nc.vector.tensor_tensor(h[:, n % 2, :], tmp[:, 2, :], tmp[:, 3, :], ALU.mult).then_inc(h_ready, 1)
                        dve.wait_ge(down_ready, i * N + (j + 1) * HC)
                        dve.wait_ge(g2_ready, i + 1)
                        dve.wait_ge(acc_ready, (i * PAIR + j + 1) * TT)
                        for t in range(TT):
                            nc.vector.scalar_tensor_tensor(acc[:, t, :], a_ps[:, t, :], g2[:, j, t:t + 1], acc[:, t, :],
                                                           ALU.mult, ALU.add).then_inc(acc_ready, 1)

            @block.scalar
            def _(act):
                core.prime(act, h_ready)
                with act.Fori(0, ROUNDS) as i:
                    for n in range(N):
                        j, c = n // HC, n % HC
                        if gated:
                            act.wait_ge(parts, (i * N + n) * 4 + 1)
                            nc.scalar.activation(tmp[:, 3, :], tmp[:, 0, :], ACT.Sigmoid, scale=ALPHA).then_inc(sig_ready, 1)
                        else:
                            act.wait_ge(up_ready, i * N + n + 1)
                            if n >= 2:
                                act.wait_ge(down_ready, i * N + n - 1)
                            nc.scalar.activation(h[:, n % 2, :], u_ps[:, n % 2, 0, :], ACT.Gelu,
                                                 bias=b1[:, j, c:c + 1]).then_inc(h_ready, 1)


def moe_L0(core, x, xt, ident, w):
    with ExitStack() as ctx:
        gate = core.sb(ctx, "m0_gate", [P, TT, EXPERTS])
        gate_t = core.sb(ctx, "m0_gate_t", [EXPERTS, TOK])
        route(core, "r0", xt, w["L0_ffn_router_weight"], w["L0_ffn_router_bias"], False, gate, gate_t, ident)
        experts(core, "e0", xt, x, gate, gate_t, w["L0_ffn_gate_up_proj"], w["L0_ffn_gate_up_bias"],
                w["L0_ffn_down_proj"], w["L0_ffn_down_bias"], hidden=512, gated=True)


def moe_L1(core, x, xt, ident, w):
    nc = core.nc
    with ExitStack() as ctx:
        gate = core.sb(ctx, "m1_gate", [P, TT, EXPERTS])
        gate_t = core.sb(ctx, "m1_gate_t", [EXPERTS, TOK])
        acc = core.sb(ctx, "m1_acc", [P, TT, D])
        rows = core.sb(ctx, "m1_rows", [P, 3, D])
        with ExitStack() as c2:
            ws = core.sb(c2, "m1_ws", [P, KC, D])
            s_ps = core.pb(c2, "m1_s_ps", [P, TT, 512])
            w_in, s_ready, b_ready, g_ready = core.sems(c2, "m1", "w_in s_ready b_ready g_ready")
            with nc.Block() as block:
                @block.sync
                def _(sp):
                    sp.dma_start(ws[:, :, :], w["L1_ffn_shared_W"].rearrange("(c p) n -> p c n", p=P)).then_inc(w_in, 16)
                    for n, k in enumerate(("L1_ffn_shared_b", "L1_ffn_gamma", "L1_ffn_beta")):
                        sp.dma_start(rows[:, n, :], bcast(w[k])).then_inc(w_in, 16)
                    sp.wait_ge(w_in, 64)

                @block.tensor
                def _(pe):
                    pe.wait_ge(w_in, 64)
                    for t in range(TT):
                        for c in range(KC):
                            last = nc.tensor.matmul(s_ps[:, t, :], xt[:, c, t * P:(t + 1) * P], ws[:, c, :],
                                                    start=(c == 0), stop=(c == KC - 1))
                        last.then_inc(s_ready, 1)

                @block.vector
                def _(dve):
                    dve.wait_ge(w_in, 64)
                    for t in range(TT):
                        dve.wait_ge(s_ready, t + 1)
                        nc.vector.tensor_tensor(acc[:, t, :], s_ps[:, t, :], rows[:, 0, :], ALU.add).then_inc(b_ready, 1)
                    for t in range(TT):
                        dve.wait_ge(g_ready, t + 1)
                        nc.vector.tensor_scalar(acc[:, t, :], acc[:, t, :], 0.5, None, ALU.mult)

                @block.scalar
                def _(act):
                    for t in range(TT):
                        act.wait_ge(b_ready, t + 1)
                        nc.scalar.activation(acc[:, t, :], acc[:, t, :], ACT.Gelu).then_inc(g_ready, 1)
        route(core, "r1", xt, w["L1_ffn_gate_W"], None, True, gate, gate_t, ident)
        experts(core, "e1", xt, acc, gate, gate_t, w["L1_ffn_W1"], w["L1_ffn_b1"], w["L1_ffn_W2"], w["L1_ffn_b2"],
                hidden=2048, gated=False)
        norm_stage(core, "n6", acc, acc, None, ident, gamma=rows[:, 1, :], beta=rows[:, 2, :], out=x)


def self_attention_L1(core, x, xt, ident, w):
    nc = core.nc
    H, DH = 16, 64
    HC = H * DH // P
    G = 4
    NG = H // G
    U = TT * NG
    q_scale = math.sqrt(DH / D) ** 2 / DH
    z_scale = math.sqrt(DH / D) * math.sqrt(D / DH) / H
    with ExitStack() as ctx:
        wqkv = core.sb(ctx, "s1_wqkv", [P, 2, KC, H * DH])
        wz = core.sb(ctx, "s1_wz", [P, HC, D])
        mask = core.sb(ctx, "s1_mask", [P, G, P])
        qk = core.sb(ctx, "s1_qk", [P, 2, HC, TOK])
        v = core.sb(ctx, "s1_v", [P, TT, H * DH])
        pr = core.sb(ctx, "s1_pr", [P, 2, G, P])
        pt = core.sb(ctx, "s1_pt", [P, 2, G, P])
        yt = core.sb(ctx, "s1_yt", [P, 2, HC, P])
        red = core.sb(ctx, "s1_red", [P, 2, 3, G])
        in_q, in_k, in_v, in_m, p_ready, p_used, s_ready, steps, exp_ready, inv_ready, norm_ready, t_ready, \
            pt_ready, y_ready, yt_ready, z_ready, z_used = core.sems(
                ctx, "s1", "in_q in_k in_v in_m p_ready p_used s_ready steps exp_ready inv_ready norm_ready t_ready "
                "pt_ready y_ready yt_ready z_ready z_used")
        ps = core.pb(ctx, "s1_ps", [P, 8, 512])
        s_bank, t_bank, y_bank, z_bank = (0, 1), (2, 3), (4, 5), 6
        with nc.Block() as block:
            @block.sync
            def _(sp):
                def load(slot, name, s):
                    sp.dma_start(wqkv[:, slot, :, :], w[name].rearrange("(c p) n -> p c n", p=P)).then_inc(s, 16)
                load(0, "L1_attn_Q", in_q)
                load(1, "L1_attn_K", in_k)
                sp.dma_start(wz[:, :, :], w["L1_attn_W"].rearrange("(c p) n -> p c n", p=P)).then_inc(in_m, 16)
                sp.dma_start(mask[:, :, :], w["mask_L1"].unsqueeze(1).broadcast_to([P, G, P])).then_inc(in_m, 16)
                sp.wait_ge(p_ready, HC)
                load(0, "L1_attn_V", in_v)

            @block.tensor
            def _(pe):
                for n in range(2 * HC):
                    a, m = n // HC, n % HC
                    if m == 0:
                        pe.wait_ge((in_q, in_k)[a], 16)
                    if n >= 8:
                        pe.wait_ge(p_used, n - 7)
                    for c in range(KC):
                        last = nc.tensor.matmul(ps[:, n % 8, :], wqkv[:, a, c, m * P:(m + 1) * P], xt[:, c, :],
                                                start=(c == 0), stop=(c == KC - 1))
                    last.then_inc(p_ready, 1)
                pe.wait_ge(in_v, 16)
                for n in range(2 * TT):
                    t, half = n // 2, n % 2
                    pe.wait_ge(p_used, 2 * HC + n - 7)
                    for c in range(KC):
                        last = nc.tensor.matmul(ps[:, n % 8, :], xt[:, c, t * P:(t + 1) * P], wqkv[:, 0, c, half * 512:(half + 1) * 512],
                                                start=(c == 0), stop=(c == KC - 1))
                    last.then_inc(p_ready, 1)
                pe.wait_ge(p_used, 2 * HC + 2 * TT)

                def scores(u):
                    t, g = u // NG, u % NG
                    if u >= 2:
                        pe.wait_ge(steps, 4 * (u - 2) + 1)
                    lo = (g % 2) * DH
                    for k in range(G):
                        c = (g // 2) * G + k
                        last = nc.tensor.matmul(ps[:, s_bank[u % 2], k * P:(k + 1) * P], qk[lo:lo + DH, 0, c, t * P:(t + 1) * P],
                                                qk[lo:lo + DH, 1, c, t * P:(t + 1) * P], start=True, stop=True)
                    last.then_inc(s_ready, 1)

                def turn(u):
                    pe.wait_ge(norm_ready, u + 1)
                    if u >= 2:
                        pe.wait_ge(pt_ready, u - 1)
                    for k in range(G):
                        last = nc.tensor.transpose(ps[:, t_bank[u % 2], k * P:(k + 1) * P], pr[:, u % 2, k, :], ident[:, :])
                    last.then_inc(t_ready, 1)

                def weigh(u):
                    t, g = u // NG, u % NG
                    pe.wait_ge(pt_ready, u + 1)
                    if u >= 2:
                        pe.wait_ge(yt_ready, u - 1)
                    lo = (g % 2) * DH
                    for k in range(G):
                        h = 2 * ((g // 2) * G + k) + g % 2
                        last = nc.tensor.matmul(ps[lo:lo + DH, y_bank[u % 2], k * P:(k + 1) * P],
                                                v[:, t, h * DH:(h + 1) * DH], pt[:, u % 2, k, :], start=True, stop=True)
                    last.then_inc(y_ready, 1)

                def project(t):
                    pe.wait_ge(yt_ready, (t + 1) * NG)
                    if t >= 1:
                        pe.wait_ge(z_used, t)
                    for c in range(HC):
                        last = nc.tensor.matmul(ps[:, z_bank, :], yt[:, t % 2, c, :], wz[:, c, :], start=(c == 0), stop=(c == HC - 1))
                    last.then_inc(z_ready, 1)

                pe.wait_ge(in_m, 32)
                for u in range(U + 3):
                    if u < U:
                        scores(u)
                    if 1 <= u <= U:
                        turn(u - 1)
                    if 2 <= u <= U + 1:
                        weigh(u - 2)
                    if u >= 3 and (u - 3) % NG == NG - 1:
                        project((u - 3) // NG)

            @block.scalar
            def _(act):
                for n in range(0, 2 * HC + 2 * TT):
                    act.wait_ge(p_ready, n + 1)
                    if n < 2 * HC:
                        nc.scalar.copy(qk[:, n // HC, n % HC, :], ps[:, n % 8, :]).then_inc(p_used, 1)
                    else:
                        m = n - 2 * HC
                        nc.scalar.copy(v[:, m // 2, (m % 2) * 512:(m % 2 + 1) * 512], ps[:, n % 8, :]).then_inc(p_used, 1)
                for u in range(U + 2):
                    if u < U:
                        act.wait_ge(steps, 4 * u + 3)
                        nc.scalar.activation(pr[:, u % 2, :, :], pr[:, u % 2, :, :], ACT.Exp).then_inc(exp_ready, 1)
                    if 1 <= u <= U:
                        act.wait_ge(t_ready, u)
                        if u >= 3:
                            act.wait_ge(y_ready, u - 2)
                        nc.scalar.copy(pt[:, (u - 1) % 2, :, :], ps[:, t_bank[(u - 1) % 2], :].rearrange("p (g n) -> p g n", g=G)
                                       ).then_inc(pt_ready, 1)
                    if u >= 2:
                        t, g = (u - 2) // NG, (u - 2) % NG
                        act.wait_ge(y_ready, u - 1)
                        if t >= 2:
                            act.wait_ge(z_ready, t - 1)
                        lo = (g % 2) * DH
                        nc.scalar.copy(yt[lo:lo + DH, t % 2, (g // 2) * G:(g // 2 + 1) * G, :],
                                       ps[lo:lo + DH, y_bank[(u - 2) % 2], :].rearrange("p (c n) -> p c n", c=G)).then_inc(yt_ready, 1)

            @block.vector
            def _(dve):
                def add(dve, t):
                    dve.wait_ge(z_ready, t + 1)
                    nc.vector.scalar_tensor_tensor(x[:, t, :], ps[:, z_bank, :], z_scale, x[:, t, :],
                                                   ALU.mult, ALU.add).then_inc(z_used, 1)

                dve.wait_ge(in_m, 32)
                for u in range(U):
                    k = u % 2
                    dve.wait_ge(s_ready, u + 1)
                    if u >= 2:
                        dve.wait_ge(t_ready, u - 1)
                    nc.vector.scalar_tensor_tensor(pr[:, k, :, :], ps[:, s_bank[k], :].rearrange("p (g n) -> p g n", g=G), q_scale,
                                                   mask[:, :, :], ALU.mult, ALU.add).then_inc(steps, 1)
                    dve.wait_ge(steps, 4 * u + 1)
                    nc.vector.reduce_max(red[:, k, 0, :], pr[:, k, :, :], AXIS.X).then_inc(steps, 1)
                    dve.wait_ge(steps, 4 * u + 2)
                    nc.vector.tensor_tensor(pr[:, k, :, :], pr[:, k, :, :], red[:, k, 0, :].unsqueeze(2).broadcast_to([P, G, P]),
                                            ALU.subtract).then_inc(steps, 1)
                    dve.wait_ge(exp_ready, u + 1)
                    nc.vector.reduce_sum(red[:, k, 1, :], pr[:, k, :, :], AXIS.X).then_inc(steps, 1)
                    dve.wait_ge(steps, 4 * u + 4)
                    nc.vector.reciprocal(red[:, k, 2, :], red[:, k, 1, :]).then_inc(inv_ready, 1)
                    dve.wait_ge(inv_ready, u + 1)
                    nc.vector.tensor_tensor(pr[:, k, :, :], pr[:, k, :, :], red[:, k, 2, :].unsqueeze(2).broadcast_to([P, G, P]),
                                            ALU.mult).then_inc(norm_ready, 1)
                    if u >= NG + 2 and (u - 2) % NG == 0:
                        add(dve, (u - 2) // NG - 1)
                add(dve, TT - 1)


FREQ = 2 * S


def transforms():
    l = np.arange(S)[:, None]
    re = np.arange(S + 1)
    im = np.arange(1, S)
    ang = lambda k: 2 * np.pi * ((l * k) % FREQ) / FREQ
    spec = np.concatenate([np.cos(ang(re)), -np.sin(ang(im))], 1)
    swapped = np.concatenate([-np.sin(ang(re)), np.cos(ang(im))], 1)
    k_re = np.concatenate([np.cos(ang(re)), np.cos(ang(im))], 1)
    k_im = np.concatenate([np.sin(ang(re)), -np.sin(ang(im))], 1)
    weight = np.where((re == 0) | (re == S), 1.0, 2.0) / FREQ
    inverse = np.concatenate([np.cos(ang(re)) * weight, -np.sin(ang(im)) * 2.0 / FREQ], 1).T
    return {"dft_x": np.stack([spec, swapped]).astype(np.float32),
            "dft_k": np.stack([k_re, k_im]).astype(np.float32),
            "dft_inverse": inverse.astype(np.float32)}


def state_space_kernel(core, spec_k, ident, w):
    nc = core.nc
    N = 64
    M = KC * N
    STEP = 8
    R = S // STEP
    mult = [b for b in range(STEP)] + [STEP * a for a in range(R)]
    PI2_HI = 6.28125
    PI2_LO = 2 * PI - PI2_HI
    ROUND = 1.5 * 2 ** 23
    ANGLES_DONE, U_DONE = 42, 69
    TOP = float(np.nextafter(np.float32(PI), np.float32(0)))
    with ExitStack() as ctx:
        par = core.sb(ctx, "k_par", [P, 4, M])
        dt = core.sb(ctx, "k_dt", [P, KC])
        dta = core.sb(ctx, "k_dta", [P, 2, M])
        ang = core.sb(ctx, "k_ang", [P, 16, M])
        turns = core.sb(ctx, "k_turns", [P, 16, M])
        mag = core.sb(ctx, "k_mag", [P, 16, M])
        pw = core.sb(ctx, "k_pw", [P, 2, 16, M])
        sm = core.sb(ctx, "k_sm", [P, 10, M])
        u = core.sb(ctx, "k_u", [P, 2, R, M])
        prod = core.sb(ctx, "k_prod", [P, 2, R, STEP, N])
        k = core.sb(ctx, "k_k", [P, KC, S])
        kt = core.sb(ctx, "k_kt", [S, D])
        dft = core.sb(ctx, "k_dft", [S, 2, FREQ])
        t_ps = core.pb(ctx, "k_t_ps", [P, 512])
        f_ps = core.pb(ctx, "k_f_ps", [P, 2, 512])
        p_in, dt_ready, steps, act_steps, im_ready, k_ready, t_ready, kt_ready, f_ready = core.sems(
            ctx, "k", "p_in dt_ready steps act_steps im_ready k_ready t_ready kt_ready f_ready")
        def factors(part, c):
            ua = u[:, part, :, c * N:(c + 1) * N].unsqueeze(2).broadcast_to([P, R, STEP, N])
            wb = pw[:, part, 0:STEP, c * N:(c + 1) * N].unsqueeze(1).broadcast_to([P, R, STEP, N])
            return ua, wb

        with nc.Block() as block:
            @block.sync
            def _(sp):
                sp.dma_start(dt[:, :], w["L1_xattn_log_dt"]).then_inc(p_in, 16)
                for n, name in enumerate(("A_re", "A_im", "C_re", "C_im")):
                    sp.dma_start(par[:, n, :].rearrange("p (c n) -> p c n", c=KC),
                                 w[f"L1_xattn_{name}"].rearrange("(c p) n -> p c n", p=P)).then_inc(p_in, 16)
                sp.dma_start(dft[:, :, :], w["dft_k"].rearrange("a l f -> l a f")).then_inc(p_in, 16)

            @block.scalar
            def _(act):
                act.wait_ge(p_in, 96)
                nc.scalar.activation(dt[:, :], dt[:, :], ACT.Exp).then_inc(dt_ready, 1)
                act.wait_ge(steps, 2 + 16)
                nc.scalar.activation(mag[:, :, :], mag[:, :, :], ACT.Exp).then_inc(act_steps, 1)
                act.wait_ge(steps, ANGLES_DONE)
                nc.scalar.activation(pw[:, 1, :, :], ang[:, :, :], ACT.Sin).then_inc(act_steps, 1)
                nc.scalar.activation(pw[:, 0, :, :], turns[:, :, :], ACT.Sin).then_inc(act_steps, 1)
                act.wait_ge(f_ready, 1)
                nc.scalar.copy(spec_k[:, :, :], f_ps[:, :, :])

            @block.vector
            def _(dve):
                done = [0]

                def step(instruction):
                    done[0] += 1
                    instruction.then_inc(steps, 1)

                def sync():
                    dve.wait_ge(steps, done[0])

                V = nc.vector
                dve.wait_ge(dt_ready, 1)
                for a in range(2):
                    step(V.tensor_tensor(dta[:, a, :].rearrange("p (c n) -> p c n", c=KC), par[:, a, :].rearrange("p (c n) -> p c n", c=KC),
                                         dt[:, :].unsqueeze(2).broadcast_to([P, KC, N]), ALU.mult))
                sync()
                for m, f in enumerate(mult):
                    step(V.tensor_scalar(mag[:, m, :], dta[:, 0, :], float(f), None, ALU.mult))
                for m, f in enumerate(mult):
                    step(V.tensor_scalar(ang[:, m, :], dta[:, 1, :], float(f), None, ALU.mult))
                sync()
                step(V.tensor_scalar(turns[:, :, :], ang[:, :, :], 1 / (2 * PI), ROUND, ALU.mult, ALU.add))
                sync()
                step(V.tensor_scalar(turns[:, :, :], turns[:, :, :], ROUND, None, ALU.subtract))
                sync()
                step(V.scalar_tensor_tensor(ang[:, :, :], turns[:, :, :], -PI2_HI, ang[:, :, :], ALU.mult, ALU.add))
                sync()
                step(V.scalar_tensor_tensor(ang[:, :, :], turns[:, :, :], -PI2_LO, ang[:, :, :], ALU.mult, ALU.add))
                sync()
                step(V.tensor_scalar(turns[:, :, :], ang[:, :, :], PI / 2, -2 * PI, ALU.is_gt, ALU.mult))
                sync()
                step(V.scalar_tensor_tensor(turns[:, :, :], ang[:, :, :], PI / 2, turns[:, :, :], ALU.add, ALU.add))
                sync()
                step(V.tensor_scalar(turns[:, :, :], turns[:, :, :], TOP, -TOP, ALU.min, ALU.max))
                step(V.tensor_scalar(ang[:, :, :], ang[:, :, :], TOP, -TOP, ALU.min, ALU.max))
                assert done[0] == ANGLES_DONE
                dve.wait_ge(act_steps, 3)
                for a in range(2):
                    step(V.tensor_tensor(pw[:, a, :, :], pw[:, a, :, :], mag[:, :, :], ALU.mult))
                sync()
                are, aim, cre, cim = (par[:, n, :] for n in range(4))
                er, ei = sm[:, 0, :], pw[:, 1, 1, :]
                step(V.tensor_scalar(er, pw[:, 0, 1, :], -1.0, None, ALU.add))
                sync()
                step(V.tensor_tensor(sm[:, 1, :], cre, er, ALU.mult))
                step(V.tensor_tensor(sm[:, 2, :], cim, ei, ALU.mult))
                step(V.tensor_tensor(sm[:, 3, :], cre, ei, ALU.mult))
                step(V.tensor_tensor(sm[:, 4, :], cim, er, ALU.mult))
                step(V.tensor_tensor(sm[:, 5, :], are, are, ALU.mult))
                step(V.tensor_tensor(sm[:, 6, :], aim, aim, ALU.mult))
                sync()
                step(V.tensor_tensor(sm[:, 1, :], sm[:, 1, :], sm[:, 2, :], ALU.subtract))
                step(V.tensor_tensor(sm[:, 3, :], sm[:, 3, :], sm[:, 4, :], ALU.add))
                step(V.tensor_tensor(sm[:, 5, :], sm[:, 5, :], sm[:, 6, :], ALU.add))
                sync()
                step(V.reciprocal(sm[:, 5, :], sm[:, 5, :]))
                step(V.tensor_tensor(sm[:, 6, :], sm[:, 1, :], are, ALU.mult))
                step(V.tensor_tensor(sm[:, 7, :], sm[:, 3, :], aim, ALU.mult))
                step(V.tensor_tensor(sm[:, 8, :], sm[:, 3, :], are, ALU.mult))
                step(V.tensor_tensor(sm[:, 9, :], sm[:, 1, :], aim, ALU.mult))
                sync()
                step(V.tensor_tensor(sm[:, 6, :], sm[:, 6, :], sm[:, 7, :], ALU.add))
                step(V.tensor_tensor(sm[:, 8, :], sm[:, 8, :], sm[:, 9, :], ALU.subtract))
                sync()
                for n in (6, 8):
                    step(V.scalar_tensor_tensor(sm[:, n, :], sm[:, n, :], 2.0, sm[:, 5, :], ALU.mult, ALU.mult))
                sync()
                dr, di = (sm[:, n, :].unsqueeze(1).broadcast_to([P, R, M]) for n in (6, 8))
                pr8, pi8 = pw[:, 0, STEP:16, :], pw[:, 1, STEP:16, :]
                t0, t1 = mag[:, 0:R, :], mag[:, R:2 * R, :]
                step(V.tensor_tensor(u[:, 0, :, :], dr, pr8, ALU.mult))
                step(V.tensor_tensor(t0, di, pi8, ALU.mult))
                step(V.tensor_tensor(u[:, 1, :, :], dr, pi8, ALU.mult))
                step(V.tensor_tensor(t1, di, pr8, ALU.mult))
                sync()
                step(V.tensor_tensor(u[:, 0, :, :], u[:, 0, :, :], t0, ALU.subtract))
                step(V.scalar_tensor_tensor(u[:, 1, :, :], u[:, 1, :, :], -1.0, t1, ALU.mult, ALU.subtract))
                sync()
                assert done[0] == U_DONE
                for c in range(KC):
                    ur, wr = factors(0, c)
                    if c:
                        dve.wait_ge(k_ready, c)
                    step(V.tensor_tensor(prod[:, 0, :, :, :], ur, wr, ALU.mult))
                    sync()
                    dve.wait_ge(im_ready, 2 * c + 2)
                    V.reduce_sum(k[:, c, :].rearrange("p (a b) -> p a b", a=R), prod[:, 0, :, :, :], AXIS.X).then_inc(k_ready, 1)
                dve.wait_ge(t_ready, 1)
                V.tensor_copy(kt[:, :], t_ps[0:S, :]).then_inc(kt_ready, 1)

            @block.gpsimd
            def _(pool):
                for c in range(KC):
                    ui, wi = factors(1, c)
                    pool.wait_ge(steps, U_DONE + c)
                    pool.wait_ge(k_ready, c)
                    nc.gpsimd.tensor_tensor(prod[:, 1, :, :, :], ui, wi, ALU.mult).then_inc(im_ready, 1)
                    pool.wait_ge(im_ready, 2 * c + 1)
                    pool.wait_ge(steps, U_DONE + c + 1)
                    nc.gpsimd.tensor_tensor(prod[:, 0, :, :, :], prod[:, 0, :, :, :], prod[:, 1, :, :, :], ALU.add).then_inc(im_ready, 1)

            @block.tensor
            def _(pe):
                pe.wait_ge(k_ready, KC)
                for c in range(KC):
                    last = nc.tensor.transpose(t_ps[0:S, c * P:(c + 1) * P], k[:, c, :], ident[:, :])
                last.then_inc(t_ready, 1)
                pe.wait_ge(kt_ready, 1)
                for a in range(2):
                    last = nc.tensor.matmul(f_ps[:, a, :], dft[:, a, :], kt[:, :], start=True, stop=True)
                last.then_inc(f_ready, 1)


def cross_attention_L1(core, x, xn, xt, ident, w):
    with ExitStack() as ctx:
        ct = core.sb(ctx, "x1_ct", [P, CC, TOK])
        top_attention(core, xt, ct, ident, w)
        spec_k = core.sb(ctx, "x1_spec_k", [P, 2, D])
        state_space_kernel(core, spec_k, ident, w)
        mixing(core, x, xn, xt, ct, spec_k, ident, w)


def top_attention(core, xt, ct, ident, w):
    nc = core.nc
    H, DH, TOP = 4, 32, 32
    PAIR = 2
    HALVES = H // 2
    UNITS = PAIR * HALVES
    ROUNDS = B // PAIR
    FAR, TAKEN = -2e38, -3e38
    with ExitStack() as ctx:
        qp = core.sb(ctx, "x1_qp", [P, CC, H, TOK])
        with ExitStack() as c2:
            wq = core.sb(c2, "x1_wq", [P, KC, H * DH])
            wkt = core.sb(c2, "x1_wkt", [P, CD])
            qt = core.sb(c2, "x1_qt", [P, TOK])
            ps = core.pb(c2, "x1_ps", [P, 8, 512])
            w_in, q_ready, qt_ready, qp_ready, qp_used = core.sems(c2, "x1", "w_in q_ready qt_ready qp_ready qp_used")
            with nc.Block() as block:
                @block.sync
                def _(sp):
                    sp.dma_start(wq[:, :, :], w["L1_xattn_Wq"].rearrange("(c p) n -> p c n", p=P)).then_inc(w_in, 16)
                    sp.dma_start(wkt[:, :], w["L1_xattn_WkT"]).then_inc(w_in, 16)

                @block.tensor
                def _(pe):
                    pe.wait_ge(w_in, 32)
                    for c in range(KC):
                        last = nc.tensor.matmul(ps[:, 0, :], wq[:, c, :], xt[:, c, :], start=(c == 0), stop=(c == KC - 1))
                    last.then_inc(q_ready, 1)
                    pe.wait_ge(qt_ready, 1)
                    for n in range(H * CC):
                        h, c = n // CC, n % CC
                        if n >= 4:
                            pe.wait_ge(qp_used, n - 3)
                        nc.tensor.matmul(ps[:, 4 + n % 4, :], wkt[h * DH:(h + 1) * DH, c * P:(c + 1) * P],
                                         qt[h * DH:(h + 1) * DH, :], start=True, stop=True).then_inc(qp_ready, 1)

                @block.scalar
                def _(act):
                    act.wait_ge(q_ready, 1)
                    nc.scalar.mul(qt[:, :], ps[:, 0, :], DH ** -0.5).then_inc(qt_ready, 1)
                    for n in range(H * CC):
                        act.wait_ge(qp_ready, n + 1)
                        nc.scalar.copy(qp[:, n % CC, n // CC, :], ps[:, 4 + n % 4, :]).then_inc(qp_used, 1)

        cx = core.sb(ctx, "x1_cx", [P, PAIR, KT, CD])
        cxt = core.sb(ctx, "x1_cxt", [P, PAIR, CC, CTX])
        mask8 = core.sb(ctx, "x1_mask8", [P, CTX], U8)
        mask = core.sb(ctx, "x1_mask", [P, CTX])
        qs = core.sb(ctx, "x1_qs", [P, 2, CC, P])
        sc = core.sb(ctx, "x1_sc", [P, 2, CTX])
        left = core.sb(ctx, "x1_left", [P, 2, CTX])
        best = core.sb(ctx, "x1_best", [P, 2, TOP])
        best_p = core.sb(ctx, "x1_best_p", [P, 2, TOP])
        red = core.sb(ctx, "x1_red", [P, 2, 3])
        two = core.sb(ctx, "x1_two", [P, S])
        mean = core.sb(ctx, "x1_mean", [P, 2, S])
        at = core.sb(ctx, "x1_at", [P, KT, S])
        s_ps = core.pb(ctx, "x1_s_ps", [P, 4 * 512])
        a_ps = core.pb(ctx, "x1_a_ps", [P, 2 * 512])
        c_ps = core.pb(ctx, "x1_c_ps", [P, 512])
        cx_in0, cx_in1, cxt_in0, cxt_in1, m_in, two_in, mask_ready, qs_ready, s_ready, sc_copied, sc_ready, steps, \
            chosen, inv_ready, small_ready, e_ready, p_ready, mean_ready, a_ready, at_ready, c_ready, ct_ready = core.sems(
                ctx, "x1", "cx_in0 cx_in1 cxt_in0 cxt_in1 m_in two_in mask_ready qs_ready s_ready sc_copied sc_ready steps "
                "chosen inv_ready small_ready e_ready p_ready mean_ready a_ready at_ready c_ready ct_ready")
        cx_in, cxt_in = (cx_in0, cx_in1), (cxt_in0, cxt_in1)
        PICKS = TOP // 8
        with nc.Block() as block:
            @block.sync
            def _(sp):
                sp.dma_start(two[:, :], w["two_eyes"]).then_inc(two_in, 16)

                def load(b, j, i):
                    if i is not None or j:
                        sp.wait_ge(mask_ready, i * PAIR + (PAIR + j) if i is not None else j)
                    sp.dma_start(mask8[:, :], w["mask_ctx"][bass.ds(b, 1), :].broadcast_to([P, CTX])).then_inc(m_in, 16)
                    if i is not None:
                        sp.wait_ge(s_ready, i * UNITS + HALVES * (j + 1) + PRIMED)
                    sp.dma_start(cxt[:, j, :, :],
                                 w["ctxT"][bass.ds(b, 1), :, :].rearrange("b (c p) n -> p (b c) n", p=P)).then_inc(cxt_in[j], 16)
                    if i is not None:
                        sp.wait_ge(c_ready, i * PAIR + j + 1 + PRIMED)
                    sp.dma_start(cx[:, j, 0:KT - 1, :],
                                 w["ctx"][bass.ds(b, 1), 0:(KT - 1) * P, :].rearrange("b (t p) n -> p (b t) n", p=P)
                                 ).then_inc(cx_in[j], 16)
                    sp.dma_start(cx[0:LAST, j, KT - 1, :],
                                 w["ctx"][bass.ds(b, 1), (KT - 1) * P:CTX, :].rearrange("b p n -> (b p) n")
                                 ).then_inc(cx_in[j], 16)

                for j in range(PAIR):
                    load(j, j, None)
                with sp.Fori(0, ROUNDS - 1) as i:
                    for j in range(PAIR):
                        load((i + 1) * PAIR + j, j, i)

            @block.tensor
            def _(pe):
                core.prime(pe, s_ready, c_ready)
                with pe.Fori(0, ROUNDS) as i:
                    def scores(u):
                        j = u // HALVES
                        pe.wait_ge(qs_ready, i * UNITS + u + 1)
                        if u % HALVES == 0:
                            pe.wait_ge(cxt_in[j], i * 16 + 16)
                        pe.wait_ge(sc_copied, i * UNITS + u + PRIMED)
                        for n in range(4):
                            a, b = 512 * n, min(512 * n + 512, CTX)
                            for c in range(CC):
                                last = nc.tensor.matmul(s_ps[:, a:b], qs[:, u % 2, c, :], cxt[:, j, c, a:b],
                                                        start=(c == 0), stop=(c == CC - 1))
                        last.then_inc(s_ready, 1)

                    def mean_attention(j):
                        pe.wait_ge(p_ready, i * UNITS + HALVES * (j + 1))
                        pe.wait_ge(mean_ready, i * UNITS + HALVES * (j + 1))
                        pe.wait_ge(at_ready, (i * PAIR + j) * 3 + PRIMED)
                        for t in range(KT):
                            rows = P if t < KT - 1 else LAST
                            for r in range(HALVES):
                                last = nc.tensor.matmul(a_ps[0:rows, t * S:(t + 1) * S], sc[:, r, t * P:t * P + rows], mean[:, r, :],
                                                        start=(r == 0), stop=(r == HALVES - 1))
                        last.then_inc(a_ready, 1)

                    def weigh(j):
                        pe.wait_ge(at_ready, (i * PAIR + j + 1) * 3 + PRIMED)
                        pe.wait_ge(cx_in[j], i * 32 + 32)
                        pe.wait_ge(ct_ready, i * PAIR + j + PRIMED)
                        for c in range(CC):
                            for t in range(KT):
                                rows = P if t < KT - 1 else LAST
                                last = nc.tensor.matmul(c_ps[:, c * S:(c + 1) * S], cx[0:rows, j, t, c * P:(c + 1) * P], at[0:rows, t, :],
                                                        start=(t == 0), stop=(t == KT - 1))
                        last.then_inc(c_ready, 1)

                    scores(0)
                    for j in range(PAIR):
                        scores(2 * j + 1)
                        if j + 1 < PAIR:
                            scores(2 * j + 2)
                        mean_attention(j)
                        weigh(j)

            @block.scalar
            def _(act):
                core.prime(act, sc_copied, at_ready, ct_ready, e_ready)
                with act.Fori(0, ROUNDS) as i:
                    def spread_mask(j):
                        act.wait_ge(m_in, (i * PAIR + j) * 16 + 16)
                        act.wait_ge(sc_ready, i * UNITS + j * HALVES + PRIMED)
                        nc.scalar.activation(mask[:, :], mask8[:, :], ACT.Copy, bias=NEG, scale=-NEG).then_inc(mask_ready, 1)

                    def copy_scores(u):
                        act.wait_ge(s_ready, i * UNITS + u + 1 + PRIMED)
                        if u >= 2:
                            act.wait_ge(a_ready, i * PAIR + u // 2)
                        nc.scalar.copy(sc[:, u % 2, :], s_ps[:, 0:CTX]).then_inc(sc_copied, 1)

                    def exponent(u):
                        k = u % 2
                        act.wait_ge(chosen, i * UNITS + u + 1)
                        nc.scalar.activation(best_p[:, k, :], best[:, k, :], ACT.Exp, bias=red[:, k, 0:1],
                                             accum_out=red[:, k, 1:2]).then_inc(small_ready, 1)
                        nc.scalar.activation(sc[:, k, :], sc[:, k, :], ACT.Exp, bias=red[:, k, 0:1]).then_inc(e_ready, 1)

                    def copy_out(j):
                        for lo, hi, rows in ((0, 8, P), (8, KT - 1, P), (KT - 1, KT, LAST)):
                            act.wait_ge(a_ready, i * PAIR + j + 1)
                            act.wait_ge(c_ready, i * PAIR + j + PRIMED)
                            nc.scalar.copy(at[0:rows, lo:hi, :], a_ps[0:rows, lo * S:hi * S].rearrange("p (t n) -> p t n", n=S)).then_inc(at_ready, 1)
                        act.wait_ge(c_ready, i * PAIR + j + 1 + PRIMED)
                        nc.scalar.copy(ct[:, :, bass.ds((i * PAIR + j) * S, S)],
                                       c_ps[:, 0:CC * S].rearrange("p (c n) -> p c n", n=S)).then_inc(ct_ready, 1)

                    spread_mask(0)
                    copy_scores(0)
                    copy_scores(1)
                    exponent(0)
                    exponent(1)
                    copy_out(0)
                    spread_mask(1)
                    copy_scores(2)
                    copy_scores(3)
                    exponent(2)
                    exponent(3)
                    copy_out(1)

            @block.gpsimd
            def _(pool):
                core.prime(pool, sc_ready)
                with pool.Fori(0, ROUNDS) as i:
                    for u in range(UNITS):
                        j, r = u // HALVES, u % HALVES
                        if u >= 2:
                            pool.wait_ge(s_ready, i * UNITS + u - 1 + PRIMED)
                        else:
                            pool.wait_ge(s_ready, i * UNITS + PRIMED)
                        nc.gpsimd.tensor_copy(qs[:, u % 2, :, :].rearrange("p c (h s) -> p c h s", h=2),
                                              qp[:, :, 2 * r:2 * r + 2, bass.ds((i * PAIR + j) * S, S)]).then_inc(qs_ready, 1)
                        if r == 0:
                            pool.wait_ge(mask_ready, i * PAIR + j + 1)
                        pool.wait_ge(sc_copied, i * UNITS + u + 1 + PRIMED)
                        nc.gpsimd.tensor_tensor(sc[:, u % 2, :], sc[:, u % 2, :], mask[:, :], ALU.add).then_inc(sc_ready, 1)

            @block.vector
            def _(dve):
                V = nc.vector
                dve.wait_ge(two_in, 16)
                with dve.Fori(0, ROUNDS) as i:
                    for u in range(UNITS):
                        k = u % 2
                        done = [0]

                        def step(instruction):
                            done[0] += 1
                            instruction.then_inc(steps, 1)
                            dve.wait_ge(steps, done[0])

                        dve.wait_ge(sc_ready, i * UNITS + u + 1 + PRIMED)
                        dve.wait_ge(e_ready, i * UNITS + max(u - 1, 0) + PRIMED)
                        step(V.memset(red[:, k, 2:3], 0.0))
                        for n in range(PICKS):
                            source = sc if n == 0 else left
                            step(V.max(best[:, k, 8 * n:8 * n + 8], source[:, k, :]))
                            step(V.match_replace(left[:, k, :], best[:, k, 8 * n:8 * n + 8], source[:, k, :], TAKEN))
                        dve.sem_clear(steps)
                        V.tensor_scalar(red[:, k, 0:1], best[:, k, 0:1], -1.0, None, ALU.mult).then_inc(chosen, 1)
                        dve.wait_ge(small_ready, i * UNITS + u + 1)
                        V.reciprocal(red[:, k, 2:3], red[:, k, 1:2]).then_inc(inv_ready, 1)
                        if u >= 2:
                            dve.wait_ge(a_ready, i * PAIR + u // 2)
                        dve.wait_ge(inv_ready, i * UNITS + u + 1)
                        V.tensor_scalar(mean[:, k, :], two[:, :], red[:, k, 2:3], 1.0 / H, ALU.mult, ALU.mult).then_inc(mean_ready, 1)
                        dve.wait_ge(e_ready, i * UNITS + u + 1 + PRIMED)
                        V.scalar_tensor_tensor(sc[:, k, :], left[:, k, :], FAR, sc[:, k, :], ALU.is_le, ALU.mult).then_inc(p_ready, 1)


def mixing(core, x, xn, xt, ct, spec_k, ident, w):
    nc = core.nc
    FC = 2048 // P
    with ExitStack() as ctx:
        y = core.sb(ctx, "mx_y", [P, TT, D])
        film = core.sb(ctx, "mx_film", [P, TT, 2 * D])
        with ExitStack() as c2:
            wv = core.sb(c2, "mx_wv", [P, CC, D])
            wf = core.sb(c2, "mx_wf", [P, 2, KC, 2 * D])
            bf = core.sb(c2, "mx_bf", [P, 2, 2 * D])
            tm8 = core.sb(c2, "mx_tm8", [P, TOK], U8)
            tm = core.sb(c2, "mx_tm", [P, TOK])
            c_t = core.sb(c2, "mx_c_t", [P, KC, TOK])
            film_in = core.sb(c2, "mx_film_in", [P, TT, 2 * D])
            mg = core.sb(c2, "mx_mg", [P, 1])
            rows = core.sb(c2, "mx_rows", [P, 3, D])
            dft = core.sb(c2, "mx_dft", [P, 2, FREQ])
            inverse = core.sb(c2, "mx_inverse", [P, S])
            xs = core.sb(c2, "mx_xs", [P, TT, D])
            films = (film_in, film)
            with ExitStack() as c3:
                ps = core.pb(c3, "mx_ps", [P, 8, 512])
                c_in, f_in, tm_ready, v_ready, ct_ready, f_ready, f_used, g_steps = core.sems(
                    c3, "mx", "c_in f_in tm_ready v_ready ct_ready f_ready f_used g_steps")
                with nc.Block() as block:
                    @block.sync
                    def _(sp):
                        sp.dma_start(wv[:, :, :], w["L1_xattn_Wv"].rearrange("(c p) n -> p c n", p=P)).then_inc(c_in, 16)
                        sp.dma_start(tm8[:, :], w["mask_x"].broadcast_to([P, TOK])).then_inc(c_in, 16)
                        for a, k in enumerate(("in", "out")):
                            sp.dma_start(wf[:, a, :, :], w[f"L1_xattn_W_film_{k}"].rearrange("(c p) n -> p c n", p=P)).then_inc(f_in, 16)
                            sp.dma_start(bf[:, a, :], bcast(w[f"L1_xattn_b_film_{k}"])).then_inc(f_in, 16)
                        sp.dma_start(mg[:, :], w["L1_xattn_mod_gate"].broadcast_to([P, 1])).then_inc(f_in, 16)
                        for n, k in enumerate(("g_norm_in", "b_norm_in", "D_skip")):
                            sp.dma_start(rows[:, n, :], bcast(w[f"L1_xattn_{k}"])).then_inc(f_in, 16)
                        for half in range(2):
                            sp.dma_start(dft[half * S:(half + 1) * S, :, :], w["dft_x"].rearrange("a l f -> l a f")).then_inc(f_in, 16)
                        sp.dma_start(inverse[:, :], w["dft_inverse"]).then_inc(f_in, 16)
                        sp.wait_ge(f_in, 11 * 16)

                    @block.tensor
                    def _(pe):
                        pe.wait_ge(c_in, 32)
                        for m in range(KC):
                            for c in range(CC):
                                last = nc.tensor.matmul(ps[:, m, :], wv[:, c, m * P:(m + 1) * P], ct[:, c, :],
                                                        start=(c == 0), stop=(c == CC - 1))
                            last.then_inc(v_ready, 1)
                        pe.wait_ge(ct_ready, KC)
                        pe.wait_ge(f_in, 11 * 16)
                        for n in range(4 * TT):
                            t, a, half = n // 4, n // 2 % 2, n % 2
                            if n >= 4:
                                pe.wait_ge(f_used, n - 3)
                            for c in range(KC):
                                last = nc.tensor.matmul(ps[:, 4 + n % 4, :], c_t[:, c, t * P:(t + 1) * P],
                                                        wf[:, a, c, half * D:(half + 1) * D], start=(c == 0), stop=(c == KC - 1))
                            last.then_inc(f_ready, 1)

                    @block.gpsimd
                    def _(pool):
                        pool.wait_ge(c_in, 32)
                        nc.gpsimd.tensor_copy(tm[:, :], tm8[:, :]).then_inc(tm_ready, 1)

                    @block.vector
                    def _(dve):
                        V = nc.vector
                        dve.wait_ge(tm_ready, 1)
                        for m in range(KC):
                            dve.wait_ge(v_ready, m + 1)
                            V.tensor_tensor(c_t[:, m, :], ps[:, m, :], tm[:, :], ALU.mult).then_inc(ct_ready, 1)
                        dve.wait_ge(f_in, 11 * 16)
                        for n in range(4 * TT):
                            t, a, half = n // 4, n // 2 % 2, n % 2
                            dve.wait_ge(f_ready, n + 1)
                            V.tensor_tensor(films[a][:, t, half * D:(half + 1) * D], ps[:, 4 + n % 4, :],
                                            bf[:, a, half * D:(half + 1) * D], ALU.add).then_inc(f_used, 1)
                        dve.wait_ge(f_used, 4 * TT)
                        for a in range(2):
                            V.tensor_scalar(films[a][:, :, 0:D], films[a][:, :, 0:D], mg[:, 0:1], 1.0, ALU.mult, ALU.add)
                            V.tensor_scalar(films[a][:, :, D:2 * D], films[a][:, :, D:2 * D], mg[:, 0:1], None, ALU.mult)

            norm_stage(core, "n4", xn, xs, None, ident, gamma=rows[:, 0, :], beta=rows[:, 1, :])
            with ExitStack() as c3:
                spec = core.sb(c3, "mx_spec", [P, 2, 2, D])
                skip = core.sb(c3, "mx_skip", [P, TT, D])
                ps = core.pb(c3, "mx_ps2", [P, 8, 512])
                xs_ready, sp_ready, spec_ready, y_ready, skip_ready, s_first, s_last = core.sems(
                    c3, "mx", "xs_ready sp_ready spec_ready y_ready skip_ready s_first s_last")
                with nc.Block() as block:
                    @block.tensor
                    def _(pe):
                        def forward(b):
                            lo, t, k = (b % 2) * S, b // 2, b % 2
                            pe.wait_ge(xs_ready, t + 1)
                            if b >= 2:
                                pe.wait_ge(spec_ready, 2 * (b - 1))
                            for a in range(2):
                                last = nc.tensor.matmul(ps[:, 2 * k + a, :], dft[lo:lo + S, a, :], xs[lo:lo + S, t, :],
                                                        start=True, stop=True)
                            last.then_inc(sp_ready, 1)

                        forward(0)
                        for b in range(B):
                            lo, t, k = (b % 2) * S, b // 2, b % 2
                            if b + 1 < B:
                                forward(b + 1)
                            pe.wait_ge(spec_ready, 2 * (b + 1))
                            for a in range(2):
                                last = nc.tensor.matmul(ps[lo:lo + S, 4 + t, :], inverse[:, :], spec[:, k, a, :],
                                                        start=(a == 0), stop=(a == 1))
                            last.then_inc(y_ready, 1)

                    @block.gpsimd
                    def _(pool):
                        for t in range(TT):
                            pool.wait_ge(xs_ready, t + 1)
                            nc.gpsimd.tensor_tensor(skip[:, t, :], xs[:, t, :], rows[:, 2, :], ALU.mult).then_inc(skip_ready, 1)

                    @block.vector
                    def _(dve):
                        V = nc.vector
                        for t in range(TT):
                            V.tensor_tensor(xs[:, t, :], xs[:, t, :], film_in[:, t, 0:D], ALU.mult).then_inc(s_first, 1)
                        for t in range(TT):
                            dve.wait_ge(s_first, t + 1)
                            V.tensor_tensor(xs[:, t, :], xs[:, t, :], film_in[:, t, D:2 * D], ALU.add).then_inc(xs_ready, 1)
                        for b in range(B):
                            k = b % 2
                            dve.wait_ge(sp_ready, b + 1)
                            if b >= 2:
                                dve.wait_ge(y_ready, b - 1)
                            for a in range(2):
                                V.tensor_tensor(spec[:, k, a, :], ps[:, 2 * k + a, :], spec_k[:, a, :], ALU.mult).then_inc(spec_ready, 1)
                        dve.wait_ge(skip_ready, TT)
                        for t in range(TT):
                            dve.wait_ge(y_ready, 2 * t + 2)
                            V.tensor_tensor(y[:, t, :], ps[:, 4 + t, :], skip[:, t, :], ALU.add).then_inc(s_last, 1)
                        for n, (other, op) in enumerate(((film[:, :, 0:D], ALU.mult), (film[:, :, D:2 * D], ALU.add), (xn[:, :, :], ALU.add))):
                            for t in range(TT):
                                dve.wait_ge(s_last, n * TT + t + 1)
                                V.tensor_tensor(y[:, t, :], y[:, t, :], other[:, t, :], op).then_inc(s_last, 1)

        with ExitStack() as c2:
            rows = core.sb(c2, "ff_rows", [P, 5, D])
            w1 = core.sb(c2, "ff_w1", [P, KC, 2048])
            w2 = core.sb(c2, "ff_w2", [P, FC, D])
            b1 = core.sb(c2, "ff_b1", [P, FC])
            h = core.sb(c2, "ff_h", [P, 2, TOK])
            r_in, w1_in, w2_in, up_ready, h_ready, down_ready, b_ready = core.sems(
                c2, "ff", "r_in w1_in w2_in up_ready h_ready down_ready b_ready")
            with nc.Block() as block:
                @block.sync
                def _(sp):
                    for n, k in enumerate(("g_ffn", "b_ffn", "g_norm_out", "b_norm_out", "b2")):
                        sp.dma_start(rows[:, n, :], bcast(w[f"L1_xattn_{k}"])).then_inc(r_in, 16)
                    sp.dma_start(w1[:, :, :], w["L1_xattn_W1"].rearrange("(c p) n -> p c n", p=P)).then_inc(w1_in, 16)
                    sp.dma_start(b1[:, :], w["L1_xattn_b1"]).then_inc(w1_in, 16)
                    sp.dma_start(w2[:, :, :], w["L1_xattn_W2"].rearrange("(c p) n -> p c n", p=P)).then_inc(w2_in, 16)
                    sp.wait_ge(r_in, 80)

            norm_stage(core, "n5", y, xn, xt, ident, gamma=rows[:, 0, :], beta=rows[:, 1, :])
            with ExitStack() as c3:
                u_ps = core.pb(c3, "ff_u_ps", [P, 2, 512])
                a_ps = core.pb(c3, "ff_a_ps", [P, TT, 512])
                with nc.Block() as block:
                    @block.tensor
                    def _(pe):
                        def up(n):
                            if n >= 2:
                                pe.wait_ge(h_ready, n - 1)
                            for c in range(KC):
                                last = nc.tensor.matmul(u_ps[:, n % 2, :], w1[:, c, n * P:(n + 1) * P], xt[:, c, :],
                                                        start=(c == 0), stop=(c == KC - 1))
                            last.then_inc(up_ready, 1)

                        pe.wait_ge(w1_in, 32)
                        pe.wait_ge(w2_in, 16)
                        up(0)
                        for n in range(FC):
                            if n + 1 < FC:
                                up(n + 1)
                            pe.wait_ge(h_ready, n + 1)
                            for t in range(TT):
                                last = nc.tensor.matmul(a_ps[:, t, :], h[:, n % 2, t * P:(t + 1) * P], w2[:, n, :],
                                                        start=(n == 0), stop=(n == FC - 1))
                            last.then_inc(down_ready, 1)

                    @block.scalar
                    def _(act):
                        act.wait_ge(w1_in, 32)
                        for n in range(FC):
                            act.wait_ge(up_ready, n + 1)
                            if n >= 2:
                                act.wait_ge(down_ready, n - 1)
                            nc.scalar.activation(h[:, n % 2, :], u_ps[:, n % 2, :], ACT.Gelu, bias=b1[:, n:n + 1]).then_inc(h_ready, 1)

                    @block.vector
                    def _(dve):
                        for t in range(TT):
                            nc.vector.tensor_tensor(y[:, t, :], y[:, t, :], rows[:, 4, :], ALU.add).then_inc(b_ready, 1)
                        dve.wait_ge(down_ready, FC)
                        for t in range(TT):
                            dve.wait_ge(b_ready, t + 1)
                            nc.vector.tensor_tensor(y[:, t, :], y[:, t, :], a_ps[:, t, :], ALU.add)
            norm_stage(core, "n7", y, xn, None, ident, gamma=rows[:, 2, :], beta=rows[:, 3, :], out=x)


def build_program(nc, w, out, start=0, upto=99):
    with ExitStack() as ctx:
        core = Core(nc, ctx)
        x = core.sb(ctx, "x", [P, TT, D])
        xn = core.sb(ctx, "xn", [P, TT, D])
        xt = core.sb(ctx, "xt", [P, KC, TOK])
        ident = core.sb(ctx, "ident", [P, P])
        x_in, x_out = core.sems(ctx, "io", "x_in x_out")
        with nc.Block() as block:
            @block.sync
            def _(sp):
                sp.dma_start(x[:, :, :], w["x"].rearrange("(t p) n -> p t n", p=P)).then_inc(x_in, 16)
                sp.dma_start(ident[:, :], w["ident"]).then_inc(x_in, 16)
                sp.wait_ge(x_in, 32)
        stages = [
            ("n0", lambda: cross_attention_L0(core, x, xt, ident, w)),
            ("n1", lambda: self_attention_L0(core, x, xt, ident, w)),
            ("n2", lambda: moe_L0(core, x, xt, ident, w)),
            ("n3", lambda: cross_attention_L1(core, x, xn, xt, ident, w)),
            ("n8", lambda: self_attention_L1(core, x, xt, ident, w)),
            ("n9", lambda: moe_L1(core, x, xt, ident, w)),
        ]
        for name, stage in stages[start:upto]:
            norm_stage(core, name, x, xn, xt, ident)
            stage()
        with nc.Block() as block:
            @block.sync
            def _(sp):
                sp.dma_start(out.rearrange("(t p) n -> p t n", p=P), x[:, :, :]).then_inc(x_out, 16)
                sp.wait_ge(x_out, 16)


def laid_out(inputs):
    a = {k: np.asarray(v) for k, v in inputs.items()}
    evens_first = np.concatenate([np.arange(0, D, 2), np.arange(1, D, 2)])
    token = np.arange(P)
    same = token[:, None] // S == token[None, :] // S
    ahead = token[None, :] - token[:, None]
    theta = (np.float32(10000.0) ** (np.float32(-2.0) * np.arange(D // 2, dtype=np.float32) / np.float32(D))).astype(np.float32)
    angle = theta[:, None] * (np.arange(TOK) % S).astype(np.float32)[None, :]
    per_head = lambda m: m.transpose(1, 2, 0).reshape(D, -1)
    w = {
        "x": a["x"].reshape(TOK, D),
        "ctx": a["ctx_768"],
        "ctxT": np.ascontiguousarray(a["ctx_768"].transpose(0, 2, 1)),
        "ident": np.eye(P, dtype=np.float32),
        "L0_xattn_Wq": a["L0_xattn_Wq"],
        "L0_xattn_WkT": np.ascontiguousarray(a["L0_xattn_Wk"].T),
        "L0_xattn_Wv": a["L0_xattn_Wv"],
        "L0_xattn_Wout": a["L0_xattn_Wout"],
        "L0_xattn_bout": a["L0_xattn_bout"],
        "L0_attn_Wq": a["L0_attn_Wq"][evens_first].T,
        "L0_attn_Wk": a["L0_attn_Wk"][evens_first].T,
        "L0_attn_Wv": a["L0_attn_Wv"].T,
        "rope_cos": np.cos(angle),
        "rope_sin": np.sin(angle),
        "mask_L0": np.where(same & (ahead <= 1), 0.0, NEG).astype(np.float32),
        "mask_L1": np.where(same & (ahead <= 0), 0.0, NEG).astype(np.float32),
        "L0_ffn_router_weight": a["L0_ffn_router_weight"].T,
        "L0_ffn_router_bias": a["L0_ffn_router_bias"],
        "L0_ffn_gate_up_proj": a["L0_ffn_gate_up_proj"],
        "L0_ffn_gate_up_bias": a["L0_ffn_gate_up_bias"].reshape(EXPERTS, -1, P).transpose(0, 2, 1),
        "L0_ffn_down_proj": a["L0_ffn_down_proj"],
        "L0_ffn_down_bias": a["L0_ffn_down_bias"],
        "L1_attn_Q": per_head(a["L1_attn_Q"]),
        "L1_attn_K": per_head(a["L1_attn_K"]),
        "L1_attn_V": per_head(a["L1_attn_V"]),
        "L1_attn_W": a["L1_attn_W"].transpose(2, 1, 0).reshape(-1, D),
        "L1_ffn_b1": a["L1_ffn_b1"].reshape(EXPERTS, -1, P).transpose(0, 2, 1),
        "mask_x": a["mask_BxS_bf1"].reshape(1, TOK).view(np.uint8),
        "mask_ctx": a["mask_BxS2_bf1"].view(np.uint8),
        "two_eyes": np.tile(np.eye(S, dtype=np.float32), (2, 1)),
        "L1_xattn_WkT": a["L1_xattn_Wk"].T,
        "L1_xattn_mod_gate": a["L1_xattn_mod_gate"].reshape(1, 1),
        **{k: a[k] for k in ("L1_ffn_W1", "L1_ffn_W2", "L1_ffn_b2", "L1_ffn_gate_W", "L1_ffn_shared_W", "L1_ffn_shared_b",
                             "L1_ffn_gamma", "L1_ffn_beta")},
        **{f"L1_xattn_{k}": a[f"L1_xattn_{k}"] for k in (
            "Wq", "Wv", "W_film_in", "b_film_in", "W_film_out", "b_film_out", "g_norm_in", "b_norm_in", "g_norm_out",
            "b_norm_out", "g_ffn", "b_ffn", "W1", "W2", "b2", "A_re", "A_im", "C_re", "C_im", "D_skip")},
        "L1_xattn_b1": a["L1_xattn_b1"].reshape(-1, P).T,
        "L1_xattn_log_dt": a["L1_xattn_log_dt"].reshape(-1, P).T,
        **transforms(),
    }
    return {k: np.ascontiguousarray(v) for k, v in w.items()}


def kernel(**inputs):
    import concourse.bacc as bacc
    from concourse.bass_utils import run_bass_kernel_spmd

    nc = bacc.Bacc("TRN2", target_bir_lowering=False, num_devices=1)
    w = laid_out(inputs)
    aps = {k: nc.dram_tensor(f"in_{k}", v.shape, mybir.dt.from_np(v.dtype), kind="ExternalInput").ap() for k, v in w.items()}
    out = nc.dram_tensor("out_x", (TOK, D), F32, kind="ExternalOutput").ap()
    build_program(nc, aps, out)
    r = run_bass_kernel_spmd(nc, [{f"in_{k}": v for k, v in w.items()}], core_ids=[0])
    return r.results[0]["out_x"].reshape(B, S, D)
```

```python
import math
from contextlib import ExitStack

import numpy as np
import concourse.bass as bass
from concourse import mybir

F32 = mybir.dt.float32
U8 = mybir.dt.uint8
ALU = mybir.AluOpType
ACT = mybir.ActivationFunctionType
AXIS = mybir.AxisListType

P = 128
B, S, D = 8, 64, 512
TOK = B * S
TT = TOK // P
KC = D // P
CTX, CD = 1601, 384
CC = CD // P
KT = -(-CTX // P)
LAST = CTX - (KT - 1) * P
EPS = 1e-5
PRIMED = 1
PAIR = 2
NEG = -1e30
EXPERTS = 8
PI = math.pi


class Core:

    def __init__(self, nc, ctx):
        self.nc, self.ctx = nc, ctx

    def sb(self, ctx, name, shape, dt=F32):
        return ctx.enter_context(self.nc.sbuf_tensor(name, list(shape), dt))

    def pb(self, ctx, name, shape, dt=F32):
        return ctx.enter_context(self.nc.psum_tensor(name, list(shape), dt))

    def sems(self, ctx, stage, names):
        made = [self.nc.alloc_semaphore(name=f"{stage}_{n}") for n in names.split()]

        def release():
            self.nc.clear_and_free_semaphores(made)
            self.nc.all_engine_barrier()

        ctx.callback(release)
        return made

    @staticmethod
    def prime(engine, *semaphores):
        for semaphore in semaphores:
            engine.sem_inc(semaphore, PRIMED)


def bcast(v, parts=P):
    return v.partition_broadcast(parts)


def norm_stage(core, name, src, normed, normed_t, ident, gamma=None, beta=None, out=None):
    nc = core.nc
    with ExitStack() as ctx:
        stats = core.sb(ctx, f"{name}_stats", [P, TT, 6])
        mv = core.sb(ctx, f"{name}_mv", [P, TT, 2])
        var = core.sb(ctx, f"{name}_var", [P, TT])
        half = core.sb(ctx, f"{name}_half", [P, TT])
        rstd = core.sb(ctx, f"{name}_rstd", [P, TT])
        tps = core.pb(ctx, f"{name}_tps", [P, TT, KC, P]) if normed_t is not None else None
        stats_ready, mv_ready, rstd_ready, normed_ready, t_ready, t_used = core.sems(
            ctx, name, "stats_ready mv_ready rstd_ready normed_ready t_ready t_used")
        steps = 1 + (gamma is not None) + (beta is not None)
        with nc.Block() as block:
            @block.vector
            def _(dve):
                for t in range(TT):
                    nc.vector.bn_stats(stats[:, t, :], src[:, t, :]).then_inc(stats_ready, 1)
                for t in range(TT):
                    dve.wait_ge(stats_ready, t + 1)
                    nc.vector.bn_aggr(mv[:, t, :], stats[:, t, :]).then_inc(mv_ready, 1)
                dve.wait_ge(rstd_ready, 3)
                for t in range(TT):
                    nc.vector.tensor_scalar(normed[:, t, :], src[:, t, :], mv[:, t, 0:1], rstd[:, t:t + 1],
                                            ALU.subtract, ALU.mult).then_inc(normed_ready, 1)
                if gamma is not None:
                    for t in range(TT):
                        dve.wait_ge(normed_ready, t + 1)
                        nc.vector.tensor_tensor(normed[:, t, :], normed[:, t, :], gamma[:, :], ALU.mult).then_inc(normed_ready, 1)
                if beta is not None:
                    for t in range(TT):
                        dve.wait_ge(normed_ready, TT + t + 1)
                        nc.vector.tensor_tensor(normed[:, t, :], normed[:, t, :], beta[:, :], ALU.add).then_inc(normed_ready, 1)
                if out is not None:
                    for t in range(TT):
                        dve.wait_ge(normed_ready, (steps - 1) * TT + t + 1)
                        nc.vector.tensor_tensor(out[:, t, :], out[:, t, :], normed[:, t, :], ALU.add)

            @block.gpsimd
            def _(pool):
                nc.gpsimd.memset(half[:, :], -0.5).then_inc(rstd_ready, 1)
                pool.wait_ge(mv_ready, TT)
                nc.gpsimd.tensor_scalar_add(var[:, :], mv[:, :, 1], EPS).then_inc(rstd_ready, 1)
                pool.wait_ge(rstd_ready, 2)
                nc.gpsimd.tensor_tensor(rstd[:, :], var[:, :], half[:, :], ALU.pow).then_inc(rstd_ready, 1)

            if normed_t is not None:
                @block.tensor
                def _(pe):
                    for t in range(TT):
                        pe.wait_ge(normed_ready, (steps - 1) * TT + t + 1)
                        for c in range(KC):
                            last = nc.tensor.transpose(tps[:, t, c, :], normed[:, t, c * P:(c + 1) * P], ident[:, :])
                        last.then_inc(t_ready, 1)

                @block.scalar
                def _(act):
                    for t in range(TT):
                        act.wait_ge(t_ready, t + 1)
                        nc.scalar.copy(normed_t[:, :, t * P:(t + 1) * P], tps[:, t, :, :])


def cross_attention_L0(core, x, xt, ident, w):
    nc = core.nc
    H, DH = 8, 64
    PAIR = 2
    UNITS = PAIR * H // 2
    with ExitStack() as ctx:
        qp = core.sb(ctx, "x0_qp", [P, CC, H, TOK])
        wv = core.sb(ctx, "x0_wv", [P, CC, D])
        wout = core.sb(ctx, "x0_wout", [P, KC, D])
        bout = core.sb(ctx, "x0_bout", [P, D])
        (w_in,) = core.sems(ctx, "x0", "w_in")
        with ExitStack() as c2:
            wq = core.sb(c2, "x0_wq", [P, KC, D])
            wkt = core.sb(c2, "x0_wkt", [P, KC, CD])
            qt = core.sb(c2, "x0_qt", [P, KC, TOK])
            ps = core.pb(c2, "x0_ps", [P, 8, 512])
            wq_in, q_ready, qt_ready, qp_ready, qp_used = core.sems(c2, "x0", "wq_in q_ready qt_ready qp_ready qp_used")
            with nc.Block() as block:
                @block.sync
                def _(sp):
                    sp.dma_start(wq[:, :, :], w["L0_xattn_Wq"].rearrange("(c p) n -> p c n", p=P)).then_inc(wq_in, 16)
                    sp.dma_start(wkt[:, :, :], w["L0_xattn_WkT"].rearrange("(c p) n -> p c n", p=P)).then_inc(wq_in, 16)
                    sp.dma_start(wv[:, :, :], w["L0_xattn_Wv"].rearrange("(c p) n -> p c n", p=P)).then_inc(w_in, 16)
                    sp.dma_start(wout[:, :, :], w["L0_xattn_Wout"].rearrange("(c p) n -> p c n", p=P)).then_inc(w_in, 16)
                    sp.dma_start(bout[:, :], bcast(w["L0_xattn_bout"])).then_inc(w_in, 16)

                @block.tensor
                def _(pe):
                    pe.wait_ge(wq_in, 32)
                    for m in range(KC):
                        for c in range(KC):
                            last = nc.tensor.matmul(ps[:, m, :], wq[:, c, m * P:(m + 1) * P], xt[:, c, :],
                                                    start=(c == 0), stop=(c == KC - 1))
                        last.then_inc(q_ready, 1)
                    for n in range(H * CC):
                        h, c = n // CC, n % CC
                        lo = (h % 2) * DH
                        pe.wait_ge(qt_ready, h // 2 + 1)
                        if n >= 4:
                            pe.wait_ge(qp_used, n - 3)
                        nc.tensor.matmul(ps[:, 4 + n % 4, :], wkt[lo:lo + DH, h // 2, c * P:(c + 1) * P],
                                         qt[lo:lo + DH, h // 2, :], start=True, stop=True).then_inc(qp_ready, 1)

                @block.scalar
                def _(act):
                    for m in range(KC):
                        act.wait_ge(q_ready, m + 1)
                        nc.scalar.mul(qt[:, m, :], ps[:, m, :], DH ** -0.5).then_inc(qt_ready, 1)
                    for n in range(H * CC):
                        act.wait_ge(qp_ready, n + 1)
                        nc.scalar.copy(qp[:, n % CC, n // CC, :], ps[:, 4 + n % 4, :]).then_inc(qp_used, 1)

        with ExitStack() as c2:
            cx = core.sb(c2, "x0_cx", [P, PAIR, KT, CD])
            cxt = core.sb(c2, "x0_cxt", [P, PAIR, CC, CTX])
            qs = core.sb(c2, "x0_qs", [P, 2, CC, P])
            pr = core.sb(c2, "x0_pr", [P, 2, CTX])
            pt = core.sb(c2, "x0_pt", [P, 2, KT, P])
            o = core.sb(c2, "x0_o", [P, 2, CD])
            nmax = core.sb(c2, "x0_nmax", [P, 2])
            total = core.sb(c2, "x0_total", [P, 2])
            inv = core.sb(c2, "x0_inv", [P, 2])
            s_ps = core.pb(c2, "x0_s_ps", [P, 4 * 512])
            t_ps = core.pb(c2, "x0_t_ps", [P, 2, 512])
            o_ps = core.pb(c2, "x0_o_ps", [P, 512])
            ot_ps = core.pb(c2, "x0_ot_ps", [P, 512])
            cx_in0, cx_in1, cxt_in0, cxt_in1, qs_ready, s_ready, max_ready, exp_ready, inv_ready, t_ready, pt_ready, \
                o_ready, o_scaled, ot_ready, ot_stored = core.sems(
                    c2, "x0", "cx_in0 cx_in1 cxt_in0 cxt_in1 qs_ready s_ready max_ready exp_ready inv_ready t_ready pt_ready "
                    "o_ready o_scaled ot_ready ot_stored")
            cx_in, cxt_in = (cx_in0, cx_in1), (cxt_in0, cxt_in1)
            GR = -(-KT // 4)
            groups = [(4 * g, min(KT, 4 * g + 4)) for g in range(GR)]
            ROUNDS = B // PAIR
            with nc.Block() as block:
                @block.sync
                def _(sp):
                    def load(b, j, i):
                        if i is not None:
                            sp.wait_ge(s_ready, i * UNITS + 4 * (j + 1) + PRIMED)
                        sp.dma_start(cxt[:, j, :, :],
                                     w["ctxT"][bass.ds(b, 1), :, :].rearrange("b (c p) n -> p (b c) n", p=P)).then_inc(cxt_in[j], 16)
                        if i is not None:
                            sp.wait_ge(o_ready, i * UNITS + 4 * (j + 1))
                        sp.dma_start(cx[:, j, 0:KT - 1, :],
                                     w["ctx"][bass.ds(b, 1), 0:(KT - 1) * P, :].rearrange("b (t p) n -> p (b t) n", p=P)
                                     ).then_inc(cx_in[j], 16)
                        sp.dma_start(cx[0:LAST, j, KT - 1, :],
                                     w["ctx"][bass.ds(b, 1), (KT - 1) * P:CTX, :].rearrange("b p n -> (b p) n")
                                     ).then_inc(cx_in[j], 16)

                    for j in range(PAIR):
                        load(j, j, None)
                    with sp.Fori(0, ROUNDS - 1) as i:
                        for j in range(PAIR):
                            load((i + 1) * PAIR + j, j, i)

                @block.gpsimd
                def _(pool):
                    with pool.Fori(0, ROUNDS) as i:
                        for u in range(UNITS):
                            j, r = u // 4, u % 4
                            if u >= 2:
                                pool.wait_ge(s_ready, i * UNITS + u - 1 + PRIMED)
                            else:
                                pool.wait_ge(s_ready, i * UNITS + PRIMED)
                            nc.gpsimd.tensor_copy(
                                qs[:, u % 2, :, :].rearrange("p c (h s) -> p c h s", h=2),
                                qp[:, :, 2 * r:2 * r + 2, bass.ds((i * PAIR + j) * S, S)]).then_inc(qs_ready, 1)

                @block.tensor
                def _(pe):
                    core.prime(pe, s_ready, t_ready)
                    with pe.Fori(0, ROUNDS) as i:
                        def scores_and_turn(u):
                            if u == UNITS:
                                for g in range(GR):
                                    turn(u - 1, g)
                                return
                            j = u // 4
                            pe.wait_ge(qs_ready, i * UNITS + u + 1)
                            if u % 4 == 0:
                                pe.wait_ge(cxt_in[j], i * 16 + 16)
                            pe.wait_ge(exp_ready, i * UNITS + u + PRIMED)
                            for n in range(4):
                                a, b = 512 * n, min(512 * n + 512, CTX)
                                for c in range(CC):
                                    last = nc.tensor.matmul(s_ps[:, a:b], qs[:, u % 2, c, :], cxt[:, j, c, a:b],
                                                            start=(c == 0), stop=(c == CC - 1))
                                if n == 3:
                                    last.then_inc(s_ready, 1)
                                if u >= 1:
                                    turn(u - 1, n)

                        def turn(u, g):
                            a, b = groups[g]
                            if g == 0:
                                pe.wait_ge(exp_ready, i * UNITS + u + 1 + PRIMED)
                            pe.wait_ge(pt_ready, i * (UNITS * GR) + max(u * GR + g - 1, 0) + PRIMED)
                            for t in range(a, b):
                                rows = P if t < KT - 1 else LAST
                                last = nc.tensor.transpose(t_ps[0:rows, g % 2, (t - a) * P:(t - a + 1) * P],
                                                           pr[:, u % 2, t * P:t * P + rows], ident[:, :])
                            last.then_inc(t_ready, 1)

                        def weigh(u):
                            j = u // 4
                            if u % 4 == 0:
                                pe.wait_ge(cx_in[j], i * 32 + 32)
                            pe.wait_ge(o_scaled, i * UNITS + u + PRIMED)
                            for t in range(KT):
                                if t % 4 == 0:
                                    pe.wait_ge(pt_ready, i * (UNITS * GR) + u * GR + t // 4 + 1 + PRIMED)
                                rows = P if t < KT - 1 else LAST
                                last = nc.tensor.matmul(o_ps[:, 0:CD], pt[0:rows, u % 2, t, :], cx[0:rows, j, t, :],
                                                        start=(t == 0), stop=(t == KT - 1))
                            last.then_inc(o_ready, 1)

                        def turn_out(u):
                            pe.wait_ge(o_scaled, i * UNITS + u + 1 + PRIMED)
                            pe.wait_ge(ot_stored, i * UNITS + u + PRIMED)
                            for c in range(CC):
                                last = nc.tensor.transpose(ot_ps[:, c * P:(c + 1) * P], o[:, u % 2, c * P:(c + 1) * P],
                                                           ident[:, :])
                            last.then_inc(ot_ready, 1)

                        scores_and_turn(0)
                        for u in range(UNITS):
                            scores_and_turn(u + 1)
                            weigh(u)
                            if u >= 1:
                                turn_out(u - 1)
                        turn_out(UNITS - 1)

                @block.vector
                def _(dve):
                    core.prime(dve, pt_ready, o_scaled, inv_ready)
                    with dve.Fori(0, ROUNDS) as i:
                        def row_max(u):
                            dve.wait_ge(s_ready, i * UNITS + u + 1 + PRIMED)
                            dve.wait_ge(exp_ready, i * UNITS + max(u - 1, 0) + PRIMED)
                            nc.vector.reduce_max(nmax[:, u % 2:u % 2 + 1], s_ps[:, 0:CTX], AXIS.X, negate=True).then_inc(max_ready, 1)

                        row_max(0)
                        for u in range(UNITS):
                            dve.wait_ge(exp_ready, i * UNITS + u + 1 + PRIMED)
                            nc.vector.reciprocal(inv[:, u % 2:u % 2 + 1], total[:, u % 2:u % 2 + 1]).then_inc(inv_ready, 1)
                            for g in (0, 2):
                                a, b = groups[g]
                                dve.wait_ge(t_ready, i * (UNITS * GR) + u * GR + g + 1 + PRIMED)
                                dve.wait_ge(pt_ready, i * (UNITS * GR) + u * GR + g + PRIMED)
                                if u >= 2:
                                    dve.wait_ge(o_ready, i * UNITS + u - 1)
                                nc.vector.tensor_copy(pt[:, u % 2, a:b, :],
                                                      t_ps[:, g % 2, 0:(b - a) * P].rearrange("p (t n) -> p t n", n=P)
                                                      ).then_inc(pt_ready, 1)
                            if u + 1 < UNITS:
                                row_max(u + 1)
                            dve.wait_ge(o_ready, i * UNITS + u + 1)
                            dve.wait_ge(inv_ready, i * UNITS + u + 1 + PRIMED)
                            if u >= 2:
                                dve.wait_ge(ot_ready, i * UNITS + u - 1)
                            nc.vector.tensor_scalar(o[:, u % 2, :], o_ps[:, 0:CD], inv[:, u % 2:u % 2 + 1], None,
                                                    ALU.mult).then_inc(o_scaled, 1)

                @block.scalar
                def _(act):
                    core.prime(act, exp_ready, ot_stored)
                    def store_out(act, i, u):
                        j, r = u // 4, u % 4
                        act.wait_ge(ot_ready, i * UNITS + u + 1)
                        nc.scalar.copy(qp[:, :, 2 * r:2 * r + 2, bass.ds((i * PAIR + j) * S, S)],
                                       ot_ps[:, 0:CC * P].rearrange("p (c h s) -> p c h s", c=CC, h=2)).then_inc(ot_stored, 1)

                    with act.Fori(0, ROUNDS) as i:
                        def exponent(u):
                            act.wait_ge(max_ready, i * UNITS + u + 1)
                            act.wait_ge(inv_ready, i * UNITS + max(u - 1, 0) + PRIMED)
                            act.wait_ge(t_ready, (i * UNITS + max(u - 1, 0)) * GR + PRIMED)
                            nc.scalar.activation(pr[:, u % 2, :], s_ps[:, 0:CTX], ACT.Exp, bias=nmax[:, u % 2:u % 2 + 1],
                                                 accum_out=total[:, u % 2:u % 2 + 1]).then_inc(exp_ready, 1)

                        exponent(0)
                        for u in range(UNITS):
                            for g in (1, 3):
                                a, b = groups[g]
                                rows = P if b < KT else LAST
                                act.wait_ge(t_ready, i * (UNITS * GR) + u * GR + g + 1 + PRIMED)
                                act.wait_ge(pt_ready, i * (UNITS * GR) + u * GR + g + PRIMED)
                                nc.scalar.copy(pt[0:rows, u % 2, a:b, :],
                                               t_ps[0:rows, g % 2, 0:(b - a) * P].rearrange("p (t n) -> p t n", n=P)
                                               ).then_inc(pt_ready, 1)
                            if u + 1 < UNITS:
                                exponent(u + 1)
                            if u >= 1:
                                store_out(act, i, u - 1)
                        store_out(act, i, UNITS - 1)

        with ExitStack() as c2:
            at = core.sb(c2, "x0_at", [P, KC, TOK])
            a_ps = core.pb(c2, "x0_a_ps", [P, KC, 512])
            y_ps = core.pb(c2, "x0_y_ps", [P, TT, 512])
            a_ready, at_ready, y_ready, xb_ready = core.sems(c2, "x0", "a_ready at_ready y_ready xb_ready")
            with nc.Block() as block:
                @block.tensor
                def _(pe):
                    pe.wait_ge(w_in, 48)
                    for m in range(KC):
                        for h in (2 * m, 2 * m + 1):
                            lo = (h % 2) * DH
                            for c in range(CC):
                                last = nc.tensor.matmul(a_ps[lo:lo + DH, m, :], wv[:, c, h * DH:(h + 1) * DH], qp[:, c, h, :],
                                                        start=(c == 0), stop=(c == CC - 1))
                        last.then_inc(a_ready, 1)
                    for m in range(KC):
                        pe.wait_ge(at_ready, m + 1)
                    for t in range(TT):
                        for c in range(KC):
                            last = nc.tensor.matmul(y_ps[:, t, :], at[:, c, t * P:(t + 1) * P], wout[:, c, :],
                                                    start=(c == 0), stop=(c == KC - 1))
                        last.then_inc(y_ready, 1)

                @block.scalar
                def _(act):
                    for m in range(KC):
                        act.wait_ge(a_ready, m + 1)
                        nc.scalar.copy(at[:, m, :], a_ps[:, m, :]).then_inc(at_ready, 1)

                @block.vector
                def _(dve):
                    dve.wait_ge(w_in, 48)
                    for t in range(TT):
                        nc.vector.tensor_tensor(x[:, t, :], x[:, t, :], bout[:, :], ALU.add).then_inc(xb_ready, 1)
                    for t in range(TT):
                        dve.wait_ge(y_ready, t + 1)
                        dve.wait_ge(xb_ready, t + 1)
                        nc.vector.tensor_tensor(x[:, t, :], x[:, t, :], y_ps[:, t, :], ALU.add)


def self_attention_L0(core, x, xt, ident, w):
    nc = core.nc
    HALF = KC // 2
    with ExitStack() as ctx:
        wq = core.sb(ctx, "s0_wq", [P, KC, D])
        wk = core.sb(ctx, "s0_wk", [P, KC, D])
        wv = core.sb(ctx, "s0_wv", [P, KC, D])
        cos = core.sb(ctx, "s0_cos", [P, HALF, TOK])
        sin = core.sb(ctx, "s0_sin", [P, HALF, TOK])
        mask = core.sb(ctx, "s0_mask", [P, P])
        rot = core.sb(ctx, "s0_rot", [P, 2, KC, TOK])
        tmp = core.sb(ctx, "s0_tmp", [P, 4, HALF, TOK])
        v = core.sb(ctx, "s0_v", [P, TT, D])
        pr = core.sb(ctx, "s0_pr", [P, TT, P])
        pt = core.sb(ctx, "s0_pt", [P, TT, P])
        red = core.sb(ctx, "s0_red", [P, 3, TT])
        in_q, in_k, in_v, in_tab, qk_ready, prod_ready, rot_ready, v_ready, vs_ready, s_ready, sm_ready, max_ready, \
            exp_ready, inv_ready, norm_ready, t_ready, pt_ready, y_ready = core.sems(
                ctx, "s0", "in_q in_k in_v in_tab qk_ready prod_ready rot_ready v_ready vs_ready s_ready sm_ready "
                "max_ready exp_ready inv_ready norm_ready t_ready pt_ready y_ready")
        qk_ps = core.pb(ctx, "s0_qk_ps", [P, KC, 512])
        r_ps = core.pb(ctx, "s0_r_ps", [P, 4, 512])
        with nc.Block() as block:
            @block.sync
            def _(sp):
                for dst, name, s in ((wq, "L0_attn_Wq", in_q), (wk, "L0_attn_Wk", in_k), (wv, "L0_attn_Wv", in_v)):
                    sp.dma_start(dst[:, :, :], w[name].rearrange("(c p) n -> p c n", p=P)).then_inc(s, 16)
                sp.dma_start(cos[:, :, :], w["rope_cos"].rearrange("(c p) n -> p c n", p=P)).then_inc(in_tab, 16)
                sp.dma_start(sin[:, :, :], w["rope_sin"].rearrange("(c p) n -> p c n", p=P)).then_inc(in_tab, 16)
                sp.dma_start(mask[:, :], w["mask_L0"]).then_inc(in_tab, 16)

            @block.tensor
            def _(pe):
                for a, (wt, s) in enumerate(((wq, in_q), (wk, in_k))):
                    pe.wait_ge(s, 16)
                    if a == 1:
                        pe.wait_ge(prod_ready, 4)
                    for m in range(KC):
                        for c in range(KC):
                            last = nc.tensor.matmul(qk_ps[:, m, :], wt[:, c, m * P:(m + 1) * P], xt[:, c, :],
                                                    start=(c == 0), stop=(c == KC - 1))
                    last.then_inc(qk_ready, 1)
                pe.wait_ge(in_v, 16)
                for t in range(TT):
                    for c in range(KC):
                        last = nc.tensor.matmul(r_ps[:, t, :], xt[:, c, t * P:(t + 1) * P], wv[:, c, :],
                                                start=(c == 0), stop=(c == KC - 1))
                    last.then_inc(v_ready, 1)
                pe.wait_ge(rot_ready, 4)
                for t in range(TT):
                    pe.wait_ge(vs_ready, t + 1)
                    for c in range(KC):
                        last = nc.tensor.matmul(r_ps[:, t, 0:P], rot[:, 0, c, t * P:(t + 1) * P], rot[:, 1, c, t * P:(t + 1) * P],
                                                start=(c == 0), stop=(c == KC - 1))
                    last.then_inc(s_ready, 1)
                for t in range(TT):
                    pe.wait_ge(norm_ready, t + 1)
                    nc.tensor.transpose(qk_ps[:, t, 0:P], pr[:, t, :], ident[:, :]).then_inc(t_ready, 1)
                for t in range(TT):
                    pe.wait_ge(pt_ready, t + 1)
                    nc.tensor.matmul(r_ps[:, t, :], pt[:, t, :], v[:, t, :], start=True, stop=True).then_inc(y_ready, 1)

            @block.vector
            def _(dve):
                dve.wait_ge(in_tab, 48)
                for a in range(2):
                    even, odd = qk_ps[:, 0:HALF, :], qk_ps[:, HALF:KC, :]
                    dve.wait_ge(qk_ready, a + 1)
                    dve.wait_ge(rot_ready, 2 * a)
                    for n, (part, table) in enumerate(((even, cos), (odd, sin), (even, sin), (odd, cos))):
                        nc.vector.tensor_tensor(tmp[:, n, :, :], part, table[:, :, :], ALU.mult).then_inc(prod_ready, 1)
                    dve.wait_ge(prod_ready, 4 * a + 4)
                    nc.vector.tensor_tensor(rot[:, a, 0:HALF, :], tmp[:, 0, :, :], tmp[:, 1, :, :], ALU.subtract).then_inc(rot_ready, 1)
                    nc.vector.tensor_tensor(rot[:, a, HALF:KC, :], tmp[:, 2, :, :], tmp[:, 3, :, :], ALU.add).then_inc(rot_ready, 1)
                for t in range(TT):
                    dve.wait_ge(s_ready, t + 1)
                    nc.vector.scalar_tensor_tensor(pr[:, t, :], r_ps[:, t, 0:P], D ** -0.5, mask[:, :],
                                                   ALU.mult, ALU.add).then_inc(sm_ready, 1)
                for t in range(TT):
                    dve.wait_ge(sm_ready, t + 1)
                    nc.vector.reduce_max(red[:, 0, t:t + 1], pr[:, t, :], AXIS.X, negate=True).then_inc(max_ready, 1)
                for t in range(TT):
                    dve.wait_ge(exp_ready, t + 1)
                    nc.vector.reciprocal(red[:, 2, t:t + 1], red[:, 1, t:t + 1]).then_inc(inv_ready, 1)
                for t in range(TT):
                    dve.wait_ge(inv_ready, t + 1)
                    nc.vector.tensor_scalar(pr[:, t, :], pr[:, t, :], red[:, 2, t:t + 1], None, ALU.mult).then_inc(norm_ready, 1)
                for t in range(TT):
                    dve.wait_ge(y_ready, t + 1)
                    nc.vector.tensor_tensor(x[:, t, :], x[:, t, :], r_ps[:, t, :], ALU.add)

            @block.scalar
            def _(act):
                for t in range(TT):
                    act.wait_ge(v_ready, t + 1)
                    nc.scalar.copy(v[:, t, :], r_ps[:, t, :]).then_inc(vs_ready, 1)
                for t in range(TT):
                    act.wait_ge(max_ready, t + 1)
                    nc.scalar.activation(pr[:, t, :], pr[:, t, :], ACT.Exp, bias=red[:, 0, t:t + 1],
                                         accum_out=red[:, 1, t:t + 1]).then_inc(exp_ready, 1)
                for t in range(TT):
                    act.wait_ge(t_ready, t + 1)
                    nc.scalar.copy(pt[:, t, :], qk_ps[:, t, 0:P]).then_inc(pt_ready, 1)


class RouteWeights:

    def __init__(self, core, ctx, name, weight, bias, w):
        self.weight, self.bias, self.w = weight, bias, w
        self.wr = core.sb(ctx, f"{name}_wr", [P, KC, EXPERTS])
        self.br = core.sb(ctx, f"{name}_br", [P, EXPERTS])
        self.before = core.sb(ctx, f"{name}_before", [P, P])
        self.w_in, self.before_in = core.sems(ctx, f"{name}w", "w_in before_in")

    def load(self, sp):
        sp.dma_start(self.wr[:, :, :], self.weight.rearrange("(c p) n -> p c n", p=P)).then_inc(self.w_in, 16)
        if self.bias is not None:
            sp.dma_start(self.br[:, :], bcast(self.bias)).then_inc(self.w_in, 16)
        sp.dma_start(self.before[:, :], self.w["before"]).then_inc(self.before_in, 16)


def route(core, name, normed_t, weights, normalise, chosen, ident):
    nc = core.nc
    gate, gate_t, slot, count = chosen
    E = EXPERTS
    NOWHERE = 2.0 ** 20
    wr, br, before, bias, w_in, before_in = weights.wr, weights.br, weights.before, weights.bias, weights.w_in, weights.before_in
    KEPT, FILL, TAKEN = 2, -1.0, -2.0
    with ExitStack() as ctx:
        sc = core.sb(ctx, f"{name}_sc", [P, TT, 2 * E])
        rep = core.sb(ctx, f"{name}_rep", [P, TT, 2 * E])
        top = core.sb(ctx, f"{name}_top", [P, TT, E])
        red = core.sb(ctx, f"{name}_red", [P, 5, TT])
        picked = core.sb(ctx, f"{name}_picked", [P, TT, E])
        away = core.sb(ctx, f"{name}_away", [P, TT, E])
        ones = core.sb(ctx, f"{name}_ones", [P, P])
        n_ps = core.pb(ctx, f"{name}_n_ps", [P, 512])
        c_ps = core.pb(ctx, f"{name}_c_ps", [P, 512])
        l_ps = core.pb(ctx, f"{name}_l_ps", [P, 512])
        g_ps = core.pb(ctx, f"{name}_g_ps", [P, 512])
        l_ready, steps, exp_ready, gate_ready, gt_ready, picked_ready, n_ready, away_ready, ones_ready = core.sems(
            ctx, name, "l_ready steps exp_ready gate_ready gt_ready picked_ready n_ready away_ready ones_ready")
        with nc.Block() as block:
            @block.gpsimd
            def _(pool):
                nc.gpsimd.memset(ones[:, :], 1.0).then_inc(ones_ready, 1)

            @block.tensor
            def _(pe):
                pe.wait_ge(w_in, 32 if bias is not None else 16)
                for t in range(TT):
                    for c in range(KC):
                        last = nc.tensor.matmul(l_ps[:, t * E:(t + 1) * E], normed_t[:, c, t * P:(t + 1) * P], wr[:, c, :],
                                                start=(c == 0), stop=(c == KC - 1))
                last.then_inc(l_ready, 1)
                pe.wait_ge(picked_ready, 1)
                pe.wait_ge(before_in, 16)
                pe.wait_ge(ones_ready, 1)
                for t in range(TT):
                    for r in range(t):
                        nc.tensor.matmul(n_ps[:, t * E:(t + 1) * E], ones[:, :], picked[:, r, :], start=(r == 0), stop=False)
                    nc.tensor.matmul(n_ps[:, t * E:(t + 1) * E], before[:, :], picked[:, t, :], start=(t == 0), stop=True)
                for t in range(TT):
                    last = nc.tensor.matmul(c_ps[0:1, 0:E], ones[:, 0:1], picked[:, t, :], start=(t == 0), stop=(t == TT - 1))
                last.then_inc(n_ready, 1)
                pe.wait_ge(gate_ready, TT)
                for t in range(TT):
                    last = nc.tensor.transpose(g_ps[0:E, t * P:(t + 1) * P], gate[:, t, :], ident[:, :])
                last.then_inc(gt_ready, 1)

            @block.scalar
            def _(act):
                for t in range(TT):
                    act.wait_ge(steps, 3 + t + 1)
                    nc.scalar.activation(sc[:, t, 0:E], sc[:, t, 0:E], ACT.Exp, bias=red[:, 0, t:t + 1],
                                         accum_out=red[:, 1, t:t + 1]).then_inc(exp_ready, 1)
                act.wait_ge(gt_ready, 1)
                nc.scalar.copy(gate_t[:, :], g_ps[0:E, :])

            @block.vector
            def _(dve):
                done = [0]

                def step(instruction):
                    done[0] += 1
                    instruction.then_inc(steps, 1)

                def sync():
                    dve.wait_ge(steps, done[0])

                step(nc.vector.memset(sc[:, :, E:2 * E], FILL))
                step(nc.vector.memset(top[:, :, :], FILL))
                dve.wait_ge(l_ready, 1)
                logits = l_ps[:, 0:TT * E].rearrange("p (t e) -> p t e", e=E)
                if bias is not None:
                    step(nc.vector.tensor_tensor(sc[:, :, 0:E], logits, br[:, :].unsqueeze(1).broadcast_to([P, TT, E]), ALU.add))
                else:
                    step(nc.vector.tensor_copy(sc[:, :, 0:E], logits))
                sync()
                for t in range(TT):
                    step(nc.vector.reduce_max(red[:, 0, t:t + 1], sc[:, t, 0:E], AXIS.X, negate=True))
                dve.wait_ge(exp_ready, TT)
                step(nc.vector.reciprocal(red[:, 2, :], red[:, 1, :]))
                sync()
                for t in range(TT):
                    step(nc.vector.tensor_scalar(sc[:, t, 0:E], sc[:, t, 0:E], red[:, 2, t:t + 1], None, ALU.mult))
                sync()
                for t in range(TT):
                    step(nc.vector.max(rep[:, t, 0:E], sc[:, t, 0:E]))
                sync()
                step(nc.vector.tensor_copy(top[:, :, 0:KEPT], rep[:, :, 0:KEPT]))
                step(nc.vector.tensor_tensor(red[:, 3, :], rep[:, :, 0], rep[:, :, 1], ALU.add))
                sync()
                step(nc.vector.reciprocal(red[:, 4, :], red[:, 3, :]))
                for t in range(TT):
                    step(nc.vector.match_replace(rep[:, t, :], top[:, t, :], sc[:, t, :], TAKEN))
                sync()
                nc.vector.tensor_scalar(picked[:, :, :], rep[:, :, 0:E], TAKEN, None, ALU.is_equal).then_inc(picked_ready, 1)
                dve.wait_ge(picked_ready, 1)
                nc.vector.tensor_scalar(away[:, :, :], picked[:, :, :], -NOWHERE, NOWHERE, ALU.mult, ALU.add).then_inc(away_ready, 1)
                dve.wait_ge(away_ready, 1)
                dve.wait_ge(n_ready, 1)
                nc.vector.tensor_tensor(slot[:, :, :], n_ps[:, 0:TT * E].rearrange("p (t e) -> p t e", e=E), away[:, :, :], ALU.add)
                nc.vector.tensor_copy(count[0:1, :], c_ps[0:1, 0:E])
                for t in range(TT):
                    ins = nc.vector.scalar_tensor_tensor(gate[:, t, :], rep[:, t, 0:E], TAKEN, sc[:, t, 0:E],
                                                         ALU.is_equal, ALU.mult)
                    if normalise:
                        step(ins)
                    else:
                        ins.then_inc(gate_ready, 1)
                if normalise:
                    sync()
                    for t in range(TT):
                        nc.vector.tensor_scalar(gate[:, t, :], gate[:, t, :], red[:, 4, t:t + 1], None,
                                                ALU.mult).then_inc(gate_ready, 1)


class ExpertWeights:

    def __init__(self, core, ctx, name, up_w, up_b, down_w, down_b, w, ahead):
        self.up_w, self.up_b, self.down_w = up_w, up_b, down_w
        self.w1 = core.sb(ctx, f"{name}_w1", [P, PAIR, KC, up_w.shape[2]])
        self.w2 = core.sb(ctx, f"{name}_w2", [P, PAIR, down_w.shape[1] // P, D])
        self.b1 = core.sb(ctx, f"{name}_b1", [P, PAIR, up_b.shape[2]])
        self.b2 = core.sb(ctx, f"{name}_b2", [EXPERTS, D])
        self.slots = core.sb(ctx, f"{name}_slots", [P, TOK])
        self.c_in, w1_in0, w1_in1, w2_in0, w2_in1 = core.sems(ctx, f"{name}w", "c_in w1_in0 w1_in1 w2_in0 w2_in1")
        self.w1_in, self.w2_in = (w1_in0, w1_in1), (w2_in0, w2_in1)
        with core.nc.Block() as block:
            @block.sync
            def _(sp):
                for load in ahead:
                    load(sp)
                sp.dma_start(self.b2[:, :], down_b).then_inc(self.c_in, 16)
                sp.dma_start(self.slots[:, :], bcast(w["slots"])).then_inc(self.c_in, 16)
                for j in range(PAIR):
                    self.load(sp, j, j)

    def load(self, sp, e, j):
        sp.dma_start(self.w1[:, j, :, :], self.up_w[bass.ds(e, 1), :, :].rearrange("e (c p) n -> p (e c) n", p=P)).then_inc(self.w1_in[j], 16)
        sp.dma_start(self.b1[:, j, :], self.up_b[bass.ds(e, 1), :, :].rearrange("e p n -> (e p) n")).then_inc(self.w1_in[j], 16)
        sp.dma_start(self.w2[:, j, :, :], self.down_w[bass.ds(e, 1), :, :].rearrange("e (c p) n -> p (e c) n", p=P)).then_inc(self.w2_in[j], 16)


def experts(core, name, normed, acc, chosen, weights, hidden, gated):
    nc = core.nc
    gate, gate_t, slot, count = chosen
    E = EXPERTS
    ALPHA, LIMIT = 1.702, 7.0
    HC = hidden // P
    w1, w2, b1, b2, slots = weights.w1, weights.w2, weights.b1, weights.b2, weights.slots
    c_in, w1_in, w2_in = weights.c_in, weights.w1_in, weights.w2_in
    UPS = w1.shape[3] // hidden
    PER = 4 // UPS
    NG = HC // PER
    ROUNDS = E // PAIR
    STEPS = 2 * PER + 2
    TURNS = E * TT
    with ExitStack() as ctx:
        g2 = core.sb(ctx, f"{name}_g2", [P, 2, PAIR, TT])
        hot = core.sb(ctx, f"{name}_hot", [P, 2, TT, P])
        back = core.sb(ctx, f"{name}_back", [P, TOK])
        xg = core.sb(ctx, f"{name}_xg", [P, KC, P])
        h = core.sb(ctx, f"{name}_h", [P, HC, P])
        y = core.sb(ctx, f"{name}_y", [P, D])
        tmp = core.sb(ctx, f"{name}_tmp", [P, 4, PER, P]) if gated else None
        a_ps = core.pb(ctx, f"{name}_a_ps", [P, TT, 512])
        u_ps = core.pb(ctx, f"{name}_u_ps", [P, 2, 4, P])
        x_ps = core.pb(ctx, f"{name}_x_ps", [P, KC, P])
        y_ps = core.pb(ctx, f"{name}_y_ps", [P, 512])
        zeroed, expert_done, g2_ready, hot_ready, x_ready, xg_ready, t_ready, back_ready, \
            up_ready, h_ready, down_ready, y_ready, sum_ready, parts, sig_ready = core.sems(
                ctx, name, "zeroed expert_done g2_ready hot_ready x_ready xg_ready t_ready "
                "back_ready up_ready h_ready down_ready y_ready sum_ready parts sig_ready")

        def turns(engine, each_turn, each_round=None, first=None, last=None):
            register = engine.alloc_register(f"{name}_turns_{engine.engine.name}")
            engine.reg_mov(register, 0)
            with engine.Fori(0, ROUNDS) as i:
                if each_round:
                    each_round(i, engine.snap(register, min_val=0, max_val=TURNS))
                for j in range(PAIR):
                    if first:
                        first(i, j)
                    tokens = engine.value_load(count[0:1, bass.ds(i * PAIR + j, 1)], min_val=0, max_val=TOK)
                    with engine.Fori(0, TT) as k:
                        with engine.If(k * P < tokens):
                            each_turn(i, j, k, engine.snap(register, min_val=0, max_val=TURNS))
                            engine.reg_add(register, register, 1)
                    if last:
                        last()
            return engine.snap(register, min_val=0, max_val=TURNS)

        with nc.Block() as block:
            @block.sync
            def _(sp):
                with sp.Fori(0, ROUNDS - 1) as i:
                    for j in range(PAIR):
                        sp.wait_ge(expert_done, i * PAIR + j + 1)
                        weights.load(sp, (i + 1) * PAIR + j, j)

            @block.gpsimd
            def _(pool):
                nc.gpsimd.memset(back[:, :], 0.0).then_inc(zeroed, 1)

            @block.tensor
            def _(pe):
                pe.wait_ge(c_in, 32)
                pe.wait_ge(zeroed, 1)
                for t in range(TT):
                    nc.tensor.matmul(a_ps[:, t, :], gate_t[:, t * P:(t + 1) * P], b2[:, :], start=True, stop=True)
                nc.tensor.matmul(y_ps[:, :], back[:, 0:P], slots[:, :], start=True, stop=True).then_inc(down_ready, 1)
                core.prime(pe, t_ready, hot_ready, back_ready)

                def first(i, j):
                    pe.wait_ge(w1_in[j], i * 32 + 32)
                    pe.wait_ge(w2_in[j], i * 16 + 16)

                def scatter(t):
                    pe.wait_ge(y_ready, t + 1)
                    for r in range(TT):
                        done = nc.tensor.matmul(a_ps[:, r, :], back[:, r * P:(r + 1) * P], y[:, :], start=False, stop=True,
                                                skip_group_check=True)
                    return done

                def each_turn(i, j, k, t):
                    pe.wait_ge(hot_ready, t + 1 + PRIMED)
                    pe.wait_ge(back_ready, t + PRIMED)
                    for c in range(KC):
                        for r in range(TT):
                            last = nc.tensor.matmul(x_ps[:, c, :], normed[:, r, c * P:(c + 1) * P], hot[:, 0, r, :],
                                                    start=(r == 0), stop=(r == TT - 1))
                    last.then_inc(x_ready, 1)
                    pe.wait_ge(xg_ready, t + 1)

                    def up(g):
                        if g >= 2:
                            pe.wait_ge(h_ready, t * NG + g - 1)
                        for n in range(PER):
                            c = g * PER + n
                            for a in range(UPS):
                                for m in range(KC):
                                    last = nc.tensor.matmul(u_ps[:, g % 2, a * PER + n, :],
                                                            w1[:, j, m, a * hidden + c * P:a * hidden + (c + 1) * P], xg[:, m, :],
                                                            start=(m == 0), stop=(m == KC - 1))
                        last.then_inc(up_ready, 1)

                    def down(g):
                        pe.wait_ge(h_ready, t * NG + g + 1)
                        for c in range(g * PER, (g + 1) * PER):
                            last = nc.tensor.matmul(y_ps[:, :], h[:, c, :], w2[:, j, c, :], start=(c == 0), stop=(c == HC - 1))
                        if g == NG - 1:
                            last.then_inc(down_ready, 1)

                    up(0)
                    for g in range(NG):
                        if g + 1 < NG:
                            up(g + 1)
                        if g == 0:
                            scatter(t)
                            for r in range(TT):
                                last = nc.tensor.transpose(x_ps[:, r, :], hot[:, 1, r, :], core.ident[:, :])
                            last.then_inc(t_ready, 1)
                        down(g)

                t = turns(pe, each_turn, first=first, last=lambda: pe.drain().then_inc(expert_done, 1))
                scatter(t).then_inc(sum_ready, 1)

            @block.vector
            def _(dve):
                V = nc.vector

                def each_round(i, t):
                    dve.wait_ge(hot_ready, t + PRIMED)
                    for n, source in enumerate((slot, gate)):
                        V.tensor_copy(g2[:, n, :, :], source[:, :, bass.ds(i * PAIR, PAIR)].rearrange("p t e -> p e t")).then_inc(g2_ready, 1)
                    dve.wait_ge(g2_ready, 2 * i + 2)

                def first(i, j):
                    dve.wait_ge(w1_in[j], i * 32 + 32)

                def take(t):
                    dve.wait_ge(down_ready, t + 1)
                    V.tensor_copy(y[:, :], y_ps[:, :]).then_inc(y_ready, 1)

                def each_turn(i, j, k, t):
                    dve.wait_ge(t_ready, t + PRIMED)
                    for r in range(TT):
                        number = slots[:, bass.ds(k * P, P)]
                        V.tensor_scalar(hot[:, 0, r, :], number, g2[:, 0, j, r:r + 1], None, ALU.is_equal)
                        last = V.tensor_scalar(hot[:, 1, r, :], number, g2[:, 0, j, r:r + 1], g2[:, 1, j, r:r + 1],
                                               ALU.is_equal, ALU.mult)
                    last.then_inc(hot_ready, 1)
                    take(t)
                    dve.wait_ge(x_ready, t + 1)
                    V.tensor_copy(xg[:, :, :], x_ps[:, :, :]).then_inc(xg_ready, 1)
                    if gated:
                        for g in range(NG):
                            done = (t * NG + g) * STEPS
                            dve.wait_ge(up_ready, t * NG + g + 1)
                            for n in range(PER):
                                c = g * PER + n
                                V.tensor_scalar(tmp[:, 0, n, :], u_ps[:, g % 2, n, :], b1[:, j, c:c + 1], LIMIT,
                                                ALU.add, ALU.min).then_inc(parts, 1)
                            for n in range(PER):
                                c = g * PER + n
                                V.tensor_scalar(tmp[:, 1, n, :], u_ps[:, g % 2, PER + n, :], b1[:, j, HC + c:HC + c + 1], LIMIT,
                                                ALU.add, ALU.min).then_inc(parts, 1)
                            dve.wait_ge(parts, done + 2 * PER)
                            V.tensor_scalar(tmp[:, 2, :, :], tmp[:, 1, :, :], -LIMIT, 1.0, ALU.max, ALU.add).then_inc(parts, 1)
                            dve.wait_ge(parts, done + 2 * PER + 1)
                            V.tensor_tensor(tmp[:, 2, :, :], tmp[:, 2, :, :], tmp[:, 0, :, :], ALU.mult).then_inc(parts, 1)
                            dve.wait_ge(parts, done + STEPS)
                            dve.wait_ge(sig_ready, t * NG + g + 1)
                            V.tensor_tensor(h[:, g * PER:(g + 1) * PER, :], tmp[:, 2, :, :], tmp[:, 3, :, :],
                                            ALU.mult).then_inc(h_ready, 1)
                    dve.wait_ge(t_ready, t + 1 + PRIMED)
                    V.tensor_copy(back[:, :].rearrange("p (r n) -> p r n", n=P), x_ps[:, :, :]).then_inc(back_ready, 1)

                dve.wait_ge(c_in, 32)
                t = turns(dve, each_turn, each_round=each_round, first=first if gated else None)
                take(t)
                dve.wait_ge(sum_ready, 1)
                for r in range(TT):
                    V.tensor_tensor(acc[:, r, :], acc[:, r, :], a_ps[:, r, :], ALU.add)

            @block.scalar
            def _(act):
                def each_turn(i, j, k, t):
                    for g in range(NG):
                        if gated:
                            act.wait_ge(parts, (t * NG + g) * STEPS + PER)
                            nc.scalar.activation(tmp[:, 3, :, :], tmp[:, 0, :, :], ACT.Sigmoid, scale=ALPHA).then_inc(sig_ready, 1)
                        else:
                            act.wait_ge(up_ready, t * NG + g + 1)
                            for n in range(PER):
                                c = g * PER + n
                                last = nc.scalar.activation(h[:, c, :], u_ps[:, g % 2, n, :], ACT.Gelu, bias=b1[:, j, c:c + 1])
                            last.then_inc(h_ready, 1)

                def first(i, j):
                    act.wait_ge(w1_in[j], i * 32 + 32)

                turns(act, each_turn, first=first)


def choice(core, ctx, name):
    return (core.sb(ctx, f"{name}_gate", [P, TT, EXPERTS]), core.sb(ctx, f"{name}_gate_t", [EXPERTS, TOK]),
            core.sb(ctx, f"{name}_slot", [P, TT, EXPERTS]), core.sb(ctx, f"{name}_count", [1, EXPERTS], mybir.dt.int32))


def moe_L0(core, x, xn, xt, ident, w):
    with ExitStack() as ctx:
        chosen = choice(core, ctx, "m0")
        router = RouteWeights(core, ctx, "r0", w["L0_ffn_router_weight"], w["L0_ffn_router_bias"], w)
        weights = ExpertWeights(core, ctx, "e0", w["L0_ffn_gate_up_proj"], w["L0_ffn_gate_up_bias"],
                                w["L0_ffn_down_proj"], w["L0_ffn_down_bias"], w, ahead=(router.load,))
        route(core, "r0", xt, router, False, chosen, ident)
        experts(core, "e0", xn, x, chosen, weights, hidden=512, gated=True)


def moe_L1(core, x, xn, xt, ident, w):
    nc = core.nc
    with ExitStack() as ctx:
        chosen = choice(core, ctx, "m1")
        acc = core.sb(ctx, "m1_acc", [P, TT, D])
        rows = core.sb(ctx, "m1_rows", [P, 3, D])
        ws = core.sb(ctx, "m1_ws", [P, KC, D])
        w_in, = core.sems(ctx, "m1w", "w_in")

        def load_shared(sp):
            sp.dma_start(ws[:, :, :], w["L1_ffn_shared_W"].rearrange("(c p) n -> p c n", p=P)).then_inc(w_in, 16)
            for n, k in enumerate(("L1_ffn_shared_b", "L1_ffn_gamma", "L1_ffn_beta")):
                sp.dma_start(rows[:, n, :], bcast(w[k])).then_inc(w_in, 16)

        router = RouteWeights(core, ctx, "r1", w["L1_ffn_gate_W"], None, w)
        weights = ExpertWeights(core, ctx, "e1", w["L1_ffn_W1"], w["L1_ffn_b1"], w["L1_ffn_W2"], w["L1_ffn_b2"], w,
                                ahead=(load_shared, router.load))
        with ExitStack() as c2:
            s_ps = core.pb(c2, "m1_s_ps", [P, TT, 512])
            s_ready, b_ready, g_ready = core.sems(c2, "m1", "s_ready b_ready g_ready")
            with nc.Block() as block:
                @block.tensor
                def _(pe):
                    pe.wait_ge(w_in, 64)
                    for t in range(TT):
                        for c in range(KC):
                            last = nc.tensor.matmul(s_ps[:, t, :], xt[:, c, t * P:(t + 1) * P], ws[:, c, :],
                                                    start=(c == 0), stop=(c == KC - 1))
                        last.then_inc(s_ready, 1)

                @block.vector
                def _(dve):
                    dve.wait_ge(w_in, 64)
                    for t in range(TT):
                        dve.wait_ge(s_ready, t + 1)
                        nc.vector.tensor_tensor(acc[:, t, :], s_ps[:, t, :], rows[:, 0, :], ALU.add).then_inc(b_ready, 1)
                    for t in range(TT):
                        dve.wait_ge(g_ready, t + 1)
                        nc.vector.tensor_scalar(acc[:, t, :], acc[:, t, :], 0.5, None, ALU.mult)

                @block.scalar
                def _(act):
                    for t in range(TT):
                        act.wait_ge(b_ready, t + 1)
                        nc.scalar.activation(acc[:, t, :], acc[:, t, :], ACT.Gelu).then_inc(g_ready, 1)
        route(core, "r1", xt, router, True, chosen, ident)
        experts(core, "e1", xn, acc, chosen, weights, hidden=2048, gated=False)
        norm_stage(core, "n6", acc, acc, None, ident, gamma=rows[:, 1, :], beta=rows[:, 2, :], out=x)


def self_attention_L1(core, x, xt, ident, w):
    nc = core.nc
    H, DH = 16, 64
    HC = H * DH // P
    G = 4
    NG = H // G
    U = TT * NG
    q_scale = math.sqrt(DH / D) ** 2 / DH
    z_scale = math.sqrt(DH / D) * math.sqrt(D / DH) / H
    with ExitStack() as ctx:
        wqkv = core.sb(ctx, "s1_wqkv", [P, 2, KC, H * DH])
        wz = core.sb(ctx, "s1_wz", [P, HC, D])
        mask = core.sb(ctx, "s1_mask", [P, G, P])
        qk = core.sb(ctx, "s1_qk", [P, 2, HC, TOK])
        v = core.sb(ctx, "s1_v", [P, TT, H * DH])
        pr = core.sb(ctx, "s1_pr", [P, 2, G, P])
        pt = core.sb(ctx, "s1_pt", [P, 2, G, P])
        yt = core.sb(ctx, "s1_yt", [P, 2, HC, P])
        red = core.sb(ctx, "s1_red", [P, 2, 3, G])
        in_q, in_k, in_v, in_m, p_ready, p_used, s_ready, steps, exp_ready, inv_ready, norm_ready, t_ready, \
            pt_ready, y_ready, yt_ready, z_ready, z_used = core.sems(
                ctx, "s1", "in_q in_k in_v in_m p_ready p_used s_ready steps exp_ready inv_ready norm_ready t_ready "
                "pt_ready y_ready yt_ready z_ready z_used")
        ps = core.pb(ctx, "s1_ps", [P, 8, 512])
        s_bank, t_bank, y_bank, z_bank = (0, 1), (2, 3), (4, 5), 6
        with nc.Block() as block:
            @block.sync
            def _(sp):
                def load(slot, name, s):
                    sp.dma_start(wqkv[:, slot, :, :], w[name].rearrange("(c p) n -> p c n", p=P)).then_inc(s, 16)
                load(0, "L1_attn_Q", in_q)
                load(1, "L1_attn_K", in_k)
                sp.dma_start(wz[:, :, :], w["L1_attn_W"].rearrange("(c p) n -> p c n", p=P)).then_inc(in_m, 16)
                sp.dma_start(mask[:, :, :], w["mask_L1"].unsqueeze(1).broadcast_to([P, G, P])).then_inc(in_m, 16)
                sp.wait_ge(p_ready, HC)
                load(0, "L1_attn_V", in_v)

            @block.tensor
            def _(pe):
                for n in range(2 * HC):
                    a, m = n // HC, n % HC
                    if m == 0:
                        pe.wait_ge((in_q, in_k)[a], 16)
                    if n >= 8:
                        pe.wait_ge(p_used, n - 7)
                    for c in range(KC):
                        last = nc.tensor.matmul(ps[:, n % 8, :], wqkv[:, a, c, m * P:(m + 1) * P], xt[:, c, :],
                                                start=(c == 0), stop=(c == KC - 1))
                    last.then_inc(p_ready, 1)
                pe.wait_ge(in_v, 16)
                for n in range(2 * TT):
                    t, half = n // 2, n % 2
                    pe.wait_ge(p_used, 2 * HC + n - 7)
                    for c in range(KC):
                        last = nc.tensor.matmul(ps[:, n % 8, :], xt[:, c, t * P:(t + 1) * P], wqkv[:, 0, c, half * 512:(half + 1) * 512],
                                                start=(c == 0), stop=(c == KC - 1))
                    last.then_inc(p_ready, 1)
                pe.wait_ge(p_used, 2 * HC + 2 * TT)

                def scores(u):
                    t, g = u // NG, u % NG
                    if u >= 2:
                        pe.wait_ge(steps, 4 * (u - 2) + 1)
                    lo = (g % 2) * DH
                    for k in range(G):
                        c = (g // 2) * G + k
                        last = nc.tensor.matmul(ps[:, s_bank[u % 2], k * P:(k + 1) * P], qk[lo:lo + DH, 0, c, t * P:(t + 1) * P],
                                                qk[lo:lo + DH, 1, c, t * P:(t + 1) * P], start=True, stop=True)
                    last.then_inc(s_ready, 1)

                def turn(u):
                    pe.wait_ge(norm_ready, u + 1)
                    if u >= 2:
                        pe.wait_ge(pt_ready, u - 1)
                    for k in range(G):
                        last = nc.tensor.transpose(ps[:, t_bank[u % 2], k * P:(k + 1) * P], pr[:, u % 2, k, :], ident[:, :])
                    last.then_inc(t_ready, 1)

                def weigh(u):
                    t, g = u // NG, u % NG
                    pe.wait_ge(pt_ready, u + 1)
                    if u >= 2:
                        pe.wait_ge(yt_ready, u - 1)
                    lo = (g % 2) * DH
                    for k in range(G):
                        h = 2 * ((g // 2) * G + k) + g % 2
                        last = nc.tensor.matmul(ps[lo:lo + DH, y_bank[u % 2], k * P:(k + 1) * P],
                                                v[:, t, h * DH:(h + 1) * DH], pt[:, u % 2, k, :], start=True, stop=True)
                    last.then_inc(y_ready, 1)

                def project(t):
                    pe.wait_ge(yt_ready, (t + 1) * NG)
                    if t >= 1:
                        pe.wait_ge(z_used, t)
                    for c in range(HC):
                        last = nc.tensor.matmul(ps[:, z_bank, :], yt[:, t % 2, c, :], wz[:, c, :], start=(c == 0), stop=(c == HC - 1))
                    last.then_inc(z_ready, 1)

                pe.wait_ge(in_m, 32)
                for u in range(U + 3):
                    if u < U:
                        scores(u)
                    if 1 <= u <= U:
                        turn(u - 1)
                    if 2 <= u <= U + 1:
                        weigh(u - 2)
                    if u >= 3 and (u - 3) % NG == NG - 1:
                        project((u - 3) // NG)

            @block.scalar
            def _(act):
                for n in range(0, 2 * HC + 2 * TT):
                    act.wait_ge(p_ready, n + 1)
                    if n < 2 * HC:
                        nc.scalar.copy(qk[:, n // HC, n % HC, :], ps[:, n % 8, :]).then_inc(p_used, 1)
                    else:
                        m = n - 2 * HC
                        nc.scalar.copy(v[:, m // 2, (m % 2) * 512:(m % 2 + 1) * 512], ps[:, n % 8, :]).then_inc(p_used, 1)
                for u in range(U + 2):
                    if u < U:
                        act.wait_ge(steps, 4 * u + 3)
                        nc.scalar.activation(pr[:, u % 2, :, :], pr[:, u % 2, :, :], ACT.Exp).then_inc(exp_ready, 1)
                    if 1 <= u <= U:
                        act.wait_ge(t_ready, u)
                        if u >= 3:
                            act.wait_ge(y_ready, u - 2)
                        nc.scalar.copy(pt[:, (u - 1) % 2, :, :], ps[:, t_bank[(u - 1) % 2], :].rearrange("p (g n) -> p g n", g=G)
                                       ).then_inc(pt_ready, 1)
                    if u >= 2:
                        t, g = (u - 2) // NG, (u - 2) % NG
                        act.wait_ge(y_ready, u - 1)
                        if t >= 2:
                            act.wait_ge(z_ready, t - 1)
                        lo = (g % 2) * DH
                        nc.scalar.copy(yt[lo:lo + DH, t % 2, (g // 2) * G:(g // 2 + 1) * G, :],
                                       ps[lo:lo + DH, y_bank[(u - 2) % 2], :].rearrange("p (c n) -> p c n", c=G)).then_inc(yt_ready, 1)

            @block.vector
            def _(dve):
                def add(dve, t):
                    dve.wait_ge(z_ready, t + 1)
                    nc.vector.scalar_tensor_tensor(x[:, t, :], ps[:, z_bank, :], z_scale, x[:, t, :],
                                                   ALU.mult, ALU.add).then_inc(z_used, 1)

                dve.wait_ge(in_m, 32)
                for u in range(U):
                    k = u % 2
                    dve.wait_ge(s_ready, u + 1)
                    if u >= 2:
                        dve.wait_ge(t_ready, u - 1)
                    nc.vector.scalar_tensor_tensor(pr[:, k, :, :], ps[:, s_bank[k], :].rearrange("p (g n) -> p g n", g=G), q_scale,
                                                   mask[:, :, :], ALU.mult, ALU.add).then_inc(steps, 1)
                    dve.wait_ge(steps, 4 * u + 1)
                    nc.vector.reduce_max(red[:, k, 0, :], pr[:, k, :, :], AXIS.X).then_inc(steps, 1)
                    dve.wait_ge(steps, 4 * u + 2)
                    nc.vector.tensor_tensor(pr[:, k, :, :], pr[:, k, :, :], red[:, k, 0, :].unsqueeze(2).broadcast_to([P, G, P]),
                                            ALU.subtract).then_inc(steps, 1)
                    dve.wait_ge(exp_ready, u + 1)
                    nc.vector.reduce_sum(red[:, k, 1, :], pr[:, k, :, :], AXIS.X).then_inc(steps, 1)
                    dve.wait_ge(steps, 4 * u + 4)
                    nc.vector.reciprocal(red[:, k, 2, :], red[:, k, 1, :]).then_inc(inv_ready, 1)
                    dve.wait_ge(inv_ready, u + 1)
                    nc.vector.tensor_tensor(pr[:, k, :, :], pr[:, k, :, :], red[:, k, 2, :].unsqueeze(2).broadcast_to([P, G, P]),
                                            ALU.mult).then_inc(norm_ready, 1)
                    if u >= NG + 2 and (u - 2) % NG == 0:
                        add(dve, (u - 2) // NG - 1)
                add(dve, TT - 1)


FREQ = 2 * S


def transforms():
    l = np.arange(S)[:, None]
    re = np.arange(S + 1)
    im = np.arange(1, S)
    ang = lambda k: 2 * np.pi * ((l * k) % FREQ) / FREQ
    spec = np.concatenate([np.cos(ang(re)), -np.sin(ang(im))], 1)
    swapped = np.concatenate([-np.sin(ang(re)), np.cos(ang(im))], 1)
    k_re = np.concatenate([np.cos(ang(re)), np.cos(ang(im))], 1)
    k_im = np.concatenate([np.sin(ang(re)), -np.sin(ang(im))], 1)
    weight = np.where((re == 0) | (re == S), 1.0, 2.0) / FREQ
    inverse = np.concatenate([np.cos(ang(re)) * weight, -np.sin(ang(im)) * 2.0 / FREQ], 1).T
    return {"dft_x": np.stack([spec, swapped]).astype(np.float32),
            "dft_k": np.stack([k_re, k_im]).astype(np.float32),
            "dft_inverse": inverse.astype(np.float32)}


def state_space_kernel(core, spec_k, ident, w):
    nc = core.nc
    N = 64
    M = KC * N
    STEP = 8
    R = S // STEP
    mult = [b for b in range(STEP)] + [STEP * a for a in range(R)]
    PI2_HI = 6.28125
    PI2_LO = 2 * PI - PI2_HI
    ROUND = 1.5 * 2 ** 23
    ANGLES_DONE, U_DONE = 42, 69
    TOP = float(np.nextafter(np.float32(PI), np.float32(0)))
    with ExitStack() as ctx:
        par = core.sb(ctx, "k_par", [P, 4, M])
        dt = core.sb(ctx, "k_dt", [P, KC])
        dta = core.sb(ctx, "k_dta", [P, 2, M])
        ang = core.sb(ctx, "k_ang", [P, 16, M])
        turns = core.sb(ctx, "k_turns", [P, 16, M])
        mag = core.sb(ctx, "k_mag", [P, 16, M])
        pw = core.sb(ctx, "k_pw", [P, 2, 16, M])
        sm = core.sb(ctx, "k_sm", [P, 10, M])
        u = core.sb(ctx, "k_u", [P, 2, R, M])
        prod = core.sb(ctx, "k_prod", [P, 2, R, STEP, N])
        k = core.sb(ctx, "k_k", [P, KC, S])
        kt = core.sb(ctx, "k_kt", [S, D])
        dft = core.sb(ctx, "k_dft", [S, 2, FREQ])
        t_ps = core.pb(ctx, "k_t_ps", [P, 512])
        f_ps = core.pb(ctx, "k_f_ps", [P, 2, 512])
        p_in, dt_ready, steps, act_steps, im_ready, k_ready, t_ready, kt_ready, f_ready = core.sems(
            ctx, "k", "p_in dt_ready steps act_steps im_ready k_ready t_ready kt_ready f_ready")
        def factors(part, c):
            ua = u[:, part, :, c * N:(c + 1) * N].unsqueeze(2).broadcast_to([P, R, STEP, N])
            wb = pw[:, part, 0:STEP, c * N:(c + 1) * N].unsqueeze(1).broadcast_to([P, R, STEP, N])
            return ua, wb

        with nc.Block() as block:
            @block.sync
            def _(sp):
                sp.dma_start(dt[:, :], w["L1_xattn_log_dt"]).then_inc(p_in, 16)
                for n, name in enumerate(("A_re", "A_im", "C_re", "C_im")):
                    sp.dma_start(par[:, n, :].rearrange("p (c n) -> p c n", c=KC),
                                 w[f"L1_xattn_{name}"].rearrange("(c p) n -> p c n", p=P)).then_inc(p_in, 16)
                sp.dma_start(dft[:, :, :], w["dft_k"].rearrange("a l f -> l a f")).then_inc(p_in, 16)

            @block.scalar
            def _(act):
                act.wait_ge(p_in, 96)
                nc.scalar.activation(dt[:, :], dt[:, :], ACT.Exp).then_inc(dt_ready, 1)
                act.wait_ge(steps, 2 + 16)
                nc.scalar.activation(mag[:, :, :], mag[:, :, :], ACT.Exp).then_inc(act_steps, 1)
                act.wait_ge(steps, ANGLES_DONE)
                nc.scalar.activation(pw[:, 1, :, :], ang[:, :, :], ACT.Sin).then_inc(act_steps, 1)
                nc.scalar.activation(pw[:, 0, :, :], turns[:, :, :], ACT.Sin).then_inc(act_steps, 1)
                act.wait_ge(f_ready, 1)
                nc.scalar.copy(spec_k[:, :, :], f_ps[:, :, :])

            @block.vector
            def _(dve):
                done = [0]

                def step(instruction):
                    done[0] += 1
                    instruction.then_inc(steps, 1)

                def sync():
                    dve.wait_ge(steps, done[0])

                V = nc.vector
                dve.wait_ge(dt_ready, 1)
                for a in range(2):
                    step(V.tensor_tensor(dta[:, a, :].rearrange("p (c n) -> p c n", c=KC), par[:, a, :].rearrange("p (c n) -> p c n", c=KC),
                                         dt[:, :].unsqueeze(2).broadcast_to([P, KC, N]), ALU.mult))
                sync()
                for m, f in enumerate(mult):
                    step(V.tensor_scalar(mag[:, m, :], dta[:, 0, :], float(f), None, ALU.mult))
                for m, f in enumerate(mult):
                    step(V.tensor_scalar(ang[:, m, :], dta[:, 1, :], float(f), None, ALU.mult))
                sync()
                step(V.tensor_scalar(turns[:, :, :], ang[:, :, :], 1 / (2 * PI), ROUND, ALU.mult, ALU.add))
                sync()
                step(V.tensor_scalar(turns[:, :, :], turns[:, :, :], ROUND, None, ALU.subtract))
                sync()
                step(V.scalar_tensor_tensor(ang[:, :, :], turns[:, :, :], -PI2_HI, ang[:, :, :], ALU.mult, ALU.add))
                sync()
                step(V.scalar_tensor_tensor(ang[:, :, :], turns[:, :, :], -PI2_LO, ang[:, :, :], ALU.mult, ALU.add))
                sync()
                step(V.tensor_scalar(turns[:, :, :], ang[:, :, :], PI / 2, -2 * PI, ALU.is_gt, ALU.mult))
                sync()
                step(V.scalar_tensor_tensor(turns[:, :, :], ang[:, :, :], PI / 2, turns[:, :, :], ALU.add, ALU.add))
                sync()
                step(V.tensor_scalar(turns[:, :, :], turns[:, :, :], TOP, -TOP, ALU.min, ALU.max))
                step(V.tensor_scalar(ang[:, :, :], ang[:, :, :], TOP, -TOP, ALU.min, ALU.max))
                assert done[0] == ANGLES_DONE
                dve.wait_ge(act_steps, 3)
                for a in range(2):
                    step(V.tensor_tensor(pw[:, a, :, :], pw[:, a, :, :], mag[:, :, :], ALU.mult))
                sync()
                are, aim, cre, cim = (par[:, n, :] for n in range(4))
                er, ei = sm[:, 0, :], pw[:, 1, 1, :]
                step(V.tensor_scalar(er, pw[:, 0, 1, :], -1.0, None, ALU.add))
                sync()
                step(V.tensor_tensor(sm[:, 1, :], cre, er, ALU.mult))
                step(V.tensor_tensor(sm[:, 2, :], cim, ei, ALU.mult))
                step(V.tensor_tensor(sm[:, 3, :], cre, ei, ALU.mult))
                step(V.tensor_tensor(sm[:, 4, :], cim, er, ALU.mult))
                step(V.tensor_tensor(sm[:, 5, :], are, are, ALU.mult))
                step(V.tensor_tensor(sm[:, 6, :], aim, aim, ALU.mult))
                sync()
                step(V.tensor_tensor(sm[:, 1, :], sm[:, 1, :], sm[:, 2, :], ALU.subtract))
                step(V.tensor_tensor(sm[:, 3, :], sm[:, 3, :], sm[:, 4, :], ALU.add))
                step(V.tensor_tensor(sm[:, 5, :], sm[:, 5, :], sm[:, 6, :], ALU.add))
                sync()
                step(V.reciprocal(sm[:, 5, :], sm[:, 5, :]))
                step(V.tensor_tensor(sm[:, 6, :], sm[:, 1, :], are, ALU.mult))
                step(V.tensor_tensor(sm[:, 7, :], sm[:, 3, :], aim, ALU.mult))
                step(V.tensor_tensor(sm[:, 8, :], sm[:, 3, :], are, ALU.mult))
                step(V.tensor_tensor(sm[:, 9, :], sm[:, 1, :], aim, ALU.mult))
                sync()
                step(V.tensor_tensor(sm[:, 6, :], sm[:, 6, :], sm[:, 7, :], ALU.add))
                step(V.tensor_tensor(sm[:, 8, :], sm[:, 8, :], sm[:, 9, :], ALU.subtract))
                sync()
                for n in (6, 8):
                    step(V.scalar_tensor_tensor(sm[:, n, :], sm[:, n, :], 2.0, sm[:, 5, :], ALU.mult, ALU.mult))
                sync()
                dr, di = (sm[:, n, :].unsqueeze(1).broadcast_to([P, R, M]) for n in (6, 8))
                pr8, pi8 = pw[:, 0, STEP:16, :], pw[:, 1, STEP:16, :]
                t0, t1 = mag[:, 0:R, :], mag[:, R:2 * R, :]
                step(V.tensor_tensor(u[:, 0, :, :], dr, pr8, ALU.mult))
                step(V.tensor_tensor(t0, di, pi8, ALU.mult))
                step(V.tensor_tensor(u[:, 1, :, :], dr, pi8, ALU.mult))
                step(V.tensor_tensor(t1, di, pr8, ALU.mult))
                sync()
                step(V.tensor_tensor(u[:, 0, :, :], u[:, 0, :, :], t0, ALU.subtract))
                step(V.scalar_tensor_tensor(u[:, 1, :, :], u[:, 1, :, :], -1.0, t1, ALU.mult, ALU.subtract))
                sync()
                assert done[0] == U_DONE
                for c in range(KC):
                    ur, wr = factors(0, c)
                    if c:
                        dve.wait_ge(k_ready, c)
                    step(V.tensor_tensor(prod[:, 0, :, :, :], ur, wr, ALU.mult))
                    sync()
                    dve.wait_ge(im_ready, 2 * c + 2)
                    V.reduce_sum(k[:, c, :].rearrange("p (a b) -> p a b", a=R), prod[:, 0, :, :, :], AXIS.X).then_inc(k_ready, 1)
                dve.wait_ge(t_ready, 1)
                V.tensor_copy(kt[:, :], t_ps[0:S, :]).then_inc(kt_ready, 1)

            @block.gpsimd
            def _(pool):
                for c in range(KC):
                    ui, wi = factors(1, c)
                    pool.wait_ge(steps, U_DONE + c)
                    pool.wait_ge(k_ready, c)
                    nc.gpsimd.tensor_tensor(prod[:, 1, :, :, :], ui, wi, ALU.mult).then_inc(im_ready, 1)
                    pool.wait_ge(im_ready, 2 * c + 1)
                    pool.wait_ge(steps, U_DONE + c + 1)
                    nc.gpsimd.tensor_tensor(prod[:, 0, :, :, :], prod[:, 0, :, :, :], prod[:, 1, :, :, :], ALU.add).then_inc(im_ready, 1)

            @block.tensor
            def _(pe):
                pe.wait_ge(k_ready, KC)
                for c in range(KC):
                    last = nc.tensor.transpose(t_ps[0:S, c * P:(c + 1) * P], k[:, c, :], ident[:, :])
                last.then_inc(t_ready, 1)
                pe.wait_ge(kt_ready, 1)
                for a in range(2):
                    last = nc.tensor.matmul(f_ps[:, a, :], dft[:, a, :], kt[:, :], start=True, stop=True)
                last.then_inc(f_ready, 1)


def cross_attention_L1(core, x, xn, xt, ident, w):
    with ExitStack() as ctx:
        ct = core.sb(ctx, "x1_ct", [P, CC, TOK])
        top_attention(core, xt, ct, ident, w)
        spec_k = core.sb(ctx, "x1_spec_k", [P, 2, D])
        state_space_kernel(core, spec_k, ident, w)
        mixing(core, x, xn, xt, ct, spec_k, ident, w)


def top_attention(core, xt, ct, ident, w):
    nc = core.nc
    H, DH, TOP = 4, 32, 32
    HALVES = H // 2
    ROUNDS = B // PAIR
    FAR, TAKEN = -2e38, -3e38
    with ExitStack() as ctx:
        qp = core.sb(ctx, "x1_qp", [P, CC, H, TOK])
        with ExitStack() as c2:
            wq = core.sb(c2, "x1_wq", [P, KC, H * DH])
            wkt = core.sb(c2, "x1_wkt", [P, CD])
            qt = core.sb(c2, "x1_qt", [P, TOK])
            ps = core.pb(c2, "x1_ps", [P, 8, 512])
            w_in, q_ready, qt_ready, qp_ready, qp_used = core.sems(c2, "x1", "w_in q_ready qt_ready qp_ready qp_used")
            with nc.Block() as block:
                @block.sync
                def _(sp):
                    sp.dma_start(wq[:, :, :], w["L1_xattn_Wq"].rearrange("(c p) n -> p c n", p=P)).then_inc(w_in, 16)
                    sp.dma_start(wkt[:, :], w["L1_xattn_WkT"]).then_inc(w_in, 16)

                @block.tensor
                def _(pe):
                    pe.wait_ge(w_in, 32)
                    for c in range(KC):
                        last = nc.tensor.matmul(ps[:, 0, :], wq[:, c, :], xt[:, c, :], start=(c == 0), stop=(c == KC - 1))
                    last.then_inc(q_ready, 1)
                    pe.wait_ge(qt_ready, 1)
                    for n in range(H * CC):
                        h, c = n // CC, n % CC
                        if n >= 4:
                            pe.wait_ge(qp_used, n - 3)
                        nc.tensor.matmul(ps[:, 4 + n % 4, :], wkt[h * DH:(h + 1) * DH, c * P:(c + 1) * P],
                                         qt[h * DH:(h + 1) * DH, :], start=True, stop=True).then_inc(qp_ready, 1)

                @block.scalar
                def _(act):
                    act.wait_ge(q_ready, 1)
                    nc.scalar.mul(qt[:, :], ps[:, 0, :], DH ** -0.5).then_inc(qt_ready, 1)
                    for n in range(H * CC):
                        act.wait_ge(qp_ready, n + 1)
                        nc.scalar.copy(qp[:, n % CC, n // CC, :], ps[:, 4 + n % 4, :]).then_inc(qp_used, 1)

        cx = core.sb(ctx, "x1_cx", [P, PAIR, KT, CD])
        cxt = core.sb(ctx, "x1_cxt", [P, PAIR, CC, CTX])
        mask8 = core.sb(ctx, "x1_mask8", [P, CTX], U8)
        mask = core.sb(ctx, "x1_mask", [P, CTX])
        qs = core.sb(ctx, "x1_qs", [P, HALVES, CC, P])
        sc = core.sb(ctx, "x1_sc", [P, PAIR, HALVES, CTX])
        left = core.sb(ctx, "x1_left", [P, HALVES, CTX])
        best = core.sb(ctx, "x1_best", [P, HALVES, TOP])
        red = core.sb(ctx, "x1_red", [P, HALVES, 3])
        two = core.sb(ctx, "x1_two", [P, S])
        mean = core.sb(ctx, "x1_mean", [P, HALVES, S])
        at = core.sb(ctx, "x1_at", [P, KT, S])
        s_ps = core.pb(ctx, "x1_s_ps", [P, 4 * 512])
        a_ps = core.pb(ctx, "x1_a_ps", [P, 2 * 512])
        c_ps = core.pb(ctx, "x1_c_ps", [P, 512])
        cx_in0, cx_in1, cxt_in0, cxt_in1, m_in, two_in, mask_ready, qs_ready, s_ready, sc_copied, sc_ready, steps, \
            chosen, inv_ready, e_ready, p_ready, mean_ready, a_ready, at_ready, c_ready, ct_ready = core.sems(
                ctx, "x1", "cx_in0 cx_in1 cxt_in0 cxt_in1 m_in two_in mask_ready qs_ready s_ready sc_copied sc_ready steps "
                "chosen inv_ready e_ready p_ready mean_ready a_ready at_ready c_ready ct_ready")
        cx_in, cxt_in = (cx_in0, cx_in1), (cxt_in0, cxt_in1)
        PICKS = TOP // 8

        def batches(engine, first, body):
            if first:
                first()
            with engine.Fori(0, ROUNDS - 1) as i:
                body(i, 0, (i, 1))
                body(i, 1, (i + 1, 0))
            body(ROUNDS - 1, 0, (ROUNDS - 1, 1))
            body(ROUNDS - 1, 1, None)

        with nc.Block() as block:
            @block.sync
            def _(sp):
                sp.dma_start(two[:, :], w["two_eyes"]).then_inc(two_in, 16)

                def load(b, j, i):
                    if i is not None or j:
                        sp.wait_ge(mask_ready, i * PAIR + (PAIR + j) if i is not None else j)
                    sp.dma_start(mask8[:, :], w["mask_ctx"][bass.ds(b, 1), :].broadcast_to([P, CTX])).then_inc(m_in, 16)
                    if i is not None:
                        sp.wait_ge(s_ready, i * (PAIR * HALVES) + (j + 1) * HALVES)
                    sp.dma_start(cxt[:, j, :, :],
                                 w["ctxT"][bass.ds(b, 1), :, :].rearrange("b (c p) n -> p (b c) n", p=P)).then_inc(cxt_in[j], 16)
                    if i is not None:
                        sp.wait_ge(c_ready, i * PAIR + (j + 1 + PRIMED))
                    sp.dma_start(cx[:, j, 0:KT - 1, :],
                                 w["ctx"][bass.ds(b, 1), 0:(KT - 1) * P, :].rearrange("b (t p) n -> p (b t) n", p=P)
                                 ).then_inc(cx_in[j], 16)
                    sp.dma_start(cx[0:LAST, j, KT - 1, :],
                                 w["ctx"][bass.ds(b, 1), (KT - 1) * P:CTX, :].rearrange("b p n -> (b p) n")
                                 ).then_inc(cx_in[j], 16)

                for j in range(PAIR):
                    load(j, j, None)
                with sp.Fori(0, ROUNDS - 1) as i:
                    for j in range(PAIR):
                        load((i + 1) * PAIR + j, j, i)

            @block.tensor
            def _(pe):
                core.prime(pe, c_ready, a_ready)

                def scores(i, j, r, very_first=False):
                    unit = (i * PAIR + j) * HALVES + r
                    pe.wait_ge(qs_ready, unit + 1)
                    if r == 0:
                        pe.wait_ge(cxt_in[j], (i + 1) * 16)
                    if not very_first:
                        pe.wait_ge(sc_copied, unit)
                    for n in range(4):
                        a, b = 512 * n, min(512 * n + 512, CTX)
                        for c in range(CC):
                            last = nc.tensor.matmul(s_ps[:, a:b], qs[:, r, c, :], cxt[:, j, c, a:b],
                                                    start=(c == 0), stop=(c == CC - 1))
                    last.then_inc(s_ready, 1)

                def mean_attention(i, j):
                    b = i * PAIR + j
                    pe.wait_ge(p_ready, (b + 1) * HALVES)
                    pe.wait_ge(mean_ready, (b + 1) * HALVES)
                    pe.wait_ge(at_ready, b * 3 + PRIMED)
                    for t in range(KT):
                        rows = P if t < KT - 1 else LAST
                        for r in range(HALVES):
                            last = nc.tensor.matmul(a_ps[0:rows, t * S:(t + 1) * S], sc[:, j, r, t * P:t * P + rows], mean[:, r, :],
                                                    start=(r == 0), stop=(r == HALVES - 1))
                    last.then_inc(a_ready, 1)

                def weigh(i, j):
                    b = i * PAIR + j
                    pe.wait_ge(at_ready, (b + 1) * 3 + PRIMED)
                    pe.wait_ge(cx_in[j], (i + 1) * 32)
                    pe.wait_ge(ct_ready, b + PRIMED)
                    for c in range(CC):
                        for t in range(KT):
                            rows = P if t < KT - 1 else LAST
                            last = nc.tensor.matmul(c_ps[:, c * S:(c + 1) * S], cx[0:rows, j, t, c * P:(c + 1) * P], at[0:rows, t, :],
                                                    start=(t == 0), stop=(t == KT - 1))
                    last.then_inc(c_ready, 1)

                def first():
                    for r in range(HALVES):
                        scores(0, 0, r, very_first=(r == 0))

                def body(i, j, following):
                    if following:
                        for r in range(HALVES):
                            scores(*following, r)
                    mean_attention(i, j)
                    weigh(i, j)

                batches(pe, first, body)

            @block.scalar
            def _(act):
                core.prime(act, at_ready, ct_ready)

                def spread_mask(i, j, very_first=False):
                    b = i * PAIR + j
                    act.wait_ge(m_in, (b + 1) * 16)
                    if not very_first:
                        act.wait_ge(sc_ready, b * HALVES)
                    nc.scalar.activation(mask[:, :], mask8[:, :], ACT.Copy, bias=NEG, scale=-NEG).then_inc(mask_ready, 1)

                def copy_scores(i, j, r, very_first=False):
                    b = i * PAIR + j
                    act.wait_ge(s_ready, b * HALVES + r + 1)
                    if not very_first:
                        act.wait_ge(a_ready, b - 1 + PRIMED)
                    nc.scalar.copy(sc[:, j, r, :], s_ps[:, 0:CTX]).then_inc(sc_copied, 1)

                def exponent(i, j, r):
                    act.wait_ge(chosen, (i * PAIR + j) * HALVES + r + 1)
                    nc.scalar.activation(sc[:, j, r, :], sc[:, j, r, :], ACT.Exp, bias=red[:, r, 0:1]).then_inc(e_ready, 1)

                def copy_out(i, j):
                    b = i * PAIR + j
                    act.wait_ge(a_ready, b + 1 + PRIMED)
                    act.wait_ge(c_ready, b + PRIMED)
                    for lo, hi, rows in ((0, 8, P), (8, KT - 1, P), (KT - 1, KT, LAST)):
                        nc.scalar.copy(at[0:rows, lo:hi, :], a_ps[0:rows, lo * S:hi * S].rearrange("p (t n) -> p t n", n=S)).then_inc(at_ready, 1)
                    act.wait_ge(c_ready, b + 1 + PRIMED)
                    nc.scalar.copy(ct[:, :, bass.ds(b * S, S)],
                                   c_ps[:, 0:CC * S].rearrange("p (c n) -> p c n", n=S)).then_inc(ct_ready, 1)

                def first():
                    spread_mask(0, 0, very_first=True)
                    for r in range(HALVES):
                        copy_scores(0, 0, r, very_first=True)

                def body(i, j, following):
                    if following:
                        spread_mask(*following)
                    for r in range(HALVES):
                        exponent(i, j, r)
                        if following:
                            copy_scores(*following, r)
                    copy_out(i, j)

                batches(act, first, body)

            @block.gpsimd
            def _(pool):
                def prepare(i, j, very_first=False):
                    b = i * PAIR + j
                    for r in range(HALVES):
                        if not very_first:
                            pool.wait_ge(s_ready, (b - 1) * HALVES + r + 1)
                        nc.gpsimd.tensor_copy(qs[:, r, :, :].rearrange("p c (h s) -> p c h s", h=2),
                                              qp[:, :, 2 * r:2 * r + 2, bass.ds(b * S, S)]).then_inc(qs_ready, 1)
                    pool.wait_ge(mask_ready, b + 1)
                    for r in range(HALVES):
                        pool.wait_ge(sc_copied, b * HALVES + r + 1)
                        nc.gpsimd.tensor_tensor(sc[:, j, r, :], sc[:, j, r, :], mask[:, :], ALU.add).then_inc(sc_ready, 1)

                batches(pool, lambda: prepare(0, 0, very_first=True),
                        lambda i, j, following: prepare(*following) if following else None)

            @block.vector
            def _(dve):
                V = nc.vector

                def body(i, j, following):
                    for r in range(HALVES):
                        unit = (i * PAIR + j) * HALVES + r
                        done = [0]

                        def step(instruction):
                            done[0] += 1
                            instruction.then_inc(steps, 1)
                            dve.wait_ge(steps, done[0])

                        dve.wait_ge(sc_ready, unit + 1)
                        step(V.memset(red[:, r, 1:2], 0.0))
                        for n in range(PICKS):
                            source = sc[:, j, r, :] if n == 0 else left[:, r, :]
                            step(V.max(best[:, r, 8 * n:8 * n + 8], source))
                            step(V.match_replace(left[:, r, :], best[:, r, 8 * n:8 * n + 8], source, TAKEN))
                            if n == 0:
                                V.tensor_scalar(red[:, r, 0:1], best[:, r, 0:1], -1.0, None, ALU.mult).then_inc(chosen, 1)
                        dve.sem_clear(steps)
                        dve.wait_ge(e_ready, unit + 1)
                        V.scalar_tensor_tensor(sc[:, j, r, :], left[:, r, :], FAR, sc[:, j, r, :], ALU.is_le, ALU.mult,
                                               accum_out=red[:, r, 1:2]).then_inc(p_ready, 1)
                        dve.wait_ge(p_ready, unit + 1)
                        V.reciprocal(red[:, r, 2:3], red[:, r, 1:2]).then_inc(inv_ready, 1)
                        dve.wait_ge(a_ready, i * PAIR + j + PRIMED)
                        dve.wait_ge(inv_ready, unit + 1)
                        V.tensor_scalar(mean[:, r, :], two[:, :], red[:, r, 2:3], 1.0 / H, ALU.mult, ALU.mult).then_inc(mean_ready, 1)

                dve.wait_ge(two_in, 16)
                batches(dve, None, body)


def mixing(core, x, xn, xt, ct, spec_k, ident, w):
    nc = core.nc
    FC = 2048 // P
    with ExitStack() as ctx:
        y = core.sb(ctx, "mx_y", [P, TT, D])
        film = core.sb(ctx, "mx_film", [P, TT, 2 * D])
        with ExitStack() as c2:
            wv = core.sb(c2, "mx_wv", [P, CC, D])
            wf = core.sb(c2, "mx_wf", [P, 2, KC, 2 * D])
            bf = core.sb(c2, "mx_bf", [P, 2, 2 * D])
            tm8 = core.sb(c2, "mx_tm8", [P, TOK], U8)
            tm = core.sb(c2, "mx_tm", [P, TOK])
            c_t = core.sb(c2, "mx_c_t", [P, KC, TOK])
            film_in = core.sb(c2, "mx_film_in", [P, TT, 2 * D])
            mg = core.sb(c2, "mx_mg", [P, 1])
            rows = core.sb(c2, "mx_rows", [P, 3, D])
            dft = core.sb(c2, "mx_dft", [P, 2, FREQ])
            inverse = core.sb(c2, "mx_inverse", [P, S])
            xs = core.sb(c2, "mx_xs", [P, TT, D])
            films = (film_in, film)
            with ExitStack() as c3:
                ps = core.pb(c3, "mx_ps", [P, 8, 512])
                c_in, f_in, tm_ready, v_ready, ct_ready, f_ready, f_used, g_steps = core.sems(
                    c3, "mx", "c_in f_in tm_ready v_ready ct_ready f_ready f_used g_steps")
                with nc.Block() as block:
                    @block.sync
                    def _(sp):
                        sp.dma_start(wv[:, :, :], w["L1_xattn_Wv"].rearrange("(c p) n -> p c n", p=P)).then_inc(c_in, 16)
                        sp.dma_start(tm8[:, :], w["mask_x"].broadcast_to([P, TOK])).then_inc(c_in, 16)
                        for a, k in enumerate(("in", "out")):
                            sp.dma_start(wf[:, a, :, :], w[f"L1_xattn_W_film_{k}"].rearrange("(c p) n -> p c n", p=P)).then_inc(f_in, 16)
                            sp.dma_start(bf[:, a, :], bcast(w[f"L1_xattn_b_film_{k}"])).then_inc(f_in, 16)
                        sp.dma_start(mg[:, :], w["L1_xattn_mod_gate"].broadcast_to([P, 1])).then_inc(f_in, 16)
                        for n, k in enumerate(("g_norm_in", "b_norm_in", "D_skip")):
                            sp.dma_start(rows[:, n, :], bcast(w[f"L1_xattn_{k}"])).then_inc(f_in, 16)
                        for half in range(2):
                            sp.dma_start(dft[half * S:(half + 1) * S, :, :], w["dft_x"].rearrange("a l f -> l a f")).then_inc(f_in, 16)
                        sp.dma_start(inverse[:, :], w["dft_inverse"]).then_inc(f_in, 16)
                        sp.wait_ge(f_in, 11 * 16)

                    @block.tensor
                    def _(pe):
                        pe.wait_ge(c_in, 32)
                        for m in range(KC):
                            for c in range(CC):
                                last = nc.tensor.matmul(ps[:, m, :], wv[:, c, m * P:(m + 1) * P], ct[:, c, :],
                                                        start=(c == 0), stop=(c == CC - 1))
                            last.then_inc(v_ready, 1)
                        pe.wait_ge(ct_ready, KC)
                        pe.wait_ge(f_in, 11 * 16)
                        for n in range(4 * TT):
                            t, a, half = n // 4, n // 2 % 2, n % 2
                            if n >= 4:
                                pe.wait_ge(f_used, n - 3)
                            for c in range(KC):
                                last = nc.tensor.matmul(ps[:, 4 + n % 4, :], c_t[:, c, t * P:(t + 1) * P],
                                                        wf[:, a, c, half * D:(half + 1) * D], start=(c == 0), stop=(c == KC - 1))
                            last.then_inc(f_ready, 1)

                    @block.gpsimd
                    def _(pool):
                        pool.wait_ge(c_in, 32)
                        nc.gpsimd.tensor_copy(tm[:, :], tm8[:, :]).then_inc(tm_ready, 1)

                    @block.vector
                    def _(dve):
                        V = nc.vector
                        dve.wait_ge(tm_ready, 1)
                        for m in range(KC):
                            dve.wait_ge(v_ready, m + 1)
                            V.tensor_tensor(c_t[:, m, :], ps[:, m, :], tm[:, :], ALU.mult).then_inc(ct_ready, 1)
                        dve.wait_ge(f_in, 11 * 16)
                        for n in range(4 * TT):
                            t, a, half = n // 4, n // 2 % 2, n % 2
                            dve.wait_ge(f_ready, n + 1)
                            V.tensor_tensor(films[a][:, t, half * D:(half + 1) * D], ps[:, 4 + n % 4, :],
                                            bf[:, a, half * D:(half + 1) * D], ALU.add).then_inc(f_used, 1)
                        dve.wait_ge(f_used, 4 * TT)
                        for a in range(2):
                            V.tensor_scalar(films[a][:, :, 0:D], films[a][:, :, 0:D], mg[:, 0:1], 1.0, ALU.mult, ALU.add)
                            V.tensor_scalar(films[a][:, :, D:2 * D], films[a][:, :, D:2 * D], mg[:, 0:1], None, ALU.mult)

            norm_stage(core, "n4", xn, xs, None, ident, gamma=rows[:, 0, :], beta=rows[:, 1, :])
            with ExitStack() as c3:
                spec = core.sb(c3, "mx_spec", [P, 2, 2, D])
                skip = core.sb(c3, "mx_skip", [P, TT, D])
                ps = core.pb(c3, "mx_ps2", [P, 8, 512])
                xs_ready, sp_ready, spec_ready, y_ready, skip_ready, s_first, s_last = core.sems(
                    c3, "mx", "xs_ready sp_ready spec_ready y_ready skip_ready s_first s_last")
                with nc.Block() as block:
                    @block.tensor
                    def _(pe):
                        def forward(b):
                            lo, t, k = (b % 2) * S, b // 2, b % 2
                            pe.wait_ge(xs_ready, t + 1)
                            if b >= 2:
                                pe.wait_ge(spec_ready, 2 * (b - 1))
                            for a in range(2):
                                last = nc.tensor.matmul(ps[:, 2 * k + a, :], dft[lo:lo + S, a, :], xs[lo:lo + S, t, :],
                                                        start=True, stop=True)
                            last.then_inc(sp_ready, 1)

                        forward(0)
                        for b in range(B):
                            lo, t, k = (b % 2) * S, b // 2, b % 2
                            if b + 1 < B:
                                forward(b + 1)
                            pe.wait_ge(spec_ready, 2 * (b + 1))
                            for a in range(2):
                                last = nc.tensor.matmul(ps[lo:lo + S, 4 + t, :], inverse[:, :], spec[:, k, a, :],
                                                        start=(a == 0), stop=(a == 1))
                            last.then_inc(y_ready, 1)

                    @block.gpsimd
                    def _(pool):
                        for t in range(TT):
                            pool.wait_ge(xs_ready, t + 1)
                            nc.gpsimd.tensor_tensor(skip[:, t, :], xs[:, t, :], rows[:, 2, :], ALU.mult).then_inc(skip_ready, 1)

                    @block.vector
                    def _(dve):
                        V = nc.vector
                        for t in range(TT):
                            V.tensor_tensor(xs[:, t, :], xs[:, t, :], film_in[:, t, 0:D], ALU.mult).then_inc(s_first, 1)
                        for t in range(TT):
                            dve.wait_ge(s_first, t + 1)
                            V.tensor_tensor(xs[:, t, :], xs[:, t, :], film_in[:, t, D:2 * D], ALU.add).then_inc(xs_ready, 1)
                        for b in range(B):
                            k = b % 2
                            dve.wait_ge(sp_ready, b + 1)
                            if b >= 2:
                                dve.wait_ge(y_ready, b - 1)
                            for a in range(2):
                                V.tensor_tensor(spec[:, k, a, :], ps[:, 2 * k + a, :], spec_k[:, a, :], ALU.mult).then_inc(spec_ready, 1)
                        dve.wait_ge(skip_ready, TT)
                        for t in range(TT):
                            dve.wait_ge(y_ready, 2 * t + 2)
                            V.tensor_tensor(y[:, t, :], ps[:, 4 + t, :], skip[:, t, :], ALU.add).then_inc(s_last, 1)
                        for n, (other, op) in enumerate(((film[:, :, 0:D], ALU.mult), (film[:, :, D:2 * D], ALU.add), (xn[:, :, :], ALU.add))):
                            for t in range(TT):
                                dve.wait_ge(s_last, n * TT + t + 1)
                                V.tensor_tensor(y[:, t, :], y[:, t, :], other[:, t, :], op).then_inc(s_last, 1)

        with ExitStack() as c2:
            rows = core.sb(c2, "ff_rows", [P, 5, D])
            w1 = core.sb(c2, "ff_w1", [P, KC, 2048])
            w2 = core.sb(c2, "ff_w2", [P, FC, D])
            b1 = core.sb(c2, "ff_b1", [P, FC])
            h = core.sb(c2, "ff_h", [P, 2, TOK])
            r_in, w1_in, w2_in, up_ready, h_ready, down_ready, b_ready = core.sems(
                c2, "ff", "r_in w1_in w2_in up_ready h_ready down_ready b_ready")
            with nc.Block() as block:
                @block.sync
                def _(sp):
                    for n, k in enumerate(("g_ffn", "b_ffn", "g_norm_out", "b_norm_out", "b2")):
                        sp.dma_start(rows[:, n, :], bcast(w[f"L1_xattn_{k}"])).then_inc(r_in, 16)
                    sp.dma_start(w1[:, :, :], w["L1_xattn_W1"].rearrange("(c p) n -> p c n", p=P)).then_inc(w1_in, 16)
                    sp.dma_start(b1[:, :], w["L1_xattn_b1"]).then_inc(w1_in, 16)
                    sp.dma_start(w2[:, :, :], w["L1_xattn_W2"].rearrange("(c p) n -> p c n", p=P)).then_inc(w2_in, 16)
                    sp.wait_ge(r_in, 80)

            norm_stage(core, "n5", y, xn, xt, ident, gamma=rows[:, 0, :], beta=rows[:, 1, :])
            with ExitStack() as c3:
                u_ps = core.pb(c3, "ff_u_ps", [P, 2, 512])
                a_ps = core.pb(c3, "ff_a_ps", [P, TT, 512])
                with nc.Block() as block:
                    @block.tensor
                    def _(pe):
                        def up(n):
                            if n >= 2:
                                pe.wait_ge(h_ready, n - 1)
                            for c in range(KC):
                                last = nc.tensor.matmul(u_ps[:, n % 2, :], w1[:, c, n * P:(n + 1) * P], xt[:, c, :],
                                                        start=(c == 0), stop=(c == KC - 1))
                            last.then_inc(up_ready, 1)

                        pe.wait_ge(w1_in, 32)
                        pe.wait_ge(w2_in, 16)
                        up(0)
                        for n in range(FC):
                            if n + 1 < FC:
                                up(n + 1)
                            pe.wait_ge(h_ready, n + 1)
                            for t in range(TT):
                                last = nc.tensor.matmul(a_ps[:, t, :], h[:, n % 2, t * P:(t + 1) * P], w2[:, n, :],
                                                        start=(n == 0), stop=(n == FC - 1))
                            last.then_inc(down_ready, 1)

                    @block.scalar
                    def _(act):
                        act.wait_ge(w1_in, 32)
                        for n in range(FC):
                            act.wait_ge(up_ready, n + 1)
                            if n >= 2:
                                act.wait_ge(down_ready, n - 1)
                            nc.scalar.activation(h[:, n % 2, :], u_ps[:, n % 2, :], ACT.Gelu, bias=b1[:, n:n + 1]).then_inc(h_ready, 1)

                    @block.vector
                    def _(dve):
                        for t in range(TT):
                            nc.vector.tensor_tensor(y[:, t, :], y[:, t, :], rows[:, 4, :], ALU.add).then_inc(b_ready, 1)
                        dve.wait_ge(down_ready, FC)
                        for t in range(TT):
                            dve.wait_ge(b_ready, t + 1)
                            nc.vector.tensor_tensor(y[:, t, :], y[:, t, :], a_ps[:, t, :], ALU.add)
            norm_stage(core, "n7", y, xn, None, ident, gamma=rows[:, 2, :], beta=rows[:, 3, :], out=x)


def build_program(nc, w, out, start=0, upto=99):
    with ExitStack() as ctx:
        core = Core(nc, ctx)
        x = core.sb(ctx, "x", [P, TT, D])
        xn = core.sb(ctx, "xn", [P, TT, D])
        xt = core.sb(ctx, "xt", [P, KC, TOK])
        ident = core.ident = core.sb(ctx, "ident", [P, P])
        x_in, x_out = core.sems(ctx, "io", "x_in x_out")
        with nc.Block() as block:
            @block.sync
            def _(sp):
                sp.dma_start(x[:, :, :], w["x"].rearrange("(t p) n -> p t n", p=P)).then_inc(x_in, 16)
                sp.dma_start(ident[:, :], w["ident"]).then_inc(x_in, 16)
                sp.wait_ge(x_in, 32)
        stages = [
            ("n0", lambda: cross_attention_L0(core, x, xt, ident, w)),
            ("n1", lambda: self_attention_L0(core, x, xt, ident, w)),
            ("n2", lambda: moe_L0(core, x, xn, xt, ident, w)),
            ("n3", lambda: cross_attention_L1(core, x, xn, xt, ident, w)),
            ("n8", lambda: self_attention_L1(core, x, xt, ident, w)),
            ("n9", lambda: moe_L1(core, x, xn, xt, ident, w)),
        ]
        for name, stage in stages[start:upto]:
            norm_stage(core, name, x, xn, xt, ident)
            stage()
        with nc.Block() as block:
            @block.sync
            def _(sp):
                sp.dma_start(out.rearrange("(t p) n -> p t n", p=P), x[:, :, :]).then_inc(x_out, 16)
                sp.wait_ge(x_out, 16)


def laid_out(inputs):
    a = {k: np.asarray(v) for k, v in inputs.items()}
    evens_first = np.concatenate([np.arange(0, D, 2), np.arange(1, D, 2)])
    token = np.arange(P)
    same = token[:, None] // S == token[None, :] // S
    ahead = token[None, :] - token[:, None]
    theta = (np.float32(10000.0) ** (np.float32(-2.0) * np.arange(D // 2, dtype=np.float32) / np.float32(D))).astype(np.float32)
    angle = theta[:, None] * (np.arange(TOK) % S).astype(np.float32)[None, :]
    per_head = lambda m: m.transpose(1, 2, 0).reshape(D, -1)
    w = {
        "x": a["x"].reshape(TOK, D),
        "ctx": a["ctx_768"],
        "ctxT": np.ascontiguousarray(a["ctx_768"].transpose(0, 2, 1)),
        "ident": np.eye(P, dtype=np.float32),
        "L0_xattn_Wq": a["L0_xattn_Wq"],
        "L0_xattn_WkT": np.ascontiguousarray(a["L0_xattn_Wk"].T),
        "L0_xattn_Wv": a["L0_xattn_Wv"],
        "L0_xattn_Wout": a["L0_xattn_Wout"],
        "L0_xattn_bout": a["L0_xattn_bout"],
        "L0_attn_Wq": a["L0_attn_Wq"][evens_first].T,
        "L0_attn_Wk": a["L0_attn_Wk"][evens_first].T,
        "L0_attn_Wv": a["L0_attn_Wv"].T,
        "rope_cos": np.cos(angle),
        "rope_sin": np.sin(angle),
        "mask_L0": np.where(same & (ahead <= 1), 0.0, NEG).astype(np.float32),
        "mask_L1": np.where(same & (ahead <= 0), 0.0, NEG).astype(np.float32),
        "L0_ffn_router_weight": a["L0_ffn_router_weight"].T,
        "L0_ffn_router_bias": a["L0_ffn_router_bias"],
        "L0_ffn_gate_up_proj": a["L0_ffn_gate_up_proj"],
        "L0_ffn_gate_up_bias": a["L0_ffn_gate_up_bias"].reshape(EXPERTS, -1, P).transpose(0, 2, 1),
        "L0_ffn_down_proj": a["L0_ffn_down_proj"],
        "L0_ffn_down_bias": a["L0_ffn_down_bias"],
        "L1_attn_Q": per_head(a["L1_attn_Q"]),
        "L1_attn_K": per_head(a["L1_attn_K"]),
        "L1_attn_V": per_head(a["L1_attn_V"]),
        "L1_attn_W": a["L1_attn_W"].transpose(2, 1, 0).reshape(-1, D),
        "L1_ffn_b1": a["L1_ffn_b1"].reshape(EXPERTS, -1, P).transpose(0, 2, 1),
        "mask_x": a["mask_BxS_bf1"].reshape(1, TOK).view(np.uint8),
        "mask_ctx": a["mask_BxS2_bf1"].view(np.uint8),
        "slots": np.arange(TOK, dtype=np.float32),
        "before": (token[:, None] < token[None, :]).astype(np.float32),
        "two_eyes": np.tile(np.eye(S, dtype=np.float32), (2, 1)),
        "L1_xattn_WkT": a["L1_xattn_Wk"].T,
        "L1_xattn_mod_gate": a["L1_xattn_mod_gate"].reshape(1, 1),
        **{k: a[k] for k in ("L1_ffn_W1", "L1_ffn_W2", "L1_ffn_b2", "L1_ffn_gate_W", "L1_ffn_shared_W", "L1_ffn_shared_b",
                             "L1_ffn_gamma", "L1_ffn_beta")},
        **{f"L1_xattn_{k}": a[f"L1_xattn_{k}"] for k in (
            "Wq", "Wv", "W_film_in", "b_film_in", "W_film_out", "b_film_out", "g_norm_in", "b_norm_in", "g_norm_out",
            "b_norm_out", "g_ffn", "b_ffn", "W1", "W2", "b2", "A_re", "A_im", "C_re", "C_im", "D_skip")},
        "L1_xattn_b1": a["L1_xattn_b1"].reshape(-1, P).T,
        "L1_xattn_log_dt": a["L1_xattn_log_dt"].reshape(-1, P).T,
        **transforms(),
    }
    return {k: np.ascontiguousarray(v) for k, v in w.items()}


def kernel(**inputs):
    import concourse.bacc as bacc
    from concourse.bass_utils import run_bass_kernel_spmd

    nc = bacc.Bacc("TRN2", target_bir_lowering=False, num_devices=1)
    w = laid_out(inputs)
    aps = {k: nc.dram_tensor(f"in_{k}", v.shape, mybir.dt.from_np(v.dtype), kind="ExternalInput").ap() for k, v in w.items()}
    out = nc.dram_tensor("out_x", (TOK, D), F32, kind="ExternalOutput").ap()
    build_program(nc, aps, out)
    r = run_bass_kernel_spmd(nc, [{f"in_{k}": v for k, v in w.items()}], core_ids=[0])
    return r.results[0]["out_x"].reshape(B, S, D)
```

```python
import math
from contextlib import ExitStack

import numpy as np
import concourse.bass as bass
from concourse import mybir

F32 = mybir.dt.float32
F32R = mybir.dt.float32r
U8 = mybir.dt.uint8
ALU = mybir.AluOpType
ACT = mybir.ActivationFunctionType
AXIS = mybir.AxisListType

P = 128
B, S, D = 8, 64, 512
TOK = B * S
TT = TOK // P
KC = D // P
CTX, CD = 1601, 384
CC = CD // P
KT = -(-CTX // P)
LAST = CTX - (KT - 1) * P
EPS = 1e-5
PRIMED = 1
PAIR = 2
NEG = -1e30
EXPERTS = 8
PI = math.pi


class Core:

    def __init__(self, nc, ctx):
        self.nc, self.ctx = nc, ctx

    def sb(self, ctx, name, shape, dt=F32):
        return ctx.enter_context(self.nc.sbuf_tensor(name, list(shape), dt))

    def pb(self, ctx, name, shape, dt=F32):
        return ctx.enter_context(self.nc.psum_tensor(name, list(shape), dt))

    def sems(self, ctx, stage, names):
        made = [self.nc.alloc_semaphore(name=f"{stage}_{n}") for n in names.split()]

        def release():
            self.nc.clear_and_free_semaphores(made)
            self.nc.all_engine_barrier()

        ctx.callback(release)
        return made

    @staticmethod
    def prime(engine, *semaphores):
        for semaphore in semaphores:
            engine.sem_inc(semaphore, PRIMED)


def bcast(v, parts=P):
    return v.partition_broadcast(parts)


class Norm:

    def __init__(self, core, ctx, name, src, normed, gamma=None, beta=None):
        self.core, self.src, self.normed, self.gamma, self.beta = core, src, normed, gamma, beta
        self.stats = core.sb(ctx, f"{name}_stats", [P, TT, 6])
        self.mv = core.sb(ctx, f"{name}_mv", [P, TT, 2])
        self.var = core.sb(ctx, f"{name}_var", [P, TT])
        self.half = core.sb(ctx, f"{name}_half", [P, TT])
        self.rstd = core.sb(ctx, f"{name}_rstd", [P, TT])
        self.stats_ready, self.mv_ready, self.rstd_ready, self.normed_ready = core.sems(
            ctx, name, "stats_ready mv_ready rstd_ready normed_ready")
        self.steps = 1 + (gamma is not None) + (beta is not None)

    def rows_ready(self, t):
        return (self.steps - 1) * TT + t + 1

    def statistics(self, dve):
        for t in range(TT):
            self.core.nc.vector.bn_stats(self.stats[:, t, :], self.src[:, t, :]).then_inc(self.stats_ready, 1)
        for t in range(TT):
            dve.wait_ge(self.stats_ready, t + 1)
            self.core.nc.vector.bn_aggr(self.mv[:, t, :], self.stats[:, t, :]).then_inc(self.mv_ready, 1)

    def inverse_deviation(self, pool):
        G = self.core.nc.gpsimd
        G.memset(self.half[:, :], -0.5).then_inc(self.rstd_ready, 1)
        pool.wait_ge(self.mv_ready, TT)
        G.tensor_scalar_add(self.var[:, :], self.mv[:, :, 1], EPS).then_inc(self.rstd_ready, 1)
        pool.wait_ge(self.rstd_ready, 2)
        G.tensor_tensor(self.rstd[:, :], self.var[:, :], self.half[:, :], ALU.pow).then_inc(self.rstd_ready, 1)

    def rows(self, dve):
        V, normed = self.core.nc.vector, self.normed
        dve.wait_ge(self.rstd_ready, 3)
        for t in range(TT):
            V.tensor_scalar(normed[:, t, :], self.src[:, t, :], self.mv[:, t, 0:1], self.rstd[:, t:t + 1],
                            ALU.subtract, ALU.mult).then_inc(self.normed_ready, 1)
        if self.gamma is not None:
            for t in range(TT):
                dve.wait_ge(self.normed_ready, t + 1)
                V.tensor_tensor(normed[:, t, :], normed[:, t, :], self.gamma[:, :], ALU.mult).then_inc(self.normed_ready, 1)
        if self.beta is not None:
            for t in range(TT):
                dve.wait_ge(self.normed_ready, TT + t + 1)
                V.tensor_tensor(normed[:, t, :], normed[:, t, :], self.beta[:, :], ALU.add).then_inc(self.normed_ready, 1)


def norm_stage(core, name, src, normed, normed_t, ident, gamma=None, beta=None, out=None):
    nc = core.nc
    with ExitStack() as ctx:
        norm = Norm(core, ctx, name, src, normed, gamma, beta)
        tps = core.pb(ctx, f"{name}_tps", [P, TT, KC, P]) if normed_t is not None else None
        t_ready, = core.sems(ctx, name, "t_ready")
        with nc.Block() as block:
            @block.vector
            def _(dve):
                norm.statistics(dve)
                norm.rows(dve)
                if out is not None:
                    for t in range(TT):
                        dve.wait_ge(norm.normed_ready, norm.rows_ready(t))
                        nc.vector.tensor_tensor(out[:, t, :], out[:, t, :], normed[:, t, :], ALU.add)

            @block.gpsimd
            def _(pool):
                norm.inverse_deviation(pool)

            if normed_t is not None:
                @block.tensor
                def _(pe):
                    for t in range(TT):
                        pe.wait_ge(norm.normed_ready, norm.rows_ready(t))
                        for c in range(KC):
                            last = nc.tensor.transpose(tps[:, t, c, :], normed[:, t, c * P:(c + 1) * P], ident[:, :])
                        last.then_inc(t_ready, 1)

                @block.scalar
                def _(act):
                    for t in range(TT):
                        act.wait_ge(t_ready, t + 1)
                        nc.scalar.copy(normed_t[:, :, t * P:(t + 1) * P], tps[:, t, :, :])


def cross_attention_L0(core, normalise, x, xn, xt, k, ident, w):
    nc = core.nc
    H, DH = 8, 64
    PAIR = 2
    UNITS = PAIR * H // 2
    with ExitStack() as ctx:
        qp = core.sb(ctx, "x0_qp", [P, CC, H, TOK])
        PIECE = CC * 512
        GR = -(-KT // 4)
        assert GR == -(-CTX // 512) == 4 and 4 * CD == PIECE
        groups = [(4 * g, min(KT, 4 * g + 4)) for g in range(GR)]
        columns = [(512 * n, min(512 * n + 512, CTX)) for n in range(GR)]
        PIECES = 2 * GR
        filters = FilterTiles(core, ctx, k, (xn, xt), w)
        stage = core.sb(ctx, "x0_stage", [P, 2, PIECE])
        in0, in1, in2, in3 = core.sems(ctx, "x0", "in0 in1 in2 in3")
        piece_in = (in0, in1, in2, in3)
        lent = x[:, :, :].rearrange("p t n -> p (t n)")
        slots = (lent[:, 0:PIECE], stage[:, 0, :], stage[:, 1, :], lent[:, PIECE:TT * D])

        def staged(n):
            if n < GR:
                a, b = columns[n]
                return slots[n][:, 0:CC * (b - a)].rearrange("p (c n) -> p c n", c=CC)
            a, b = groups[n - GR]
            return slots[n - GR][0:P if b < KT else LAST, 0:(b - a) * CD].rearrange("p (t n) -> p t n", n=CD)

        def load(sp, b, n):
            slot = staged(n)
            if n < GR:
                lo, hi = columns[n]
                sp.dma_start(slot, w["ctxT"][bass.ds(b, 1), :, lo:hi].rearrange("b (c p) n -> p (b c) n", p=P)
                             ).then_inc(piece_in[n], 16)
            else:
                lo, hi = groups[n - GR]
                source = w["ctx"][bass.ds(b, 1), lo * P:min(hi * P, CTX), :]
                if hi < KT:
                    source = source.rearrange("b (t p) n -> p (b t) n", p=P)
                else:
                    source = source.rearrange("b p n -> p b n")
                sp.dma_start(slot, source).then_inc(piece_in[n - GR], 16)

        with ExitStack() as c2:
            wq = core.sb(c2, "x0_wq", [P, KC, D])
            wkt = core.sb(c2, "x0_wkt", [P, KC, CD])
            qt = core.sb(c2, "x0_qt", [P, KC, TOK])
            wq_in, q_ready, qt_ready, qp_ready, qp_used = core.sems(c2, "x0", "wq_in q_ready qt_ready qp_ready qp_used")
            with nc.Block() as block:
                @block.sync
                def _(sp):
                    sp.dma_start(wq[:, :, :], w["L0_xattn_Wq"].rearrange("(c p) n -> p c n", p=P)).then_inc(wq_in, 16)
                    sp.dma_start(wkt[:, :, :], w["L0_xattn_WkT"].rearrange("(c p) n -> p c n", p=P)).then_inc(wq_in, 16)

            normalise()
            ps = core.pb(c2, "x0_ps", [P, 8, 512])
            with nc.Block() as block:
                @block.sync
                def _(sp):
                    for n in range(GR):
                        load(sp, 0, n)
                    filters.load(sp)

                @block.tensor
                def _(pe):
                    pe.wait_ge(wq_in, 32)
                    for m in range(KC):
                        for c in range(KC):
                            last = nc.tensor.matmul(ps[:, m, :], wq[:, c, m * P:(m + 1) * P], xt[:, c, :],
                                                    start=(c == 0), stop=(c == KC - 1))
                        last.then_inc(q_ready, 1)
                    for n in range(H * CC):
                        h, c = n // CC, n % CC
                        lo = (h % 2) * DH
                        pe.wait_ge(qt_ready, h // 2 + 1)
                        if n >= 4:
                            pe.wait_ge(qp_used, n - 3)
                        nc.tensor.matmul(ps[:, 4 + n % 4, :], wkt[lo:lo + DH, h // 2, c * P:(c + 1) * P],
                                         qt[lo:lo + DH, h // 2, :], start=True, stop=True).then_inc(qp_ready, 1)

                @block.scalar
                def _(act):
                    for m in range(KC):
                        act.wait_ge(q_ready, m + 1)
                        nc.scalar.mul(qt[:, m, :], ps[:, m, :], DH ** -0.5).then_inc(qt_ready, 1)
                    for n in range(H * CC):
                        act.wait_ge(qp_ready, n + 1)
                        nc.scalar.copy(qp[:, n % CC, n // CC, :], ps[:, 4 + n % 4, :]).then_inc(qp_used, 1)

        with ExitStack() as c2:
            EVEN = CTX + CTX % 2
            ROUNDS = B // PAIR
            PARTS = ((0, 0), (1, 0), (0, 1))
            cxt = core.sb(c2, "x0_cxt", [P, 2, CC, EVEN], F32R)
            cx = core.sb(c2, "x0_cx", [P, 2, KT, CD], F32R)
            qs = core.sb(c2, "x0_qs", [P, 2, 2, CC, P], F32R)
            pr = core.sb(c2, "x0_pr", [P, CTX])
            pt = core.sb(c2, "x0_pt", [P, 2, KT, P], F32R)
            o = core.sb(c2, "x0_o", [P, 2, CD])
            qf = core.sb(c2, "x0_qf", [P, CC, P])
            nmax = core.sb(c2, "x0_nmax", [P, 2])
            total = core.sb(c2, "x0_total", [P, 2])
            inv = core.sb(c2, "x0_inv", [P, 2])
            s_ps = core.pb(c2, "x0_s_ps", [P, 4 * 512])
            t_ps = core.pb(c2, "x0_t_ps", [P, 2, 512])
            o_ps = core.pb(c2, "x0_o_ps", [P, 512])
            ot_ps = core.pb(c2, "x0_ot_ps", [P, 512])
            pad_ready, high_ready, low_ready, qh_ready, qs_ready, s_ready, max_ready, exp_ready, inv_ready, \
                t_ready, pth_ready, pt_ready, o_ready, o_scaled, ot_ready, ot_stored = core.sems(
                    c2, "x0", "pad_ready high_ready low_ready qh_ready qs_ready s_ready max_ready exp_ready "
                    "inv_ready t_ready pth_ready pt_ready o_ready o_scaled ot_ready ot_stored")
            def piece(n):
                if n < GR:
                    a, b = columns[n]
                    return staged(n), cxt[:, 0, :, a:b], cxt[:, 1, :, a:b]
                a, b = groups[n - GR]
                rows = P if b < KT else LAST
                return staged(n), cx[0:rows, 0, a:b, :], cx[0:rows, 1, a:b, :]

            with nc.Block() as block:
                @block.sync
                def _(sp):
                    for n in range(GR, PIECES):
                        sp.wait_ge(low_ready, n - GR + 1)
                        load(sp, 0, n)
                    with sp.Fori(0, B - 1) as b:
                        for n in range(PIECES):
                            sp.wait_ge(low_ready, b * PIECES + (PIECES + n - GR + 1))
                            load(sp, b + 1, n)

                @block.gpsimd
                def _(pool):
                    nc.gpsimd.tensor_scalar(cxt[:, :, :, CTX:EVEN], ident[:, 0:2 * CC].rearrange("p (a c n) -> p a c n", a=2, n=1), 0.0, None,
                                            ALU.mult).then_inc(pad_ready, 1)

                    def low_parts(i, j, first):
                        for n in range(first, first + GR):
                            slot, high, low = piece(n)
                            pool.wait_ge(high_ready, (i * PAIR + j) * PIECES + n + 1)
                            nc.gpsimd.tensor_tensor(low, slot, high.bitcast(F32), ALU.subtract).then_inc(low_ready, 1)

                    core.prime(pool, qs_ready)
                    def queries(i, u):
                        j, r = u // 4, u % 4
                        pool.wait_ge(s_ready, i * UNITS + max(u - 1, 0) + PRIMED)
                        first_row = (i * PAIR + j) * S
                        if u >= UNITS:
                            first_row = pool.snap(next_row, min_val=0, max_val=TOK - S)
                        source = qp[:, :, 2 * r:2 * r + 2, bass.ds(first_row, S)]
                        high, low = (qs[:, u % 2, part, :, :].rearrange("p c (h s) -> p c h s", h=2) for part in range(2))
                        pool.wait_ge(qs_ready, i * UNITS + u + PRIMED)
                        full = qf[:, :, :].rearrange("p c (h s) -> p c h s", h=2)
                        for copy in (high, full):
                            nc.gpsimd.tensor_copy(copy, source).then_inc(qh_ready, 1)
                        pool.wait_ge(qh_ready, i * (2 * UNITS) + 2 * u + 2)
                        nc.gpsimd.tensor_tensor(low, full, high.bitcast(F32), ALU.subtract).then_inc(qs_ready, 1)

                    next_row = pool.alloc_register("x0_next_row")
                    pool.reg_mov(next_row, PAIR * S)
                    queries(0, 0)
                    queries(0, 1)
                    with pool.Fori(0, ROUNDS) as i:
                        pool.wait_ge(low_ready, i * (PAIR * PIECES) + GR)
                        low_parts(i, 0, GR)
                        for u in (2, 3, 4):
                            queries(i, u)
                        low_parts(i, 1, 0)
                        queries(i, 5)
                        low_parts(i, 1, GR)
                        queries(i, 6)
                        queries(i, 7)
                        with pool.If(i < ROUNDS - 1):
                            queries(i, 8)
                            low_parts(i, 2, 0)
                            queries(i, 9)
                        pool.reg_add(next_row, next_row, PAIR * S)

                @block.tensor
                def _(pe):
                    core.prime(pe, s_ready, t_ready, o_ready)
                    pe.wait_ge(pad_ready, 1)

                    def scores(i, u, between=None):
                        j = u // 4
                        pe.wait_ge(qs_ready, i * UNITS + u + 1 + PRIMED)
                        pe.wait_ge(exp_ready, i * UNITS + u + PRIMED)
                        for n, (a, b) in enumerate(columns):
                            if u % 4 == 0:
                                pe.wait_ge(low_ready, (i * PAIR + j) * PIECES + n + 1)
                            b += b % 2
                            for m, (p, q) in enumerate(PARTS):
                                for c in range(CC):
                                    last = nc.tensor.matmul(s_ps[:, a:b], qs[:, u % 2, p, c, :], cxt[:, q, c, a:b],
                                                            start=(m + c == 0), stop=(m + c == len(PARTS) + CC - 2))
                            if n == GR - 1:
                                last.then_inc(s_ready, 1)
                            if between is not None:
                                turn(i, between, n)

                    def turn(i, u, g):
                        a, b = groups[g]
                        if g == 0:
                            pe.wait_ge(exp_ready, i * UNITS + u + 1 + PRIMED)
                        pe.wait_ge(pt_ready, i * (UNITS * GR) + max(u * GR + g - 1, 0) + PRIMED)
                        for t in range(a, b):
                            rows = P if t < KT - 1 else LAST
                            last = nc.tensor.transpose(t_ps[0:rows, g % 2, (t - a) * P:(t - a + 1) * P],
                                                       pr[:, t * P:t * P + rows], ident[:, :])
                        last.then_inc(t_ready, 1)

                    def weigh(i, u):
                        j = u // 4
                        pe.wait_ge(o_scaled, i * UNITS + u + PRIMED)
                        for t in range(KT):
                            if t % 4 == 0:
                                if u % 4 == 0:
                                    pe.wait_ge(low_ready, (i * PAIR + j) * PIECES + GR + t // 4 + 1)
                                pe.wait_ge(pt_ready, i * (UNITS * GR) + u * GR + t // 4 + 1 + PRIMED)
                            rows = P if t < KT - 1 else LAST
                            for m, (p, q) in enumerate(PARTS):
                                last = nc.tensor.matmul(o_ps[:, 0:CD], pt[0:rows, p, t, :], cx[0:rows, q, t, :],
                                                        start=(t + m == 0), stop=(t + m == KT - 1 + len(PARTS) - 1))
                        last.then_inc(o_ready, 1)

                    def turn_out(i, u):
                        pe.wait_ge(o_scaled, i * UNITS + u + 1 + PRIMED)
                        pe.wait_ge(ot_stored, i * UNITS + u + PRIMED)
                        for c in range(CC):
                            last = nc.tensor.transpose(ot_ps[:, c * P:(c + 1) * P], o[:, u % 2, c * P:(c + 1) * P],
                                                       ident[:, :])
                        last.then_inc(ot_ready, 1)

                    scores(0, 0)
                    with pe.Fori(0, ROUNDS) as i:
                        for u in range(UNITS):
                            if u + 1 < UNITS:
                                scores(i, u + 1, between=u)
                            else:
                                with pe.If(i < ROUNDS - 1):
                                    scores(i, UNITS)
                                for g in range(GR):
                                    turn(i, u, g)
                            weigh(i, u)
                            if u >= 1:
                                turn_out(i, u - 1)
                        turn_out(i, UNITS - 1)

                @block.vector
                def _(dve):
                    core.prime(dve, pt_ready, o_scaled, inv_ready)
                    for n in range(GR):
                        slot, high, low = piece(n)
                        dve.wait_ge(high_ready, n + 1)
                        nc.vector.tensor_tensor(low, slot, high.bitcast(F32), ALU.subtract).then_inc(low_ready, 1)
                    dve.wait_ge(filters.dt_ready, 1)

                    def row_max(i, u):
                        dve.wait_ge(s_ready, i * UNITS + u + 1 + PRIMED)
                        dve.wait_ge(exp_ready, i * UNITS + max(u - 1, 0) + PRIMED)
                        nc.vector.reduce_max(nmax[:, u % 2:u % 2 + 1], s_ps[:, 0:CTX], AXIS.X, negate=True).then_inc(max_ready, 1)

                    row_max(0, 0)
                    with dve.Fori(0, ROUNDS) as i:
                        for u in range(UNITS):
                            dve.wait_ge(exp_ready, i * UNITS + u + 1 + PRIMED)
                            nc.vector.reciprocal(inv[:, u % 2:u % 2 + 1], total[:, u % 2:u % 2 + 1]).then_inc(inv_ready, 1)
                            for g, (a, b) in enumerate(groups):
                                rows = P if b < KT else LAST
                                dve.wait_ge(pth_ready, i * (UNITS * GR) + u * GR + g + 1)
                                nc.vector.tensor_tensor(pt[0:rows, 1, a:b, :],
                                                        t_ps[0:rows, g % 2, 0:(b - a) * P].rearrange("p (t n) -> p t n", n=P),
                                                        pt[0:rows, 0, a:b, :].bitcast(F32), ALU.subtract).then_inc(pt_ready, 1)
                            if u + 1 < UNITS:
                                row_max(i, u + 1)
                            else:
                                with dve.If(i < ROUNDS - 1):
                                    row_max(i, UNITS)
                            filters.vector_part(dve, i, u)
                            dve.wait_ge(o_ready, i * UNITS + u + 1 + PRIMED)
                            dve.wait_ge(inv_ready, i * UNITS + u + 1 + PRIMED)
                            if u >= 2:
                                dve.wait_ge(ot_ready, i * UNITS + u - 1)
                            nc.vector.tensor_scalar(o[:, u % 2, :], o_ps[:, 0:CD], inv[:, u % 2:u % 2 + 1], None,
                                                    ALU.mult).then_inc(o_scaled, 1)

                @block.scalar
                def _(act):
                    core.prime(act, exp_ready, ot_stored)
                    def high_parts(i, j, first, last):
                        for n in range(first, last):
                            slot, high, _ = piece(n)
                            act.wait_ge(piece_in[n % GR], (i * PAIR + j) * 32 + (16 if n < GR else 32))
                            act.wait_ge(s_ready if n < GR else o_ready, i * UNITS + 4 * j + PRIMED)
                            nc.scalar.copy(high, slot).then_inc(high_ready, 1)

                    high_parts(0, 0, 0, GR)
                    filters.step_sizes(act)
                    def exponent(i, u):
                        act.wait_ge(max_ready, i * UNITS + u + 1)
                        act.wait_ge(inv_ready, i * UNITS + max(u - 1, 0) + PRIMED)
                        act.wait_ge(t_ready, (i * UNITS + u) * GR + PRIMED)
                        nc.scalar.activation(pr[:, :], s_ps[:, 0:CTX], ACT.Exp, bias=nmax[:, u % 2:u % 2 + 1],
                                             accum_out=total[:, u % 2:u % 2 + 1]).then_inc(exp_ready, 1)

                    exponent(0, 0)
                    with act.Fori(0, ROUNDS) as i:
                        def store_out(u):
                            j, r = u // 4, u % 4
                            act.wait_ge(ot_ready, i * UNITS + u + 1)
                            nc.scalar.copy(qp[:, :, 2 * r:2 * r + 2, bass.ds((i * PAIR + j) * S, S)],
                                           ot_ps[:, 0:CC * P].rearrange("p (c h s) -> p c h s", c=CC, h=2)).then_inc(ot_stored, 1)

                        high_parts(i, 0, GR, PIECES)
                        for u in range(UNITS):
                            for g, (a, b) in enumerate(groups):
                                rows = P if b < KT else LAST
                                act.wait_ge(t_ready, i * (UNITS * GR) + u * GR + g + 1 + PRIMED)
                                act.wait_ge(o_ready, i * UNITS + u + PRIMED)
                                nc.scalar.copy(pt[0:rows, 0, a:b, :],
                                               t_ps[0:rows, g % 2, 0:(b - a) * P].rearrange("p (t n) -> p t n", n=P)
                                               ).then_inc(pth_ready, 1)
                            if u == 2:
                                high_parts(i, 1, 0, 1)
                            if u + 1 < UNITS:
                                exponent(i, u + 1)
                            if u == 2:
                                high_parts(i, 1, 1, GR)
                            if u == UNITS - 2:
                                with act.If(i < ROUNDS - 1):
                                    high_parts(i, 2, 0, GR)
                            if u == UNITS - 1:
                                with act.If(i < ROUNDS - 1):
                                    exponent(i, UNITS)
                            filters.scalar_part(act, i, u)
                            if u == 3:
                                high_parts(i, 1, GR, PIECES)
                            if u >= 1:
                                store_out(u - 1)
                        store_out(UNITS - 1)

        with ExitStack() as c2:
            wv = core.sb(c2, "x0_wv", [P, CC, D])
            wout = core.sb(c2, "x0_wout", [P, KC, D])
            bout = core.sb(c2, "x0_bout", [P, D])
            at = core.sb(c2, "x0_at", [P, KC, TOK])
            a_ps = core.pb(c2, "x0_a_ps", [P, KC, 512])
            y_ps = core.pb(c2, "x0_y_ps", [P, TT, 512])
            wv_in, wout_in, x_in, a_ready, at_ready, y_ready, xb_ready = core.sems(c2, "x0", "wv_in wout_in x_in a_ready at_ready y_ready xb_ready")
            with nc.Block() as block:
                @block.sync
                def _(sp):
                    sp.dma_start(wv[:, :, :], w["L0_xattn_Wv"].rearrange("(c p) n -> p c n", p=P)).then_inc(wv_in, 16)
                    sp.dma_start(wout[:, :, :], w["L0_xattn_Wout"].rearrange("(c p) n -> p c n", p=P)).then_inc(wout_in, 16)
                    sp.dma_start(bout[:, :], bcast(w["L0_xattn_bout"])).then_inc(x_in, 16)
                    sp.dma_start(x[:, :, :], w["x"].rearrange("(t p) n -> p t n", p=P)).then_inc(x_in, 16)

                @block.tensor
                def _(pe):
                    pe.wait_ge(wv_in, 16)
                    for m in range(KC):
                        for h in (2 * m, 2 * m + 1):
                            lo = (h % 2) * DH
                            for c in range(CC):
                                last = nc.tensor.matmul(a_ps[lo:lo + DH, m, :], wv[:, c, h * DH:(h + 1) * DH], qp[:, c, h, :],
                                                        start=(c == 0), stop=(c == CC - 1))
                        last.then_inc(a_ready, 1)
                    for m in range(KC):
                        pe.wait_ge(at_ready, m + 1)
                    pe.wait_ge(wout_in, 16)
                    for t in range(TT):
                        for c in range(KC):
                            last = nc.tensor.matmul(y_ps[:, t, :], at[:, c, t * P:(t + 1) * P], wout[:, c, :],
                                                    start=(c == 0), stop=(c == KC - 1))
                        last.then_inc(y_ready, 1)

                @block.scalar
                def _(act):
                    for m in range(KC):
                        act.wait_ge(a_ready, m + 1)
                        nc.scalar.copy(at[:, m, :], a_ps[:, m, :]).then_inc(at_ready, 1)

                @block.vector
                def _(dve):
                    dve.wait_ge(x_in, 32)
                    for t in range(TT):
                        nc.vector.tensor_tensor(x[:, t, :], x[:, t, :], bout[:, :], ALU.add).then_inc(xb_ready, 1)
                    for t in range(TT):
                        dve.wait_ge(y_ready, t + 1)
                        dve.wait_ge(xb_ready, t + 1)
                        nc.vector.tensor_tensor(x[:, t, :], x[:, t, :], y_ps[:, t, :], ALU.add)


def self_attention_L0(core, normalise, x, xt, ident, w):
    nc = core.nc
    HALF = KC // 2
    with ExitStack() as ctx:
        wq = core.sb(ctx, "s0_wq", [P, KC, D])
        wk = core.sb(ctx, "s0_wk", [P, KC, D])
        wv = core.sb(ctx, "s0_wv", [P, KC, D])
        cos = core.sb(ctx, "s0_cos", [P, HALF, TOK])
        sin = core.sb(ctx, "s0_sin", [P, HALF, TOK])
        mask = core.sb(ctx, "s0_mask", [P, P])
        rot = core.sb(ctx, "s0_rot", [P, 2, KC, TOK])
        tmp = core.sb(ctx, "s0_tmp", [P, 4, HALF, TOK])
        v = core.sb(ctx, "s0_v", [P, TT, D])
        pr = core.sb(ctx, "s0_pr", [P, TT, P])
        pt = core.sb(ctx, "s0_pt", [P, TT, P])
        red = core.sb(ctx, "s0_red", [P, 3, TT])
        in_q, in_k, in_v, in_tab, qk_ready, prod_ready, rot_ready, v_ready, vs_ready, s_ready, sm_ready, max_ready, \
            exp_ready, inv_ready, norm_ready, t_ready, pt_ready, y_ready = core.sems(
                ctx, "s0", "in_q in_k in_v in_tab qk_ready prod_ready rot_ready v_ready vs_ready s_ready sm_ready "
                "max_ready exp_ready inv_ready norm_ready t_ready pt_ready y_ready")
        with nc.Block() as block:
            @block.sync
            def _(sp):
                for dst, name, s in ((wq, "L0_attn_Wq", in_q), (wk, "L0_attn_Wk", in_k), (wv, "L0_attn_Wv", in_v)):
                    sp.dma_start(dst[:, :, :], w[name].rearrange("(c p) n -> p c n", p=P)).then_inc(s, 16)
                sp.dma_start(cos[:, :, :], w["rope_cos"].rearrange("(c p) n -> p c n", p=P)).then_inc(in_tab, 16)
                sp.dma_start(sin[:, :, :], w["rope_sin"].rearrange("(c p) n -> p c n", p=P)).then_inc(in_tab, 16)
                sp.dma_start(mask[:, :], w["mask_L0"]).then_inc(in_tab, 16)

        normalise()
        qk_ps = core.pb(ctx, "s0_qk_ps", [P, KC, 512])
        r_ps = core.pb(ctx, "s0_r_ps", [P, 4, 512])
        with nc.Block() as block:
            @block.tensor
            def _(pe):
                for a, (wt, s) in enumerate(((wq, in_q), (wk, in_k))):
                    pe.wait_ge(s, 16)
                    if a == 1:
                        pe.wait_ge(prod_ready, 4)
                    for m in range(KC):
                        for c in range(KC):
                            last = nc.tensor.matmul(qk_ps[:, m, :], wt[:, c, m * P:(m + 1) * P], xt[:, c, :],
                                                    start=(c == 0), stop=(c == KC - 1))
                    last.then_inc(qk_ready, 1)
                pe.wait_ge(in_v, 16)
                for t in range(TT):
                    for c in range(KC):
                        last = nc.tensor.matmul(r_ps[:, t, :], xt[:, c, t * P:(t + 1) * P], wv[:, c, :],
                                                start=(c == 0), stop=(c == KC - 1))
                    last.then_inc(v_ready, 1)
                pe.wait_ge(rot_ready, 4)
                for t in range(TT):
                    pe.wait_ge(vs_ready, t + 1)
                    for c in range(KC):
                        last = nc.tensor.matmul(r_ps[:, t, 0:P], rot[:, 0, c, t * P:(t + 1) * P], rot[:, 1, c, t * P:(t + 1) * P],
                                                start=(c == 0), stop=(c == KC - 1))
                    last.then_inc(s_ready, 1)
                for t in range(TT):
                    pe.wait_ge(norm_ready, t + 1)
                    nc.tensor.transpose(qk_ps[:, t, 0:P], pr[:, t, :], ident[:, :]).then_inc(t_ready, 1)
                for t in range(TT):
                    pe.wait_ge(pt_ready, t + 1)
                    nc.tensor.matmul(r_ps[:, t, :], pt[:, t, :], v[:, t, :], start=True, stop=True).then_inc(y_ready, 1)

            @block.vector
            def _(dve):
                dve.wait_ge(in_tab, 48)
                for a in range(2):
                    even, odd = qk_ps[:, 0:HALF, :], qk_ps[:, HALF:KC, :]
                    dve.wait_ge(qk_ready, a + 1)
                    dve.wait_ge(rot_ready, 2 * a)
                    for n, (part, table) in enumerate(((even, cos), (odd, sin), (even, sin), (odd, cos))):
                        nc.vector.tensor_tensor(tmp[:, n, :, :], part, table[:, :, :], ALU.mult).then_inc(prod_ready, 1)
                    dve.wait_ge(prod_ready, 4 * a + 4)
                    nc.vector.tensor_tensor(rot[:, a, 0:HALF, :], tmp[:, 0, :, :], tmp[:, 1, :, :], ALU.subtract).then_inc(rot_ready, 1)
                    nc.vector.tensor_tensor(rot[:, a, HALF:KC, :], tmp[:, 2, :, :], tmp[:, 3, :, :], ALU.add).then_inc(rot_ready, 1)
                for t in range(TT):
                    dve.wait_ge(s_ready, t + 1)
                    nc.vector.scalar_tensor_tensor(pr[:, t, :], r_ps[:, t, 0:P], D ** -0.5, mask[:, :],
                                                   ALU.mult, ALU.add).then_inc(sm_ready, 1)
                for t in range(TT):
                    dve.wait_ge(sm_ready, t + 1)
                    nc.vector.reduce_max(red[:, 0, t:t + 1], pr[:, t, :], AXIS.X, negate=True).then_inc(max_ready, 1)
                for t in range(TT):
                    dve.wait_ge(exp_ready, t + 1)
                    nc.vector.reciprocal(red[:, 2, t:t + 1], red[:, 1, t:t + 1]).then_inc(inv_ready, 1)
                for t in range(TT):
                    dve.wait_ge(inv_ready, t + 1)
                    nc.vector.tensor_scalar(pr[:, t, :], pr[:, t, :], red[:, 2, t:t + 1], None, ALU.mult).then_inc(norm_ready, 1)
                for t in range(TT):
                    dve.wait_ge(y_ready, t + 1)
                    nc.vector.tensor_tensor(x[:, t, :], x[:, t, :], r_ps[:, t, :], ALU.add)

            @block.scalar
            def _(act):
                for t in range(TT):
                    act.wait_ge(v_ready, t + 1)
                    nc.scalar.copy(v[:, t, :], r_ps[:, t, :]).then_inc(vs_ready, 1)
                for t in range(TT):
                    act.wait_ge(max_ready, t + 1)
                    nc.scalar.activation(pr[:, t, :], pr[:, t, :], ACT.Exp, bias=red[:, 0, t:t + 1],
                                         accum_out=red[:, 1, t:t + 1]).then_inc(exp_ready, 1)
                for t in range(TT):
                    act.wait_ge(t_ready, t + 1)
                    nc.scalar.copy(pt[:, t, :], qk_ps[:, t, 0:P]).then_inc(pt_ready, 1)


class RouteWeights:

    def __init__(self, core, ctx, name, weight, bias, w):
        self.weight, self.bias, self.w = weight, bias, w
        self.wr = core.sb(ctx, f"{name}_wr", [P, KC, EXPERTS])
        self.br = core.sb(ctx, f"{name}_br", [P, EXPERTS])
        self.before = core.sb(ctx, f"{name}_before", [P, P])
        self.w_in, self.before_in = core.sems(ctx, f"{name}w", "w_in before_in")

    def load(self, sp):
        sp.dma_start(self.wr[:, :, :], self.weight.rearrange("(c p) n -> p c n", p=P)).then_inc(self.w_in, 16)
        if self.bias is not None:
            sp.dma_start(self.br[:, :], bcast(self.bias)).then_inc(self.w_in, 16)
        sp.dma_start(self.before[:, :], self.w["before"]).then_inc(self.before_in, 16)


def route(core, name, normed_t, weights, normalise, chosen, ident):
    nc = core.nc
    gate, gate_t, slot, count = chosen
    E = EXPERTS
    NOWHERE = 2.0 ** 20
    wr, br, before, bias, w_in, before_in = weights.wr, weights.br, weights.before, weights.bias, weights.w_in, weights.before_in
    KEPT, FILL, TAKEN = 2, -1.0, -2.0
    with ExitStack() as ctx:
        sc = core.sb(ctx, f"{name}_sc", [P, TT, 2 * E])
        rep = core.sb(ctx, f"{name}_rep", [P, TT, 2 * E])
        top = core.sb(ctx, f"{name}_top", [P, TT, E])
        red = core.sb(ctx, f"{name}_red", [P, 5, TT])
        picked = core.sb(ctx, f"{name}_picked", [P, TT, E])
        away = core.sb(ctx, f"{name}_away", [P, TT, E])
        ones = core.sb(ctx, f"{name}_ones", [P, P])
        n_ps = core.pb(ctx, f"{name}_n_ps", [P, 512])
        c_ps = core.pb(ctx, f"{name}_c_ps", [P, 512])
        l_ps = core.pb(ctx, f"{name}_l_ps", [P, 512])
        g_ps = core.pb(ctx, f"{name}_g_ps", [P, 512])
        l_ready, steps, exp_ready, gate_ready, gt_ready, picked_ready, n_ready, away_ready, ones_ready = core.sems(
            ctx, name, "l_ready steps exp_ready gate_ready gt_ready picked_ready n_ready away_ready ones_ready")
        with nc.Block() as block:
            @block.gpsimd
            def _(pool):
                nc.gpsimd.memset(ones[:, :], 1.0).then_inc(ones_ready, 1)

            @block.tensor
            def _(pe):
                pe.wait_ge(w_in, 32 if bias is not None else 16)
                for t in range(TT):
                    for c in range(KC):
                        last = nc.tensor.matmul(l_ps[:, t * E:(t + 1) * E], normed_t[:, c, t * P:(t + 1) * P], wr[:, c, :],
                                                start=(c == 0), stop=(c == KC - 1))
                last.then_inc(l_ready, 1)
                pe.wait_ge(picked_ready, 1)
                pe.wait_ge(before_in, 16)
                pe.wait_ge(ones_ready, 1)
                for t in range(TT):
                    for r in range(t):
                        nc.tensor.matmul(n_ps[:, t * E:(t + 1) * E], ones[:, :], picked[:, r, :], start=(r == 0), stop=False)
                    nc.tensor.matmul(n_ps[:, t * E:(t + 1) * E], before[:, :], picked[:, t, :], start=(t == 0), stop=True)
                for t in range(TT):
                    last = nc.tensor.matmul(c_ps[0:1, 0:E], ones[:, 0:1], picked[:, t, :], start=(t == 0), stop=(t == TT - 1))
                last.then_inc(n_ready, 1)
                pe.wait_ge(gate_ready, TT)
                for t in range(TT):
                    last = nc.tensor.transpose(g_ps[0:E, t * P:(t + 1) * P], gate[:, t, :], ident[:, :])
                last.then_inc(gt_ready, 1)

            @block.scalar
            def _(act):
                for t in range(TT):
                    act.wait_ge(steps, 3 + t + 1)
                    nc.scalar.activation(sc[:, t, 0:E], sc[:, t, 0:E], ACT.Exp, bias=red[:, 0, t:t + 1],
                                         accum_out=red[:, 1, t:t + 1]).then_inc(exp_ready, 1)
                act.wait_ge(gt_ready, 1)
                nc.scalar.copy(gate_t[:, :], g_ps[0:E, :])

            @block.vector
            def _(dve):
                done = [0]

                def step(instruction):
                    done[0] += 1
                    instruction.then_inc(steps, 1)

                def sync():
                    dve.wait_ge(steps, done[0])

                step(nc.vector.memset(sc[:, :, E:2 * E], FILL))
                step(nc.vector.memset(top[:, :, :], FILL))
                dve.wait_ge(l_ready, 1)
                logits = l_ps[:, 0:TT * E].rearrange("p (t e) -> p t e", e=E)
                if bias is not None:
                    step(nc.vector.tensor_tensor(sc[:, :, 0:E], logits, br[:, :].unsqueeze(1).broadcast_to([P, TT, E]), ALU.add))
                else:
                    step(nc.vector.tensor_copy(sc[:, :, 0:E], logits))
                sync()
                for t in range(TT):
                    step(nc.vector.reduce_max(red[:, 0, t:t + 1], sc[:, t, 0:E], AXIS.X, negate=True))
                dve.wait_ge(exp_ready, TT)
                step(nc.vector.reciprocal(red[:, 2, :], red[:, 1, :]))
                sync()
                for t in range(TT):
                    step(nc.vector.tensor_scalar(sc[:, t, 0:E], sc[:, t, 0:E], red[:, 2, t:t + 1], None, ALU.mult))
                sync()
                for t in range(TT):
                    step(nc.vector.max(rep[:, t, 0:E], sc[:, t, 0:E]))
                sync()
                step(nc.vector.tensor_copy(top[:, :, 0:KEPT], rep[:, :, 0:KEPT]))
                step(nc.vector.tensor_tensor(red[:, 3, :], rep[:, :, 0], rep[:, :, 1], ALU.add))
                sync()
                step(nc.vector.reciprocal(red[:, 4, :], red[:, 3, :]))
                for t in range(TT):
                    step(nc.vector.match_replace(rep[:, t, :], top[:, t, :], sc[:, t, :], TAKEN))
                sync()
                nc.vector.tensor_scalar(picked[:, :, :], rep[:, :, 0:E], TAKEN, None, ALU.is_equal).then_inc(picked_ready, 1)
                dve.wait_ge(picked_ready, 1)
                nc.vector.tensor_scalar(away[:, :, :], picked[:, :, :], -NOWHERE, NOWHERE, ALU.mult, ALU.add).then_inc(away_ready, 1)
                dve.wait_ge(away_ready, 1)
                dve.wait_ge(n_ready, 1)
                nc.vector.tensor_tensor(slot[:, :, :], n_ps[:, 0:TT * E].rearrange("p (t e) -> p t e", e=E), away[:, :, :], ALU.add)
                nc.vector.tensor_copy(count[0:1, :], c_ps[0:1, 0:E])
                for t in range(TT):
                    ins = nc.vector.scalar_tensor_tensor(gate[:, t, :], rep[:, t, 0:E], TAKEN, sc[:, t, 0:E],
                                                         ALU.is_equal, ALU.mult)
                    if normalise:
                        step(ins)
                    else:
                        ins.then_inc(gate_ready, 1)
                if normalise:
                    sync()
                    for t in range(TT):
                        nc.vector.tensor_scalar(gate[:, t, :], gate[:, t, :], red[:, 4, t:t + 1], None,
                                                ALU.mult).then_inc(gate_ready, 1)


class ExpertWeights:

    def __init__(self, core, ctx, name, up_w, up_b, down_w, down_b, w, ahead):
        self.up_w, self.up_b, self.down_w = up_w, up_b, down_w
        self.w1 = core.sb(ctx, f"{name}_w1", [P, PAIR, KC, up_w.shape[2]])
        self.w2 = core.sb(ctx, f"{name}_w2", [P, PAIR, down_w.shape[1] // P, D])
        self.b1 = core.sb(ctx, f"{name}_b1", [P, PAIR, up_b.shape[2]])
        self.b2 = core.sb(ctx, f"{name}_b2", [EXPERTS, D])
        self.slots = core.sb(ctx, f"{name}_slots", [P, TOK])
        self.c_in, w1_in0, w1_in1, w2_in0, w2_in1 = core.sems(ctx, f"{name}w", "c_in w1_in0 w1_in1 w2_in0 w2_in1")
        self.w1_in, self.w2_in = (w1_in0, w1_in1), (w2_in0, w2_in1)
        with core.nc.Block() as block:
            @block.sync
            def _(sp):
                for load in ahead:
                    load(sp)
                sp.dma_start(self.b2[:, :], down_b).then_inc(self.c_in, 16)
                sp.dma_start(self.slots[:, :], bcast(w["slots"])).then_inc(self.c_in, 16)
                for j in range(PAIR):
                    self.load(sp, j, j)

    def load(self, sp, e, j):
        sp.dma_start(self.w1[:, j, :, :], self.up_w[bass.ds(e, 1), :, :].rearrange("e (c p) n -> p (e c) n", p=P)).then_inc(self.w1_in[j], 16)
        sp.dma_start(self.b1[:, j, :], self.up_b[bass.ds(e, 1), :, :].rearrange("e p n -> (e p) n")).then_inc(self.w1_in[j], 16)
        sp.dma_start(self.w2[:, j, :, :], self.down_w[bass.ds(e, 1), :, :].rearrange("e (c p) n -> p (e c) n", p=P)).then_inc(self.w2_in[j], 16)


def experts(core, name, normed, free, acc, chosen, weights, hidden, gated):
    nc = core.nc
    gate, gate_t, slot, count = chosen
    E = EXPERTS
    ALPHA, LIMIT = 1.702, 7.0
    HC = hidden // P
    w1, w2, b1, b2, slots = weights.w1, weights.w2, weights.b1, weights.b2, weights.slots
    c_in, w1_in, w2_in = weights.c_in, weights.w1_in, weights.w2_in
    UPS = w1.shape[3] // hidden
    PER = 4 // UPS
    NG = HC // PER
    ROUNDS = E // PAIR
    STEPS = 2 * PER + 2
    TURNS = E * TT
    with ExitStack() as ctx:
        g2 = core.sb(ctx, f"{name}_g2", [P, 2, PAIR, TT])
        rows = core.sb(ctx, f"{name}_rows", [P, 2, TT, D], F32R)
        hot = core.sb(ctx, f"{name}_hot", [P, TT, P], F32R)
        back = core.sb(ctx, f"{name}_back", [P, TOK], F32R)
        gs = core.sb(ctx, f"{name}_gs", [P, 1])
        xg = normed[:, 0, :].rearrange("p (c n) -> p c n", n=P)
        h = free[:, :, :].rearrange("p c n -> p (c n)").rearrange("p (c n) -> p c n", n=P)
        y = core.sb(ctx, f"{name}_y", [P, 2, D], F32R)
        tmp = core.sb(ctx, f"{name}_tmp", [P, 4, PER, P]) if gated else None
        a_ps = core.pb(ctx, f"{name}_a_ps", [P, TT, 512])
        u_ps = core.pb(ctx, f"{name}_u_ps", [P, 2, 4, P])
        x_ps = core.pb(ctx, f"{name}_x_ps", [P, KC, P])
        y_ps = core.pb(ctx, f"{name}_y_ps", [P, 512])
        zeroed, expert_done, g2_ready, hot_ready, x_ready, xg_ready, t_ready, back_ready, \
            up_ready, h_ready, down_ready, y_ready, sum_ready, parts, sig_ready, rows_ready, gp_ready, gs_ready, high_ready = core.sems(
                ctx, name, "zeroed expert_done g2_ready hot_ready x_ready xg_ready t_ready "
                "back_ready up_ready h_ready down_ready y_ready sum_ready parts sig_ready "
                "rows_ready gp_ready gs_ready high_ready")

        def turns(engine, each_turn, each_round=None, first=None, last=None):
            register = engine.alloc_register(f"{name}_turns_{engine.engine.name}")
            engine.reg_mov(register, 0)

            def turn(i, j, k):
                each_turn(i, j, k, engine.snap(register, min_val=0, max_val=TURNS))
                engine.reg_add(register, register, 1)

            with engine.Fori(0, ROUNDS) as i:
                if each_round:
                    each_round(i, engine.snap(register, min_val=0, max_val=TURNS))
                for j in range(PAIR):
                    if first:
                        first(i, j)
                    tokens = engine.value_load(count[0:1, bass.ds(i * PAIR + j, 1)], min_val=0, max_val=TOK)
                    turn(i, j, 0)
                    with engine.If(tokens > P):
                        with engine.Fori(1, TT) as k:
                            with engine.If(k * P < tokens):
                                turn(i, j, k)
                    if last:
                        last()
            return engine.snap(register, min_val=0, max_val=TURNS)

        with nc.Block() as block:
            @block.sync
            def _(sp):
                with sp.Fori(0, ROUNDS - 1) as i:
                    for j in range(PAIR):
                        sp.wait_ge(expert_done, i * PAIR + j + 1)
                        weights.load(sp, (i + 1) * PAIR + j, j)

            @block.gpsimd
            def _(pool):
                nc.gpsimd.tensor_scalar(back[:, :], normed[:, 0, :], 0.0, None, ALU.mult).then_inc(zeroed, 1)
                nc.gpsimd.memset(gs[:, :], 0.0).then_inc(zeroed, 1)

            @block.tensor
            def _(pe):
                pe.wait_ge(c_in, 32)
                pe.wait_ge(zeroed, 2)
                for t in range(TT):
                    nc.tensor.matmul(a_ps[:, t, :], gate_t[:, t * P:(t + 1) * P], b2[:, :], start=True, stop=True)
                nc.tensor.matmul(y_ps[:, :], back[:, 0:P].bitcast(F32), slots[:, :], start=True, stop=True).then_inc(down_ready, 1)
                pe.wait_ge(rows_ready, 2)
                core.prime(pe, t_ready, hot_ready, back_ready)

                def first(i, j):
                    pe.wait_ge(w1_in[j], i * 32 + 32)
                    pe.wait_ge(w2_in[j], i * 16 + 16)

                def scatter(t):
                    pe.wait_ge(y_ready, t + 1)
                    for r in range(TT):
                        for part in range(2):
                            done = nc.tensor.matmul(a_ps[:, r, :], back[:, r * P:(r + 1) * P], y[:, part, :], start=False, stop=True,
                                                    skip_group_check=True)
                    return done

                def each_turn(i, j, k, t):
                    pe.wait_ge(hot_ready, t + 1 + PRIMED)
                    pe.wait_ge(back_ready, t + PRIMED)
                    for c in range(KC):
                        for r in range(TT):
                            for part in range(2):
                                last = nc.tensor.matmul(x_ps[:, c, :], rows[:, part, r, c * P:(c + 1) * P], hot[:, r, :],
                                                        start=(r + part == 0), stop=(r + part == TT))
                    last.then_inc(x_ready, 1)
                    pe.wait_ge(xg_ready, t + 1)

                    def up(g):
                        if g >= 2:
                            pe.wait_ge(h_ready, t * NG + g - 1)
                        for n in range(PER):
                            c = g * PER + n
                            for a in range(UPS):
                                for m in range(KC):
                                    last = nc.tensor.matmul(u_ps[:, g % 2, a * PER + n, :],
                                                            w1[:, j, m, a * hidden + c * P:a * hidden + (c + 1) * P], xg[:, m, :],
                                                            start=(m == 0), stop=(m == KC - 1))
                        last.then_inc(up_ready, 1)

                    def down(g):
                        pe.wait_ge(h_ready, t * NG + g + 1)
                        if g == 0:
                            pe.wait_ge(gs_ready, t + 1)
                        for c in range(g * PER, (g + 1) * PER):
                            last = nc.tensor.matmul(y_ps[:, :], h[:, c, :], w2[:, j, c, :], start=(c == 0), stop=(c == HC - 1))
                        if g == NG - 1:
                            last.then_inc(down_ready, 1)

                    up(0)
                    for g in range(NG):
                        if g + 1 < NG:
                            up(g + 1)
                        if g == 0:
                            pe.wait_ge(y_ready, t + 1)
                            for r in range(TT):
                                last = nc.tensor.matmul(y_ps[:, 0:1], hot[:, r, :].bitcast(F32), g2[:, 1, j, r:r + 1],
                                                        start=(r == 0), stop=(r == TT - 1))
                            last.then_inc(gp_ready, 1)
                            scatter(t)
                            for r in range(TT):
                                last = nc.tensor.transpose(x_ps[:, r, :], hot[:, r, :].bitcast(F32), core.ident[:, :])
                            last.then_inc(t_ready, 1)
                        down(g)

                t = turns(pe, each_turn, first=first, last=lambda: pe.drain().then_inc(expert_done, 1))
                scatter(t).then_inc(sum_ready, 1)

            @block.vector
            def _(dve):
                V = nc.vector

                def each_round(i, t):
                    dve.wait_ge(hot_ready, t + PRIMED)
                    for n, source in enumerate((slot, gate)):
                        V.tensor_copy(g2[:, n, :, :], source[:, :, bass.ds(i * PAIR, PAIR)].rearrange("p t e -> p e t")).then_inc(g2_ready, 1)
                    dve.wait_ge(g2_ready, 2 * i + 2)

                def first(i, j):
                    dve.wait_ge(w1_in[j], i * 32 + 32)

                def take(t):
                    dve.wait_ge(down_ready, t + 1)
                    V.tensor_scalar(y[:, 0, :], y_ps[:, :], gs[:, 0:1], None, ALU.mult).then_inc(high_ready, 1)
                    dve.wait_ge(high_ready, t + 1)
                    V.scalar_tensor_tensor(y[:, 1, :], y_ps[:, :], gs[:, 0:1], y[:, 0, :].bitcast(F32), ALU.mult,
                                           ALU.subtract).then_inc(y_ready, 1)

                def take_gates(t):
                    dve.wait_ge(gp_ready, t + 1)
                    V.tensor_copy(gs[:, :], y_ps[:, 0:1]).then_inc(gs_ready, 1)

                def each_turn(i, j, k, t):
                    dve.wait_ge(t_ready, t + PRIMED)
                    for r in range(TT):
                        number = slots[:, bass.ds(k * P, P)]
                        last = V.tensor_scalar(hot[:, r, :], number, g2[:, 0, j, r:r + 1], None, ALU.is_equal)
                    last.then_inc(hot_ready, 1)
                    dve.wait_ge(x_ready, t + 1)
                    V.tensor_copy(xg, x_ps[:, :, :]).then_inc(xg_ready, 1)
                    take(t)
                    if not gated:
                        take_gates(t)
                    if gated:
                        for g in range(NG):
                            done = (t * NG + g) * STEPS
                            dve.wait_ge(up_ready, t * NG + g + 1)
                            for n in range(PER):
                                c = g * PER + n
                                V.tensor_scalar(tmp[:, 0, n, :], u_ps[:, g % 2, n, :], b1[:, j, c:c + 1], LIMIT,
                                                ALU.add, ALU.min).then_inc(parts, 1)
                            for n in range(PER):
                                c = g * PER + n
                                V.tensor_scalar(tmp[:, 1, n, :], u_ps[:, g % 2, PER + n, :], b1[:, j, HC + c:HC + c + 1], LIMIT,
                                                ALU.add, ALU.min).then_inc(parts, 1)
                            dve.wait_ge(parts, done + 2 * PER)
                            V.tensor_scalar(tmp[:, 2, :, :], tmp[:, 1, :, :], -LIMIT, 1.0, ALU.max, ALU.add).then_inc(parts, 1)
                            dve.wait_ge(parts, done + 2 * PER + 1)
                            V.tensor_tensor(tmp[:, 2, :, :], tmp[:, 2, :, :], tmp[:, 0, :, :], ALU.mult).then_inc(parts, 1)
                            dve.wait_ge(parts, done + STEPS)
                            dve.wait_ge(sig_ready, t * NG + g + 1)
                            V.tensor_tensor(h[:, g * PER:(g + 1) * PER, :], tmp[:, 2, :, :], tmp[:, 3, :, :],
                                            ALU.mult).then_inc(h_ready, 1)
                            if g == 0:
                                take_gates(t)
                    dve.wait_ge(t_ready, t + 1 + PRIMED)
                    V.tensor_copy(back[:, :].rearrange("p (r n) -> p r n", n=P), x_ps[:, :, :]).then_inc(back_ready, 1)

                V.tensor_copy(rows[:, 0, :, :], normed[:, :, :]).then_inc(rows_ready, 1)
                dve.wait_ge(rows_ready, 1)
                V.tensor_tensor(rows[:, 1, :, :], normed[:, :, :], rows[:, 0, :, :].bitcast(F32), ALU.subtract).then_inc(rows_ready, 1)
                dve.wait_ge(c_in, 32)
                dve.wait_ge(zeroed, 2)
                t = turns(dve, each_turn, each_round=each_round, first=first if gated else None)
                take(t)
                dve.wait_ge(sum_ready, 1)
                for r in range(TT):
                    V.tensor_tensor(acc[:, r, :], acc[:, r, :], a_ps[:, r, :], ALU.add)

            @block.scalar
            def _(act):
                def each_turn(i, j, k, t):
                    for g in range(NG):
                        if gated:
                            act.wait_ge(parts, (t * NG + g) * STEPS + PER)
                            nc.scalar.activation(tmp[:, 3, :, :], tmp[:, 0, :, :], ACT.Sigmoid, scale=ALPHA).then_inc(sig_ready, 1)
                        else:
                            act.wait_ge(up_ready, t * NG + g + 1)
                            for n in range(PER):
                                c = g * PER + n
                                last = nc.scalar.activation(h[:, c, :], u_ps[:, g % 2, n, :], ACT.Gelu, bias=b1[:, j, c:c + 1])
                            last.then_inc(h_ready, 1)

                def first(i, j):
                    act.wait_ge(w1_in[j], i * 32 + 32)

                turns(act, each_turn, first=first)


def choice(core, ctx, name):
    return (core.sb(ctx, f"{name}_gate", [P, TT, EXPERTS]), core.sb(ctx, f"{name}_gate_t", [EXPERTS, TOK]),
            core.sb(ctx, f"{name}_slot", [P, TT, EXPERTS]), core.sb(ctx, f"{name}_count", [1, EXPERTS], mybir.dt.int32))


def moe_L0(core, normalise, x, xn, xt, ident, w):
    with ExitStack() as ctx:
        chosen = choice(core, ctx, "m0")
        router = RouteWeights(core, ctx, "r0", w["L0_ffn_router_weight"], w["L0_ffn_router_bias"], w)
        weights = ExpertWeights(core, ctx, "e0", w["L0_ffn_gate_up_proj"], w["L0_ffn_gate_up_bias"],
                                w["L0_ffn_down_proj"], w["L0_ffn_down_bias"], w, ahead=(router.load,))
        normalise()
        route(core, "r0", xt, router, False, chosen, ident)
        experts(core, "e0", xn, xt, x, chosen, weights, hidden=512, gated=True)


def moe_L1(core, normalise, x, xn, xt, ident, w):
    nc = core.nc
    with ExitStack() as ctx:
        chosen = choice(core, ctx, "m1")
        acc = core.sb(ctx, "m1_acc", [P, TT, D])
        rows = core.sb(ctx, "m1_rows", [P, 3, D])
        ws = core.sb(ctx, "m1_ws", [P, KC, D])
        w_in, = core.sems(ctx, "m1w", "w_in")

        def load_shared(sp):
            sp.dma_start(ws[:, :, :], w["L1_ffn_shared_W"].rearrange("(c p) n -> p c n", p=P)).then_inc(w_in, 16)
            for n, k in enumerate(("L1_ffn_shared_b", "L1_ffn_gamma", "L1_ffn_beta")):
                sp.dma_start(rows[:, n, :], bcast(w[k])).then_inc(w_in, 16)

        router = RouteWeights(core, ctx, "r1", w["L1_ffn_gate_W"], None, w)
        weights = ExpertWeights(core, ctx, "e1", w["L1_ffn_W1"], w["L1_ffn_b1"], w["L1_ffn_W2"], w["L1_ffn_b2"], w,
                                ahead=(load_shared, router.load))
        normalise()
        with ExitStack() as c2:
            s_ps = core.pb(c2, "m1_s_ps", [P, TT, 512])
            s_ready, b_ready, g_ready = core.sems(c2, "m1", "s_ready b_ready g_ready")
            with nc.Block() as block:
                @block.tensor
                def _(pe):
                    pe.wait_ge(w_in, 64)
                    for t in range(TT):
                        for c in range(KC):
                            last = nc.tensor.matmul(s_ps[:, t, :], xt[:, c, t * P:(t + 1) * P], ws[:, c, :],
                                                    start=(c == 0), stop=(c == KC - 1))
                        last.then_inc(s_ready, 1)

                @block.vector
                def _(dve):
                    dve.wait_ge(w_in, 64)
                    for t in range(TT):
                        dve.wait_ge(s_ready, t + 1)
                        nc.vector.tensor_tensor(acc[:, t, :], s_ps[:, t, :], rows[:, 0, :], ALU.add).then_inc(b_ready, 1)
                    for t in range(TT):
                        dve.wait_ge(g_ready, t + 1)
                        nc.vector.tensor_scalar(acc[:, t, :], acc[:, t, :], 0.5, None, ALU.mult)

                @block.scalar
                def _(act):
                    for t in range(TT):
                        act.wait_ge(b_ready, t + 1)
                        nc.scalar.activation(acc[:, t, :], acc[:, t, :], ACT.Gelu).then_inc(g_ready, 1)
        route(core, "r1", xt, router, True, chosen, ident)
        experts(core, "e1", xn, xt, acc, chosen, weights, hidden=2048, gated=False)
        norm_stage(core, "n6", acc, acc, None, ident, gamma=rows[:, 1, :], beta=rows[:, 2, :], out=x)


def self_attention_L1(core, normalise, x, xt, ident, w):
    nc = core.nc
    H, DH = 16, 64
    HC = H * DH // P
    G = 4
    NG = H // G
    U = TT * NG
    q_scale = math.sqrt(DH / D) ** 2 / DH
    z_scale = math.sqrt(DH / D) * math.sqrt(D / DH) / H
    with ExitStack() as ctx:
        wqkv = core.sb(ctx, "s1_wqkv", [P, 2, KC, H * DH])
        wz = core.sb(ctx, "s1_wz", [P, HC, D])
        mask = core.sb(ctx, "s1_mask", [P, G, P])
        qk = core.sb(ctx, "s1_qk", [P, 2, HC, TOK])
        v = core.sb(ctx, "s1_v", [P, TT, H * DH])
        pr = core.sb(ctx, "s1_pr", [P, 2, G, P])
        pt = core.sb(ctx, "s1_pt", [P, 2, G, P])
        yt = core.sb(ctx, "s1_yt", [P, 2, HC, P])
        red = core.sb(ctx, "s1_red", [P, 2, 3, G])
        in_q, in_k, in_v, in_m, p_ready, p_used, s_ready, steps, exp_ready, inv_ready, norm_ready, t_ready, \
            pt_ready, y_ready, yt_ready, z_ready, z_used = core.sems(
                ctx, "s1", "in_q in_k in_v in_m p_ready p_used s_ready steps exp_ready inv_ready norm_ready t_ready "
                "pt_ready y_ready yt_ready z_ready z_used")
        with nc.Block() as block:
            @block.sync
            def _(sp):
                def load(slot, name, s):
                    sp.dma_start(wqkv[:, slot, :, :], w[name].rearrange("(c p) n -> p c n", p=P)).then_inc(s, 16)
                load(0, "L1_attn_Q", in_q)
                load(1, "L1_attn_K", in_k)
                sp.dma_start(wz[:, :, :], w["L1_attn_W"].rearrange("(c p) n -> p c n", p=P)).then_inc(in_m, 16)
                sp.dma_start(mask[:, :, :], w["mask_L1"].unsqueeze(1).broadcast_to([P, G, P])).then_inc(in_m, 16)

        normalise()
        ps = core.pb(ctx, "s1_ps", [P, 8, 512])
        s_bank, t_bank, y_bank, z_bank = (0, 1), (2, 3), (4, 5), 6
        with nc.Block() as block:
            @block.sync
            def _(sp):
                sp.wait_ge(p_ready, HC)
                sp.dma_start(wqkv[:, 0, :, :], w["L1_attn_V"].rearrange("(c p) n -> p c n", p=P)).then_inc(in_v, 16)

            @block.tensor
            def _(pe):
                for n in range(2 * HC):
                    a, m = n // HC, n % HC
                    if m == 0:
                        pe.wait_ge((in_q, in_k)[a], 16)
                    if n >= 8:
                        pe.wait_ge(p_used, n - 7)
                    for c in range(KC):
                        last = nc.tensor.matmul(ps[:, n % 8, :], wqkv[:, a, c, m * P:(m + 1) * P], xt[:, c, :],
                                                start=(c == 0), stop=(c == KC - 1))
                    last.then_inc(p_ready, 1)
                pe.wait_ge(in_v, 16)
                for n in range(2 * TT):
                    t, half = n // 2, n % 2
                    pe.wait_ge(p_used, 2 * HC + n - 7)
                    for c in range(KC):
                        last = nc.tensor.matmul(ps[:, n % 8, :], xt[:, c, t * P:(t + 1) * P], wqkv[:, 0, c, half * 512:(half + 1) * 512],
                                                start=(c == 0), stop=(c == KC - 1))
                    last.then_inc(p_ready, 1)
                pe.wait_ge(p_used, 2 * HC + 2 * TT)

                def scores(u):
                    t, g = u // NG, u % NG
                    if u >= 2:
                        pe.wait_ge(steps, 4 * (u - 2) + 1)
                    lo = (g % 2) * DH
                    for k in range(G):
                        c = (g // 2) * G + k
                        last = nc.tensor.matmul(ps[:, s_bank[u % 2], k * P:(k + 1) * P], qk[lo:lo + DH, 0, c, t * P:(t + 1) * P],
                                                qk[lo:lo + DH, 1, c, t * P:(t + 1) * P], start=True, stop=True)
                    last.then_inc(s_ready, 1)

                def turn(u):
                    pe.wait_ge(norm_ready, u + 1)
                    if u >= 2:
                        pe.wait_ge(pt_ready, u - 1)
                    for k in range(G):
                        last = nc.tensor.transpose(ps[:, t_bank[u % 2], k * P:(k + 1) * P], pr[:, u % 2, k, :], ident[:, :])
                    last.then_inc(t_ready, 1)

                def weigh(u):
                    t, g = u // NG, u % NG
                    pe.wait_ge(pt_ready, u + 1)
                    if u >= 2:
                        pe.wait_ge(yt_ready, u - 1)
                    lo = (g % 2) * DH
                    for k in range(G):
                        h = 2 * ((g // 2) * G + k) + g % 2
                        last = nc.tensor.matmul(ps[lo:lo + DH, y_bank[u % 2], k * P:(k + 1) * P],
                                                v[:, t, h * DH:(h + 1) * DH], pt[:, u % 2, k, :], start=True, stop=True)
                    last.then_inc(y_ready, 1)

                def project(t):
                    pe.wait_ge(yt_ready, (t + 1) * NG)
                    if t >= 1:
                        pe.wait_ge(z_used, t)
                    for c in range(HC):
                        last = nc.tensor.matmul(ps[:, z_bank, :], yt[:, t % 2, c, :], wz[:, c, :], start=(c == 0), stop=(c == HC - 1))
                    last.then_inc(z_ready, 1)

                pe.wait_ge(in_m, 32)
                for u in range(U + 3):
                    if u < U:
                        scores(u)
                    if 1 <= u <= U:
                        turn(u - 1)
                    if 2 <= u <= U + 1:
                        weigh(u - 2)
                    if u >= 3 and (u - 3) % NG == NG - 1:
                        project((u - 3) // NG)

            @block.scalar
            def _(act):
                for n in range(0, 2 * HC + 2 * TT):
                    act.wait_ge(p_ready, n + 1)
                    if n < 2 * HC:
                        nc.scalar.copy(qk[:, n // HC, n % HC, :], ps[:, n % 8, :]).then_inc(p_used, 1)
                    else:
                        m = n - 2 * HC
                        nc.scalar.copy(v[:, m // 2, (m % 2) * 512:(m % 2 + 1) * 512], ps[:, n % 8, :]).then_inc(p_used, 1)
                for u in range(U + 2):
                    if u < U:
                        act.wait_ge(steps, 4 * u + 3)
                        nc.scalar.activation(pr[:, u % 2, :, :], pr[:, u % 2, :, :], ACT.Exp).then_inc(exp_ready, 1)
                    if 1 <= u <= U:
                        act.wait_ge(t_ready, u)
                        if u >= 3:
                            act.wait_ge(y_ready, u - 2)
                        nc.scalar.copy(pt[:, (u - 1) % 2, :, :], ps[:, t_bank[(u - 1) % 2], :].rearrange("p (g n) -> p g n", g=G)
                                       ).then_inc(pt_ready, 1)
                    if u >= 2:
                        t, g = (u - 2) // NG, (u - 2) % NG
                        act.wait_ge(y_ready, u - 1)
                        if t >= 2:
                            act.wait_ge(z_ready, t - 1)
                        lo = (g % 2) * DH
                        nc.scalar.copy(yt[lo:lo + DH, t % 2, (g // 2) * G:(g // 2 + 1) * G, :],
                                       ps[lo:lo + DH, y_bank[(u - 2) % 2], :].rearrange("p (c n) -> p c n", c=G)).then_inc(yt_ready, 1)

            @block.vector
            def _(dve):
                def add(dve, t):
                    dve.wait_ge(z_ready, t + 1)
                    nc.vector.scalar_tensor_tensor(x[:, t, :], ps[:, z_bank, :], z_scale, x[:, t, :],
                                                   ALU.mult, ALU.add).then_inc(z_used, 1)

                dve.wait_ge(in_m, 32)
                for u in range(U):
                    k = u % 2
                    dve.wait_ge(s_ready, u + 1)
                    if u >= 2:
                        dve.wait_ge(t_ready, u - 1)
                    nc.vector.scalar_tensor_tensor(pr[:, k, :, :], ps[:, s_bank[k], :].rearrange("p (g n) -> p g n", g=G), q_scale,
                                                   mask[:, :, :], ALU.mult, ALU.add).then_inc(steps, 1)
                    dve.wait_ge(steps, 4 * u + 1)
                    nc.vector.reduce_max(red[:, k, 0, :], pr[:, k, :, :], AXIS.X).then_inc(steps, 1)
                    dve.wait_ge(steps, 4 * u + 2)
                    nc.vector.tensor_tensor(pr[:, k, :, :], pr[:, k, :, :], red[:, k, 0, :].unsqueeze(2).broadcast_to([P, G, P]),
                                            ALU.subtract).then_inc(steps, 1)
                    dve.wait_ge(exp_ready, u + 1)
                    nc.vector.reduce_sum(red[:, k, 1, :], pr[:, k, :, :], AXIS.X).then_inc(steps, 1)
                    dve.wait_ge(steps, 4 * u + 4)
                    nc.vector.reciprocal(red[:, k, 2, :], red[:, k, 1, :]).then_inc(inv_ready, 1)
                    dve.wait_ge(inv_ready, u + 1)
                    nc.vector.tensor_tensor(pr[:, k, :, :], pr[:, k, :, :], red[:, k, 2, :].unsqueeze(2).broadcast_to([P, G, P]),
                                            ALU.mult).then_inc(norm_ready, 1)
                    if u >= NG + 2 and (u - 2) % NG == 0:
                        add(dve, (u - 2) // NG - 1)
                add(dve, TT - 1)


FREQ = 2 * S


def transforms():
    l = np.arange(S)[:, None]
    re = np.arange(S + 1)
    im = np.arange(1, S)
    ang = lambda k: 2 * np.pi * ((l * k) % FREQ) / FREQ
    spec = np.concatenate([np.cos(ang(re)), -np.sin(ang(im))], 1)
    swapped = np.concatenate([-np.sin(ang(re)), np.cos(ang(im))], 1)
    k_re = np.concatenate([np.cos(ang(re)), np.cos(ang(im))], 1)
    k_im = np.concatenate([np.sin(ang(re)), -np.sin(ang(im))], 1)
    weight = np.where((re == 0) | (re == S), 1.0, 2.0) / FREQ
    inverse = np.concatenate([np.cos(ang(re)) * weight, -np.sin(ang(im)) * 2.0 / FREQ], 1).T
    return {"dft_x": np.stack([spec, swapped]).astype(np.float32),
            "dft_k": np.stack([k_re, k_im]).astype(np.float32),
            "dft_inverse": inverse.astype(np.float32)}


class FilterTiles:

    N = 64
    STEP = 8
    R = S // STEP
    PARTS = 8
    QUARTER = R // 4

    def __init__(self, core, ctx, k, scratch, w):
        self.core, self.k, self.w = core, k, w
        N, R, STEP = self.N, self.R, self.STEP
        self.par = core.sb(ctx, "k_par", [P, 4, KC, N])
        self.dts = core.sb(ctx, "k_dts", [P, KC])
        self.cur = core.sb(ctx, "k_cur", [P, 4, N])
        self.dt = core.sb(ctx, "k_dt", [P, 1])
        self.dta = core.sb(ctx, "k_dta", [P, 2, N])
        self.mag = core.sb(ctx, "k_mag", [P, 2 * R, N])
        self.pw, self.ang = (s[:, :, :].rearrange("p t n -> p (t n)").rearrange("p (a m n) -> p a m n", a=2, n=N)
                             for s in scratch)
        self.sm = core.sb(ctx, "k_sm", [P, 8, N])
        self.u = core.sb(ctx, "k_u", [P, 2, R, N])
        self.kt = core.sb(ctx, "k_kt", [P, S])
        self.k_in, self.dt_ready, self.steps, self.mag_ready, self.angles_ready, self.powers_ready = core.sems(
            ctx, "k", "k_in dt_ready steps mag_ready angles_ready powers_ready")

    def load(self, sp):
        sp.dma_start(self.dts[:, :], self.w["L1_xattn_log_dt"]).then_inc(self.k_in, 16)
        for n, name in enumerate(("A_re", "A_im", "C_re", "C_im")):
            sp.dma_start(self.par[:, n, :, :], self.w[f"L1_xattn_{name}"].rearrange("(c p) n -> p c n", p=P)).then_inc(self.k_in, 16)

    def step_sizes(self, act):
        act.wait_ge(self.k_in, 80)
        self.core.nc.scalar.activation(self.dts[:, :], self.dts[:, :], ACT.Exp).then_inc(self.dt_ready, 1)

    def scalar_part(self, act, i, part):
        A = self.core.nc.scalar
        if part == 1:
            act.wait_ge(self.mag_ready, i + 1)
            A.activation(self.mag[:, :, :], self.mag[:, :, :], ACT.Exp).then_inc(self.powers_ready, 1)
        elif part == 3:
            act.wait_ge(self.angles_ready, i + 1)
            for n in range(2):
                A.activation(self.pw[:, 1 - n, :, :], self.ang[:, n, :, :], ACT.Sin).then_inc(self.powers_ready, 1)

    def vector_part(self, dve, i, part):
        V = self.core.nc.vector
        N, R, STEP, QUARTER = self.N, self.R, self.STEP, self.QUARTER
        ang, turns = self.ang[:, 0, :, :], self.ang[:, 1, :, :]
        mag, pw, sm, u, dta, cur = self.mag, self.pw, self.sm, self.u, self.dta, self.cur
        mult = [b for b in range(STEP)] + [STEP * a for a in range(R)]
        PI2_HI = 6.28125
        PI2_LO = 2 * PI - PI2_HI
        ROUND = 1.5 * 2 ** 23
        TOP = float(np.nextafter(np.float32(PI), np.float32(0)))
        done = [0]

        def step(instruction):
            done[0] += 1
            instruction.then_inc(self.steps, 1)

        def sync():
            dve.wait_ge(self.steps, done[0])

        def quarter(n):
            for part in range(2):
                ua = u[:, part, n * QUARTER:(n + 1) * QUARTER, :].unsqueeze(2).broadcast_to([P, QUARTER, STEP, N])
                wb = pw[:, part, 0:STEP, :].unsqueeze(1).broadcast_to([P, QUARTER, STEP, N])
                step(V.tensor_tensor(self.ang[:, part, :, :].rearrange("p (a b) n -> p a b n", b=STEP), ua, wb, ALU.mult))
            sync()
            step(V.tensor_tensor(ang, ang, turns, ALU.add))
            sync()
            width = QUARTER * STEP
            step(V.reduce_sum(self.kt[:, n * width:(n + 1) * width], ang, AXIS.X))

        if part == 0:
            V.tensor_copy(cur[:, :, :], self.par[:, :, bass.ds(i, 1), :].rearrange("p a c n -> p a (c n)")).then_inc(self.steps, 1)
            V.tensor_copy(self.dt[:, :], self.dts[:, bass.ds(i, 1)]).then_inc(self.steps, 1)
            done[0] += 2
            sync()
            for a in range(2):
                step(V.tensor_scalar(dta[:, a, :], cur[:, a, :], self.dt[:, 0:1], None, ALU.mult))
            sync()
            for m, f in enumerate(mult):
                last = V.tensor_scalar(mag[:, m, :], dta[:, 0, :], float(f), None, ALU.mult)
            last.then_inc(self.mag_ready, 1)
            for m, f in enumerate(mult):
                step(V.tensor_scalar(ang[:, m, :], dta[:, 1, :], float(f), None, ALU.mult))
        elif part == 1:
            step(V.tensor_scalar(turns, ang, 1 / (2 * PI), ROUND, ALU.mult, ALU.add))
            sync()
            step(V.tensor_scalar(turns, turns, ROUND, None, ALU.subtract))
            sync()
            step(V.scalar_tensor_tensor(ang, turns, -PI2_HI, ang, ALU.mult, ALU.add))
            sync()
            step(V.scalar_tensor_tensor(ang, turns, -PI2_LO, ang, ALU.mult, ALU.add))
        elif part == 2:
            step(V.tensor_scalar(turns, ang, PI / 2, -2 * PI, ALU.is_gt, ALU.mult))
            sync()
            step(V.scalar_tensor_tensor(turns, ang, PI / 2, turns, ALU.add, ALU.add))
            sync()
            step(V.tensor_scalar(ang, ang, TOP, -TOP, ALU.min, ALU.max))
            V.tensor_scalar(turns, turns, TOP, -TOP, ALU.min, ALU.max).then_inc(self.angles_ready, 1)
        elif part == 4:
            dve.wait_ge(self.powers_ready, i * 3 + 3)
            for a in range(2):
                step(V.tensor_tensor(pw[:, a, :, :], pw[:, a, :, :], mag[:, :, :], ALU.mult))
            sync()
            are, aim, cre, cim = (cur[:, n, :] for n in range(4))
            er, ei = sm[:, 0, :], pw[:, 1, 1, :]
            step(V.tensor_scalar(er, pw[:, 0, 1, :], -1.0, None, ALU.add))
            sync()
            step(V.tensor_tensor(sm[:, 1, :], cre, er, ALU.mult))
            step(V.tensor_tensor(sm[:, 2, :], cim, ei, ALU.mult))
            step(V.tensor_tensor(sm[:, 3, :], cre, ei, ALU.mult))
            step(V.tensor_tensor(sm[:, 4, :], cim, er, ALU.mult))
            step(V.tensor_tensor(sm[:, 5, :], are, are, ALU.mult))
            step(V.tensor_tensor(sm[:, 6, :], aim, aim, ALU.mult))
            sync()
            step(V.tensor_tensor(sm[:, 1, :], sm[:, 1, :], sm[:, 2, :], ALU.subtract))
            step(V.tensor_tensor(sm[:, 3, :], sm[:, 3, :], sm[:, 4, :], ALU.add))
            step(V.tensor_tensor(sm[:, 5, :], sm[:, 5, :], sm[:, 6, :], ALU.add))
            sync()
            step(V.reciprocal(sm[:, 5, :], sm[:, 5, :]))
            step(V.tensor_tensor(sm[:, 6, :], sm[:, 1, :], are, ALU.mult))
            step(V.tensor_tensor(sm[:, 4, :], sm[:, 3, :], aim, ALU.mult))
            step(V.tensor_tensor(sm[:, 7, :], sm[:, 3, :], are, ALU.mult))
            step(V.tensor_tensor(sm[:, 2, :], sm[:, 1, :], aim, ALU.mult))
            sync()
            step(V.tensor_tensor(sm[:, 6, :], sm[:, 6, :], sm[:, 4, :], ALU.add))
            step(V.tensor_tensor(sm[:, 7, :], sm[:, 7, :], sm[:, 2, :], ALU.subtract))
            sync()
            for n in (6, 7):
                step(V.scalar_tensor_tensor(sm[:, n, :], sm[:, n, :], 2.0, sm[:, 5, :], ALU.mult, ALU.mult))
        elif part == 5:
            dr, di = (sm[:, n, :].unsqueeze(1).broadcast_to([P, R, N]) for n in (6, 7))
            pr8, pi8 = pw[:, 0, STEP:STEP + R, :], pw[:, 1, STEP:STEP + R, :]
            t0, t1 = mag[:, 0:R, :], mag[:, R:2 * R, :]
            step(V.tensor_tensor(u[:, 0, :, :], dr, pr8, ALU.mult))
            step(V.tensor_tensor(t0, di, pi8, ALU.mult))
            step(V.tensor_tensor(u[:, 1, :, :], dr, pi8, ALU.mult))
            step(V.tensor_tensor(t1, di, pr8, ALU.mult))
            sync()
            step(V.tensor_tensor(u[:, 0, :, :], u[:, 0, :, :], t0, ALU.subtract))
            step(V.scalar_tensor_tensor(u[:, 1, :, :], u[:, 1, :, :], -1.0, t1, ALU.mult, ALU.subtract))
            sync()
            quarter(0)
        elif part == 6:
            quarter(1)
            sync()
            quarter(2)
        elif part == 7:
            quarter(3)
            sync()
            step(V.tensor_copy(self.k[:, bass.ds(i, 1), :].rearrange("p c l -> p (c l)"), self.kt[:, :]))
        if done[0]:
            sync()
            dve.sem_clear(self.steps)


def filter_spectrum(core, k, spec_k, ident, w):
    nc = core.nc
    with ExitStack() as ctx:
        kt = core.sb(ctx, "k_rows", [S, D])
        dft = core.sb(ctx, "k_dft", [S, 2, FREQ])
        t_ps = core.pb(ctx, "k_t_ps", [P, 512])
        f_ps = core.pb(ctx, "k_f_ps", [P, 2, 512])
        dft_in, t_ready, kt_ready, f_ready = core.sems(ctx, "s", "dft_in t_ready kt_ready f_ready")
        with nc.Block() as block:
            @block.sync
            def _(sp):
                sp.dma_start(dft[:, :, :], w["dft_k"].rearrange("a l f -> l a f")).then_inc(dft_in, 16)

            @block.tensor
            def _(pe):
                for c in range(KC):
                    last = nc.tensor.transpose(t_ps[0:S, c * P:(c + 1) * P], k[:, c, :], ident[:, :])
                last.then_inc(t_ready, 1)
                pe.wait_ge(dft_in, 16)
                pe.wait_ge(kt_ready, 1)
                for a in range(2):
                    last = nc.tensor.matmul(f_ps[:, a, :], dft[:, a, :], kt[:, :], start=True, stop=True)
                last.then_inc(f_ready, 1)

            @block.vector
            def _(dve):
                dve.wait_ge(t_ready, 1)
                nc.vector.tensor_copy(kt[:, :], t_ps[0:S, :]).then_inc(kt_ready, 1)

            @block.scalar
            def _(act):
                act.wait_ge(f_ready, 1)
                nc.scalar.copy(spec_k[:, :, :], f_ps[:, :, :])


def cross_attention_L1(core, normalise, x, xn, xt, k, ident, w):
    with ExitStack() as ctx:
        ct = core.sb(ctx, "x1_ct", [P, CC, TOK])
        top_attention(core, normalise, xt, ct, ident, w)
        spec_k = core.sb(ctx, "x1_spec_k", [P, 2, D])
        filter_spectrum(core, k, spec_k, ident, w)
        mixing(core, x, xn, xt, ct, spec_k, ident, w)


def top_attention(core, normalise, xt, ct, ident, w):
    nc = core.nc
    H, DH, TOP = 4, 32, 32
    HALVES = H // 2
    ROUNDS = B // PAIR
    TAKEN = -3e38
    with ExitStack() as ctx:
        qp = core.sb(ctx, "x1_qp", [P, CC, H, TOK])
        with ExitStack() as c2:
            wq = core.sb(c2, "x1_wq", [P, KC, H * DH])
            wkt = core.sb(c2, "x1_wkt", [P, CD])
            qt = core.sb(c2, "x1_qt", [P, TOK])
            w_in, q_ready, qt_ready, qp_ready, qp_used = core.sems(c2, "x1", "w_in q_ready qt_ready qp_ready qp_used")
            with nc.Block() as block:
                @block.sync
                def _(sp):
                    sp.dma_start(wq[:, :, :], w["L1_xattn_Wq"].rearrange("(c p) n -> p c n", p=P)).then_inc(w_in, 16)
                    sp.dma_start(wkt[:, :], w["L1_xattn_WkT"]).then_inc(w_in, 16)

            normalise()
            ps = core.pb(c2, "x1_ps", [P, 8, 512])
            with nc.Block() as block:
                @block.tensor
                def _(pe):
                    pe.wait_ge(w_in, 32)
                    for c in range(KC):
                        last = nc.tensor.matmul(ps[:, 0, :], wq[:, c, :], xt[:, c, :], start=(c == 0), stop=(c == KC - 1))
                    last.then_inc(q_ready, 1)
                    pe.wait_ge(qt_ready, 1)
                    for n in range(H * CC):
                        h, c = n // CC, n % CC
                        if n >= 4:
                            pe.wait_ge(qp_used, n - 3)
                        nc.tensor.matmul(ps[:, 4 + n % 4, :], wkt[h * DH:(h + 1) * DH, c * P:(c + 1) * P],
                                         qt[h * DH:(h + 1) * DH, :], start=True, stop=True).then_inc(qp_ready, 1)

                @block.scalar
                def _(act):
                    act.wait_ge(q_ready, 1)
                    nc.scalar.mul(qt[:, :], ps[:, 0, :], DH ** -0.5).then_inc(qt_ready, 1)
                    for n in range(H * CC):
                        act.wait_ge(qp_ready, n + 1)
                        nc.scalar.copy(qp[:, n % CC, n // CC, :], ps[:, 4 + n % 4, :]).then_inc(qp_used, 1)

        cx = core.sb(ctx, "x1_cx", [P, PAIR, KT, CD])
        cxt = core.sb(ctx, "x1_cxt", [P, PAIR, CC, CTX])
        mask8 = core.sb(ctx, "x1_mask8", [P, CTX], U8)
        mask = core.sb(ctx, "x1_mask", [P, CTX])
        qs = core.sb(ctx, "x1_qs", [P, HALVES, CC, P])
        sc = core.sb(ctx, "x1_sc", [P, PAIR, HALVES, CTX])
        left = core.sb(ctx, "x1_left", [P, HALVES, CTX])
        best = core.sb(ctx, "x1_best", [P, HALVES, TOP])
        best_p = core.sb(ctx, "x1_best_p", [P, HALVES, TOP])
        red = core.sb(ctx, "x1_red", [P, HALVES, 3])
        two = core.sb(ctx, "x1_two", [P, S])
        mean = core.sb(ctx, "x1_mean", [P, HALVES, S])
        at = core.sb(ctx, "x1_at", [P, KT, S])
        s_ps = core.pb(ctx, "x1_s_ps", [P, 4 * 512])
        a_ps = core.pb(ctx, "x1_a_ps", [P, 2 * 512])
        c_ps = core.pb(ctx, "x1_c_ps", [P, 512])
        cx_in0, cx_in1, cxt_in0, cxt_in1, m_in, two_in, mask_ready, qs_ready, s_ready, sc_copied, sc_ready, steps, \
            max_ready, chosen, sum_ready, left_ready, inv_ready, p_ready, mean_ready, a_ready, at_ready, c_ready, ct_ready = core.sems(
                ctx, "x1", "cx_in0 cx_in1 cxt_in0 cxt_in1 m_in two_in mask_ready qs_ready s_ready sc_copied sc_ready steps "
                "max_ready chosen sum_ready left_ready inv_ready p_ready mean_ready a_ready at_ready c_ready ct_ready")
        cx_in, cxt_in = (cx_in0, cx_in1), (cxt_in0, cxt_in1)
        PICKS = TOP // 8

        def batches(engine, first, body):
            first()
            with engine.Fori(0, ROUNDS - 1) as i:
                body(i, 0, (i, 1), (i + 1, 0))
                body(i, 1, (i + 1, 0), (i + 1, 1))
            body(ROUNDS - 1, 0, (ROUNDS - 1, 1), None)
            body(ROUNDS - 1, 1, None, None)

        with nc.Block() as block:
            @block.sync
            def _(sp):
                sp.dma_start(two[:, :], w["two_eyes"]).then_inc(two_in, 16)

                def load(b, j, i):
                    if i is not None or j:
                        sp.wait_ge(mask_ready, i * PAIR + (PAIR + j) if i is not None else j)
                    sp.dma_start(mask8[:, :], w["mask_ctx"][bass.ds(b, 1), :].broadcast_to([P, CTX])).then_inc(m_in, 16)
                    if i is not None:
                        sp.wait_ge(s_ready, i * (PAIR * HALVES) + (j + 1) * HALVES)
                    sp.dma_start(cxt[:, j, :, :],
                                 w["ctxT"][bass.ds(b, 1), :, :].rearrange("b (c p) n -> p (b c) n", p=P)).then_inc(cxt_in[j], 16)
                    if i is not None:
                        sp.wait_ge(c_ready, i * PAIR + (j + 1 + PRIMED))
                    sp.dma_start(cx[:, j, 0:KT - 1, :],
                                 w["ctx"][bass.ds(b, 1), 0:(KT - 1) * P, :].rearrange("b (t p) n -> p (b t) n", p=P)
                                 ).then_inc(cx_in[j], 16)
                    sp.dma_start(cx[0:LAST, j, KT - 1, :],
                                 w["ctx"][bass.ds(b, 1), (KT - 1) * P:CTX, :].rearrange("b p n -> (b p) n")
                                 ).then_inc(cx_in[j], 16)

                for j in range(PAIR):
                    load(j, j, None)
                with sp.Fori(0, ROUNDS - 1) as i:
                    for j in range(PAIR):
                        load((i + 1) * PAIR + j, j, i)

            @block.tensor
            def _(pe):
                core.prime(pe, c_ready, a_ready)

                def scores(i, j, r, very_first=False):
                    unit = (i * PAIR + j) * HALVES + r
                    pe.wait_ge(qs_ready, unit + 1)
                    if r == 0:
                        pe.wait_ge(cxt_in[j], (i + 1) * 16)
                    if not very_first:
                        pe.wait_ge(sc_copied, unit)
                    for n in range(4):
                        a, b = 512 * n, min(512 * n + 512, CTX)
                        for c in range(CC):
                            last = nc.tensor.matmul(s_ps[:, a:b], qs[:, r, c, :], cxt[:, j, c, a:b],
                                                    start=(c == 0), stop=(c == CC - 1))
                    last.then_inc(s_ready, 1)

                def mean_attention(i, j):
                    b = i * PAIR + j
                    pe.wait_ge(p_ready, (b + 1) * HALVES + PRIMED)
                    pe.wait_ge(mean_ready, (b + 1) * HALVES)
                    pe.wait_ge(at_ready, b * 3 + PRIMED)
                    for t in range(KT):
                        rows = P if t < KT - 1 else LAST
                        for r in range(HALVES):
                            last = nc.tensor.matmul(a_ps[0:rows, t * S:(t + 1) * S], sc[:, j, r, t * P:t * P + rows], mean[:, r, :],
                                                    start=(r == 0), stop=(r == HALVES - 1))
                    last.then_inc(a_ready, 1)

                def weigh(i, j):
                    b = i * PAIR + j
                    pe.wait_ge(at_ready, (b + 1) * 3 + PRIMED)
                    pe.wait_ge(cx_in[j], (i + 1) * 32)
                    pe.wait_ge(ct_ready, b + PRIMED)
                    for c in range(CC):
                        for t in range(KT):
                            rows = P if t < KT - 1 else LAST
                            last = nc.tensor.matmul(c_ps[:, c * S:(c + 1) * S], cx[0:rows, j, t, c * P:(c + 1) * P], at[0:rows, t, :],
                                                    start=(t == 0), stop=(t == KT - 1))
                    last.then_inc(c_ready, 1)

                def first():
                    for j in range(PAIR):
                        for r in range(HALVES):
                            scores(0, j, r, very_first=(j + r == 0))

                def body(i, j, after, later):
                    mean_attention(i, j)
                    if later:
                        scores(*later, 0)
                    weigh(i, j)
                    if later:
                        scores(*later, 1)

                batches(pe, first, body)

            @block.scalar
            def _(act):
                core.prime(act, at_ready, ct_ready)

                def spread_mask(i, j, very_first=False):
                    b = i * PAIR + j
                    act.wait_ge(m_in, (b + 1) * 16)
                    if not very_first:
                        act.wait_ge(sc_ready, b * HALVES)
                    nc.scalar.activation(mask[:, :], mask8[:, :], ACT.Copy, bias=NEG, scale=-NEG).then_inc(mask_ready, 1)

                def copy_scores(i, j, r, reused=True):
                    b = i * PAIR + j
                    act.wait_ge(s_ready, b * HALVES + r + 1)
                    if reused:
                        act.wait_ge(a_ready, b - 1 + PRIMED)
                    nc.scalar.copy(sc[:, j, r, :], s_ps[:, 0:CTX]).then_inc(sc_copied, 1)

                def exponent(i, j, r):
                    act.wait_ge(max_ready, (i * PAIR + j) * HALVES + r + 1)
                    nc.scalar.activation(sc[:, j, r, :], sc[:, j, r, :], ACT.Exp, bias=red[:, r, 0:1])

                def exponent_left(i, j, r):
                    act.wait_ge(chosen, (i * PAIR + j) * HALVES + r + 1)
                    nc.scalar.activation(best_p[:, r, :], best[:, r, :], ACT.Exp, bias=red[:, r, 0:1],
                                         accum_out=red[:, r, 1:2]).then_inc(sum_ready, 1)
                    nc.scalar.activation(left[:, r, :], left[:, r, :], ACT.Exp, bias=red[:, r, 0:1]).then_inc(left_ready, 1)

                def copy_attention(i, j):
                    b = i * PAIR + j
                    act.wait_ge(a_ready, b + 1 + PRIMED)
                    act.wait_ge(c_ready, b + PRIMED)
                    for lo, hi, rows in ((0, 8, P), (8, KT - 1, P), (KT - 1, KT, LAST)):
                        nc.scalar.copy(at[0:rows, lo:hi, :], a_ps[0:rows, lo * S:hi * S].rearrange("p (t n) -> p t n", n=S)).then_inc(at_ready, 1)

                def copy_out(i, j):
                    b = i * PAIR + j
                    act.wait_ge(c_ready, b + 1 + PRIMED)
                    nc.scalar.copy(ct[:, :, bass.ds(b * S, S)],
                                   c_ps[:, 0:CC * S].rearrange("p (c n) -> p c n", n=S)).then_inc(ct_ready, 1)

                def first():
                    spread_mask(0, 0, very_first=True)
                    for r in range(HALVES):
                        copy_scores(0, 0, r, reused=False)
                    exponent(0, 0, 0)
                    spread_mask(0, 1)
                    exponent_left(0, 0, 0)
                    copy_scores(0, 1, 0, reused=False)
                    exponent(0, 0, 1)
                    exponent_left(0, 0, 1)
                    copy_scores(0, 1, 1, reused=False)
                    exponent(0, 1, 0)

                def body(i, j, after, later):
                    copy_attention(i, j)
                    if later:
                        spread_mask(*later)
                    if after:
                        exponent_left(*after, 0)
                    if later:
                        copy_scores(*later, 0)
                    if after:
                        exponent(*after, 1)
                    copy_out(i, j)
                    if after:
                        exponent_left(*after, 1)
                    if later:
                        copy_scores(*later, 1)
                        exponent(*later, 0)

                batches(act, first, body)

            @block.gpsimd
            def _(pool):
                core.prime(pool, p_ready)

                def queries(i, j, r, very_first=False):
                    b = i * PAIR + j
                    if not very_first:
                        pool.wait_ge(s_ready, (b - 1) * HALVES + r + 1)
                    nc.gpsimd.tensor_copy(qs[:, r, :, :].rearrange("p c (h s) -> p c h s", h=2),
                                          qp[:, :, 2 * r:2 * r + 2, bass.ds(b * S, S)]).then_inc(qs_ready, 1)

                def mask_scores(i, j, r):
                    b = i * PAIR + j
                    pool.wait_ge(mask_ready, b + 1)
                    pool.wait_ge(sc_copied, b * HALVES + r + 1)
                    nc.gpsimd.tensor_tensor(sc[:, j, r, :], sc[:, j, r, :], mask[:, :], ALU.add).then_inc(sc_ready, 1)

                def keep_chosen(i, j, r):
                    pool.wait_ge(left_ready, (i * PAIR + j) * HALVES + r + 1)
                    nc.gpsimd.tensor_tensor(sc[:, j, r, :], sc[:, j, r, :], left[:, r, :], ALU.subtract).then_inc(p_ready, 1)

                def first():
                    for j in range(PAIR):
                        for r in range(HALVES):
                            queries(0, j, r, very_first=(j == 0))
                        for r in range(HALVES):
                            if j == 1:
                                keep_chosen(0, 0, r)
                            mask_scores(0, j, r)

                def body(i, j, after, later):
                    if later:
                        for r in range(HALVES):
                            queries(*later, r)
                    for r in range(HALVES):
                        if after:
                            keep_chosen(*after, r)
                        if later:
                            mask_scores(*later, r)

                batches(pool, first, body)

            @block.vector
            def _(dve):
                V = nc.vector

                def finish(i, j, r):
                    b = i * PAIR + j
                    dve.wait_ge(sum_ready, b * HALVES + r + 1)
                    V.reciprocal(red[:, r, 2:3], red[:, r, 1:2]).then_inc(inv_ready, 1)
                    dve.wait_ge(a_ready, b + PRIMED)
                    dve.wait_ge(inv_ready, b * HALVES + r + 1)
                    V.tensor_scalar(mean[:, r, :], two[:, :], red[:, r, 2:3], 1.0 / H, ALU.mult, ALU.mult).then_inc(mean_ready, 1)

                def pick(i, j, r, before=None):
                    unit = (i * PAIR + j) * HALVES + r
                    done = [0]

                    def step(instruction):
                        done[0] += 1
                        instruction.then_inc(steps, 1)
                        dve.wait_ge(steps, done[0])

                    dve.wait_ge(sc_ready, unit + 1)
                    if before:
                        dve.wait_ge(p_ready, unit - 1 + PRIMED)
                    step(V.memset(best[:, r, :], NEG))
                    for n in range(PICKS):
                        source = sc[:, j, r, :] if n == 0 else left[:, r, :]
                        step(V.max(best[:, r, 8 * n:8 * n + 8], source))
                        step(V.match_replace(left[:, r, :], best[:, r, 8 * n:8 * n + 8], source, TAKEN))
                        if n == 0:
                            V.tensor_scalar(red[:, r, 0:1], best[:, r, 0:1], -1.0, None, ALU.mult).then_inc(max_ready, 1)
                        if n == 1 and before:
                            finish(*before)
                    dve.sem_inc(chosen, 1)
                    dve.sem_clear(steps)

                def body(i, j, after, later):
                    pick(i, j, 1, before=(i, j, 0))
                    if after:
                        pick(*after, 0, before=(i, j, 1))
                    else:
                        finish(i, j, 1)

                dve.wait_ge(two_in, 16)
                batches(dve, lambda: pick(0, 0, 0), body)


def mixing(core, x, xn, xt, ct, spec_k, ident, w):
    nc = core.nc
    FC = 2048 // P
    with ExitStack() as ctx:
        y = core.sb(ctx, "mx_y", [P, TT, D])
        film = core.sb(ctx, "mx_film", [P, TT, 2 * D])
        with ExitStack() as c2:
            wv = core.sb(c2, "mx_wv", [P, CC, D])
            wf = core.sb(c2, "mx_wf", [P, 2, KC, 2 * D])
            bf = core.sb(c2, "mx_bf", [P, 2, 2 * D])
            tm8 = core.sb(c2, "mx_tm8", [P, TOK], U8)
            tm = core.sb(c2, "mx_tm", [P, TOK])
            c_t = core.sb(c2, "mx_c_t", [P, KC, TOK])
            film_in = core.sb(c2, "mx_film_in", [P, TT, 2 * D])
            mg = core.sb(c2, "mx_mg", [P, 1])
            rows = core.sb(c2, "mx_rows", [P, 3, D])
            dft = core.sb(c2, "mx_dft", [P, 2, FREQ])
            inverse = core.sb(c2, "mx_inverse", [P, S])
            xs = core.sb(c2, "mx_xs", [P, TT, D])
            films = (film_in, film)
            with ExitStack() as c3:
                ps = core.pb(c3, "mx_ps", [P, 8, 512])
                norm = Norm(core, c3, "n4", xn, xs, gamma=rows[:, 0, :], beta=rows[:, 1, :])
                c_in, n_in, f_in, tm_ready, v_ready, ct_ready, f_ready, f_used, g_steps, s_first = core.sems(
                    c3, "mx", "c_in n_in f_in tm_ready v_ready ct_ready f_ready f_used g_steps s_first")
                with nc.Block() as block:
                    @block.sync
                    def _(sp):
                        sp.dma_start(wv[:, :, :], w["L1_xattn_Wv"].rearrange("(c p) n -> p c n", p=P)).then_inc(c_in, 16)
                        sp.dma_start(tm8[:, :], w["mask_x"].broadcast_to([P, TOK])).then_inc(c_in, 16)
                        for n, k in enumerate(("g_norm_in", "b_norm_in", "D_skip")):
                            sp.dma_start(rows[:, n, :], bcast(w[f"L1_xattn_{k}"])).then_inc(n_in, 16)
                        for a, k in enumerate(("in", "out")):
                            sp.dma_start(wf[:, a, :, :], w[f"L1_xattn_W_film_{k}"].rearrange("(c p) n -> p c n", p=P)).then_inc(f_in, 16)
                            sp.dma_start(bf[:, a, :], bcast(w[f"L1_xattn_b_film_{k}"])).then_inc(f_in, 16)
                        sp.dma_start(mg[:, :], w["L1_xattn_mod_gate"].broadcast_to([P, 1])).then_inc(f_in, 16)
                        for half in range(2):
                            sp.dma_start(dft[half * S:(half + 1) * S, :, :], w["dft_x"].rearrange("a l f -> l a f")).then_inc(f_in, 16)
                        sp.dma_start(inverse[:, :], w["dft_inverse"]).then_inc(f_in, 16)
                        sp.wait_ge(f_in, 8 * 16)

                    @block.tensor
                    def _(pe):
                        pe.wait_ge(c_in, 32)
                        for m in range(KC):
                            for c in range(CC):
                                last = nc.tensor.matmul(ps[:, m, :], wv[:, c, m * P:(m + 1) * P], ct[:, c, :],
                                                        start=(c == 0), stop=(c == CC - 1))
                            last.then_inc(v_ready, 1)
                        pe.wait_ge(ct_ready, KC)
                        pe.wait_ge(f_in, 8 * 16)
                        for n in range(4 * TT):
                            a, t, half = n // (2 * TT), n // 2 % TT, n % 2
                            if n >= 4:
                                pe.wait_ge(f_used, n - 3)
                            for c in range(KC):
                                last = nc.tensor.matmul(ps[:, 4 + n % 4, :], c_t[:, c, t * P:(t + 1) * P],
                                                        wf[:, a, c, half * D:(half + 1) * D], start=(c == 0), stop=(c == KC - 1))
                            last.then_inc(f_ready, 1)

                    @block.gpsimd
                    def _(pool):
                        pool.wait_ge(c_in, 32)
                        nc.gpsimd.tensor_copy(tm[:, :], tm8[:, :]).then_inc(tm_ready, 1)
                        norm.inverse_deviation(pool)

                    @block.vector
                    def _(dve):
                        V = nc.vector
                        norm.statistics(dve)
                        dve.wait_ge(tm_ready, 1)
                        for m in range(KC):
                            dve.wait_ge(v_ready, m + 1)
                            V.tensor_tensor(c_t[:, m, :], ps[:, m, :], tm[:, :], ALU.mult).then_inc(ct_ready, 1)
                        dve.wait_ge(n_in, 48)
                        dve.wait_ge(f_in, 8 * 16)

                        def take(n):
                            a, t, half = n // (2 * TT), n // 2 % TT, n % 2
                            dve.wait_ge(f_ready, n + 1)
                            V.tensor_tensor(films[a][:, t, half * D:(half + 1) * D], ps[:, 4 + n % 4, :],
                                            bf[:, a, half * D:(half + 1) * D], ALU.add).then_inc(f_used, 1)

                        def gate(a):
                            dve.wait_ge(f_used, (a + 1) * 2 * TT)
                            V.tensor_scalar(films[a][:, :, 0:D], films[a][:, :, 0:D], mg[:, 0:1], 1.0, ALU.mult, ALU.add).then_inc(g_steps, 1)
                            V.tensor_scalar(films[a][:, :, D:2 * D], films[a][:, :, D:2 * D], mg[:, 0:1], None, ALU.mult).then_inc(g_steps, 1)

                        for n in range(2 * TT):
                            take(n)
                        norm.rows(dve)
                        gate(0)
                        dve.wait_ge(g_steps, 2)
                        for t in range(TT):
                            dve.wait_ge(norm.normed_ready, norm.rows_ready(t))
                            V.tensor_tensor(xs[:, t, :], xs[:, t, :], film_in[:, t, 0:D], ALU.mult).then_inc(s_first, 1)
                            take(2 * TT + 2 * t)
                            take(2 * TT + 2 * t + 1)
                            dve.wait_ge(s_first, t + 1)
                            V.tensor_tensor(xs[:, t, :], xs[:, t, :], film_in[:, t, D:2 * D], ALU.add)
                        gate(1)

            with ExitStack() as c3:
                spec = core.sb(c3, "mx_spec", [P, 2, 2, D])
                skip = core.sb(c3, "mx_skip", [P, TT, D])
                ps = core.pb(c3, "mx_ps2", [P, 8, 512])
                sp_ready, spec_ready, y_ready, skip_ready, s_last = core.sems(
                    c3, "mx", "sp_ready spec_ready y_ready skip_ready s_last")
                with nc.Block() as block:
                    @block.tensor
                    def _(pe):
                        def forward(b):
                            lo, t, k = (b % 2) * S, b // 2, b % 2
                            if b >= 2:
                                pe.wait_ge(spec_ready, 2 * (b - 1))
                            for a in range(2):
                                last = nc.tensor.matmul(ps[:, 2 * k + a, :], dft[lo:lo + S, a, :], xs[lo:lo + S, t, :],
                                                        start=True, stop=True)
                            last.then_inc(sp_ready, 1)

                        forward(0)
                        for b in range(B):
                            lo, t, k = (b % 2) * S, b // 2, b % 2
                            if b + 1 < B:
                                forward(b + 1)
                            pe.wait_ge(spec_ready, 2 * (b + 1))
                            for a in range(2):
                                last = nc.tensor.matmul(ps[lo:lo + S, 4 + t, :], inverse[:, :], spec[:, k, a, :],
                                                        start=(a == 0), stop=(a == 1))
                            last.then_inc(y_ready, 1)

                    @block.gpsimd
                    def _(pool):
                        for t in range(TT):
                            nc.gpsimd.tensor_tensor(skip[:, t, :], xs[:, t, :], rows[:, 2, :], ALU.mult).then_inc(skip_ready, 1)

                    @block.vector
                    def _(dve):
                        V = nc.vector
                        for b in range(B):
                            k = b % 2
                            dve.wait_ge(sp_ready, b + 1)
                            if b >= 2:
                                dve.wait_ge(y_ready, b - 1)
                            for a in range(2):
                                V.tensor_tensor(spec[:, k, a, :], ps[:, 2 * k + a, :], spec_k[:, a, :], ALU.mult).then_inc(spec_ready, 1)
                        dve.wait_ge(skip_ready, TT)
                        for t in range(TT):
                            dve.wait_ge(y_ready, 2 * t + 2)
                            V.tensor_tensor(y[:, t, :], ps[:, 4 + t, :], skip[:, t, :], ALU.add).then_inc(s_last, 1)
                        for n, (other, op) in enumerate(((film[:, :, 0:D], ALU.mult), (film[:, :, D:2 * D], ALU.add), (xn[:, :, :], ALU.add))):
                            for t in range(TT):
                                dve.wait_ge(s_last, n * TT + t + 1)
                                V.tensor_tensor(y[:, t, :], y[:, t, :], other[:, t, :], op).then_inc(s_last, 1)

        with ExitStack() as c2:
            rows = core.sb(c2, "ff_rows", [P, 5, D])
            w1 = core.sb(c2, "ff_w1", [P, KC, 2048])
            w2 = core.sb(c2, "ff_w2", [P, FC, D])
            b1 = core.sb(c2, "ff_b1", [P, FC])
            h = core.sb(c2, "ff_h", [P, 2, TOK])
            r_in, w1_in, w2_in, up_ready, h_ready, down_ready, b_ready = core.sems(
                c2, "ff", "r_in w1_in w2_in up_ready h_ready down_ready b_ready")
            with nc.Block() as block:
                @block.sync
                def _(sp):
                    for n, k in enumerate(("g_ffn", "b_ffn", "g_norm_out", "b_norm_out", "b2")):
                        sp.dma_start(rows[:, n, :], bcast(w[f"L1_xattn_{k}"])).then_inc(r_in, 16)
                    sp.dma_start(w1[:, :, :], w["L1_xattn_W1"].rearrange("(c p) n -> p c n", p=P)).then_inc(w1_in, 16)
                    sp.dma_start(b1[:, :], w["L1_xattn_b1"]).then_inc(w1_in, 16)
                    sp.dma_start(w2[:, :, :], w["L1_xattn_W2"].rearrange("(c p) n -> p c n", p=P)).then_inc(w2_in, 16)
                    sp.wait_ge(r_in, 80)

            norm_stage(core, "n5", y, xn, xt, ident, gamma=rows[:, 0, :], beta=rows[:, 1, :])
            with ExitStack() as c3:
                u_ps = core.pb(c3, "ff_u_ps", [P, 2, 512])
                a_ps = core.pb(c3, "ff_a_ps", [P, TT, 512])
                with nc.Block() as block:
                    @block.tensor
                    def _(pe):
                        def up(n):
                            if n >= 2:
                                pe.wait_ge(h_ready, n - 1)
                            for c in range(KC):
                                last = nc.tensor.matmul(u_ps[:, n % 2, :], w1[:, c, n * P:(n + 1) * P], xt[:, c, :],
                                                        start=(c == 0), stop=(c == KC - 1))
                            last.then_inc(up_ready, 1)

                        pe.wait_ge(w1_in, 32)
                        pe.wait_ge(w2_in, 16)
                        up(0)
                        for n in range(FC):
                            if n + 1 < FC:
                                up(n + 1)
                            pe.wait_ge(h_ready, n + 1)
                            for t in range(TT):
                                last = nc.tensor.matmul(a_ps[:, t, :], h[:, n % 2, t * P:(t + 1) * P], w2[:, n, :],
                                                        start=(n == 0), stop=(n == FC - 1))
                            last.then_inc(down_ready, 1)

                    @block.scalar
                    def _(act):
                        act.wait_ge(w1_in, 32)
                        for n in range(FC):
                            act.wait_ge(up_ready, n + 1)
                            if n >= 2:
                                act.wait_ge(down_ready, n - 1)
                            nc.scalar.activation(h[:, n % 2, :], u_ps[:, n % 2, :], ACT.Gelu, bias=b1[:, n:n + 1]).then_inc(h_ready, 1)

                    @block.vector
                    def _(dve):
                        for t in range(TT):
                            nc.vector.tensor_tensor(y[:, t, :], y[:, t, :], rows[:, 4, :], ALU.add).then_inc(b_ready, 1)
                        dve.wait_ge(down_ready, FC)
                        for t in range(TT):
                            dve.wait_ge(b_ready, t + 1)
                            nc.vector.tensor_tensor(y[:, t, :], y[:, t, :], a_ps[:, t, :], ALU.add)
            norm_stage(core, "n7", y, xn, None, ident, gamma=rows[:, 2, :], beta=rows[:, 3, :], out=x)


def build_program(nc, w, out, start=0, upto=99):
    with ExitStack() as ctx:
        core = Core(nc, ctx)
        x = core.sb(ctx, "x", [P, TT, D])
        xn = core.sb(ctx, "xn", [P, TT, D])
        xt = core.sb(ctx, "xt", [P, KC, TOK])
        k = core.sb(ctx, "k", [P, KC, S])
        ident = core.ident = core.sb(ctx, "ident", [P, P])
        x_in, x_out = core.sems(ctx, "io", "x_in x_out")
        with nc.Block() as block:
            @block.sync
            def _(sp):
                sp.dma_start(x[:, :, :], w["x"].rearrange("(t p) n -> p t n", p=P)).then_inc(x_in, 16)
                sp.dma_start(ident[:, :], w["ident"]).then_inc(x_in, 16)
                sp.wait_ge(x_in, 32)
        stages = [
            ("n0", lambda normalise: cross_attention_L0(core, normalise, x, xn, xt, k, ident, w)),
            ("n1", lambda normalise: self_attention_L0(core, normalise, x, xt, ident, w)),
            ("n2", lambda normalise: moe_L0(core, normalise, x, xn, xt, ident, w)),
            ("n3", lambda normalise: cross_attention_L1(core, normalise, x, xn, xt, k, ident, w)),
            ("n8", lambda normalise: self_attention_L1(core, normalise, x, xt, ident, w)),
            ("n9", lambda normalise: moe_L1(core, normalise, x, xn, xt, ident, w)),
        ]
        for name, stage in stages[start:upto]:
            stage(lambda: norm_stage(core, name, x, xn, xt, ident))
        with nc.Block() as block:
            @block.sync
            def _(sp):
                sp.dma_start(out.rearrange("(t p) n -> p t n", p=P), x[:, :, :]).then_inc(x_out, 16)
                sp.wait_ge(x_out, 16)


def laid_out(inputs):
    a = {k: np.asarray(v) for k, v in inputs.items()}
    evens_first = np.concatenate([np.arange(0, D, 2), np.arange(1, D, 2)])
    token = np.arange(P)
    same = token[:, None] // S == token[None, :] // S
    ahead = token[None, :] - token[:, None]
    theta = (np.float32(10000.0) ** (np.float32(-2.0) * np.arange(D // 2, dtype=np.float32) / np.float32(D))).astype(np.float32)
    angle = theta[:, None] * (np.arange(TOK) % S).astype(np.float32)[None, :]
    per_head = lambda m: m.transpose(1, 2, 0).reshape(D, -1)
    w = {
        "x": a["x"].reshape(TOK, D),
        "ctx": a["ctx_768"],
        "ctxT": np.ascontiguousarray(a["ctx_768"].transpose(0, 2, 1)),
        "ident": np.eye(P, dtype=np.float32),
        "L0_xattn_Wq": a["L0_xattn_Wq"],
        "L0_xattn_WkT": np.ascontiguousarray(a["L0_xattn_Wk"].T),
        "L0_xattn_Wv": a["L0_xattn_Wv"],
        "L0_xattn_Wout": a["L0_xattn_Wout"],
        "L0_xattn_bout": a["L0_xattn_bout"],
        "L0_attn_Wq": a["L0_attn_Wq"][evens_first].T,
        "L0_attn_Wk": a["L0_attn_Wk"][evens_first].T,
        "L0_attn_Wv": a["L0_attn_Wv"].T,
        "rope_cos": np.cos(angle),
        "rope_sin": np.sin(angle),
        "mask_L0": np.where(same & (ahead <= 1), 0.0, NEG).astype(np.float32),
        "mask_L1": np.where(same & (ahead <= 0), 0.0, NEG).astype(np.float32),
        "L0_ffn_router_weight": a["L0_ffn_router_weight"].T,
        "L0_ffn_router_bias": a["L0_ffn_router_bias"],
        "L0_ffn_gate_up_proj": a["L0_ffn_gate_up_proj"],
        "L0_ffn_gate_up_bias": a["L0_ffn_gate_up_bias"].reshape(EXPERTS, -1, P).transpose(0, 2, 1),
        "L0_ffn_down_proj": a["L0_ffn_down_proj"],
        "L0_ffn_down_bias": a["L0_ffn_down_bias"],
        "L1_attn_Q": per_head(a["L1_attn_Q"]),
        "L1_attn_K": per_head(a["L1_attn_K"]),
        "L1_attn_V": per_head(a["L1_attn_V"]),
        "L1_attn_W": a["L1_attn_W"].transpose(2, 1, 0).reshape(-1, D),
        "L1_ffn_b1": a["L1_ffn_b1"].reshape(EXPERTS, -1, P).transpose(0, 2, 1),
        "mask_x": a["mask_BxS_bf1"].reshape(1, TOK).view(np.uint8),
        "mask_ctx": a["mask_BxS2_bf1"].view(np.uint8),
        "slots": np.arange(TOK, dtype=np.float32),
        "before": (token[:, None] < token[None, :]).astype(np.float32),
        "two_eyes": np.tile(np.eye(S, dtype=np.float32), (2, 1)),
        "L1_xattn_WkT": a["L1_xattn_Wk"].T,
        "L1_xattn_mod_gate": a["L1_xattn_mod_gate"].reshape(1, 1),
        **{k: a[k] for k in ("L1_ffn_W1", "L1_ffn_W2", "L1_ffn_b2", "L1_ffn_gate_W", "L1_ffn_shared_W", "L1_ffn_shared_b",
                             "L1_ffn_gamma", "L1_ffn_beta")},
        **{f"L1_xattn_{k}": a[f"L1_xattn_{k}"] for k in (
            "Wq", "Wv", "W_film_in", "b_film_in", "W_film_out", "b_film_out", "g_norm_in", "b_norm_in", "g_norm_out",
            "b_norm_out", "g_ffn", "b_ffn", "W1", "W2", "b2", "A_re", "A_im", "C_re", "C_im", "D_skip")},
        "L1_xattn_b1": a["L1_xattn_b1"].reshape(-1, P).T,
        "L1_xattn_log_dt": a["L1_xattn_log_dt"].reshape(-1, P).T,
        **transforms(),
    }
    return {k: np.ascontiguousarray(v) for k, v in w.items()}


def kernel(**inputs):
    import concourse.bacc as bacc
    from concourse.bass_utils import run_bass_kernel_spmd

    nc = bacc.Bacc("TRN2", target_bir_lowering=False, num_devices=1)
    w = laid_out(inputs)
    aps = {k: nc.dram_tensor(f"in_{k}", v.shape, mybir.dt.from_np(v.dtype), kind="ExternalInput").ap() for k, v in w.items()}
    out = nc.dram_tensor("out_x", (TOK, D), F32, kind="ExternalOutput").ap()
    build_program(nc, aps, out)
    r = run_bass_kernel_spmd(nc, [{f"in_{k}": v for k, v in w.items()}], core_ids=[0])
    return r.results[0]["out_x"].reshape(B, S, D)
```
